# Optimizing a Trainium2 kernel written in Bass

```python
import numpy as np
import jax
import jax.numpy as jnp

def _softmax(x, axis=-1):
    return jax.nn.softmax(x, axis=axis)

def _gelu(x):
    return jax.nn.gelu(x, approximate=True)

def _silu(x):
    return jax.nn.silu(x)

def _sigmoid(x):
    return jax.nn.sigmoid(x)

def _layernorm(x, axis=-1, eps=1e-05):
    m = jnp.mean(x, axis=axis, keepdims=True)
    v = jnp.var(x, axis=axis, keepdims=True)
    return (x - m) / jnp.sqrt(v + eps)

def _scatter_add(tgt, idx, src, axis=0):
    return tgt.at[idx].add(src)

def _segment_sum(src, seg, n):
    return jax.ops.segment_sum(src, seg, n)
kernel_name = 'mk_xattn_seq_d4_seqx_r4_90f5fc'

def setup_inputs(seed: int=0):
    np.random.seed(seed)
    _w = jnp.asarray

    def _rec_inputs():
        import jax
        import jax.numpy as jnp
        _rk = jax.random.key(seed)
        x = -0.0002928 + 1 * jax.random.normal(jax.random.fold_in(_rk, 1), (8, 256, 512), jnp.float32)
        _lenS = 256 - jax.random.randint(jax.random.fold_in(_rk, 7), (8,), 0, max(1, 256 // 4) + 1, jnp.int32)
        _lenS2 = 256 - jax.random.randint(jax.random.fold_in(_rk, 8), (8,), 0, max(1, 256 // 4) + 1, jnp.int32)
        _ctx_2048P = jax.random.normal(jax.random.fold_in(_rk, 12), (8, 16, 512), jnp.float32)
        _ctx_2048c = jax.random.dirichlet(jax.random.fold_in(_rk, 512), 0.3 * jnp.ones((16,), jnp.float32), (8, 256))
        _ctx_2048t = jnp.einsum('bsk,bkd->bsd', _ctx_2048c, _ctx_2048P)
        _ctx_2048t = _ctx_2048t * jax.lax.rsqrt(jnp.mean(jnp.square(_ctx_2048t)) + 1e-12) * 0.953939
        ctx_2048 = -1.39393e-06 + 0.999914 * (_ctx_2048t + 0.3 * jax.random.normal(jax.random.fold_in(_rk, 612), (8, 256, 512), jnp.float32))
        _validS = jnp.arange(256)[None, :] < _lenS[:, None]
        _validS2 = jnp.arange(256)[None, :] < _lenS2[:, None]
        _causal = jnp.tril(jnp.ones((256, 256), dtype=bool))
        mask_Bx1x2048_bf1 = jnp.ones((8, 1, 512), dtype=bool)
        mask_BxS2_ik0 = jnp.where(jnp.broadcast_to(_validS2[:, :], (8, 256)), 0, 1).astype(jnp.int32)
        mask_Bx1xSxS2_ff0 = jnp.where(jnp.ones((8, 1, 256, 256), dtype=bool), 0.0, -1000000000.0).astype(jnp.float32)
        return (x, ctx_2048, mask_Bx1x2048_bf1, mask_BxS2_ik0, mask_Bx1xSxS2_ff0)
    x, ctx_2048, mask_Bx1x2048_bf1, mask_BxS2_ik0, mask_Bx1xSxS2_ff0 = _rec_inputs()

    def _L0_xattn_setup():
        import jax, jax.numpy as jnp
        import numpy as np
        import math
        N_HEADS = 16
        EPS = 1e-05

        def _masked_instance_norm(x, mask):
            m = mask.astype(x.dtype)
            x = x * m
            n_valid = jnp.sum(m, axis=-1, keepdims=True)
            mean = jnp.sum(x, axis=-1, keepdims=True) / n_valid
            var = jnp.sum(x * x, axis=-1, keepdims=True) / n_valid - mean * mean
            x = (x - mean) / jnp.sqrt(jax.nn.relu(var) + EPS)
            return x * m
        key = jax.random.key(seed)
        ks = jax.random.split(key, 8)
        bs, c, t1, t2 = (2, 256, 512, 512)
        s = 1.0 / math.sqrt(c)
        return {'x': jax.random.normal(ks[0], (bs, c, t1), jnp.float32), 'mask': jnp.ones((bs, 1, t1), jnp.bool_), 'kv': jax.random.normal(ks[1], (bs, c, t2), jnp.float32), 'kv_mask': jnp.ones((bs, 1, t2), jnp.bool_), 'Wq': jax.random.normal(ks[2], (c, c), jnp.float32) * s, 'bq': jnp.zeros((c,), jnp.float32), 'Wk': jax.random.normal(ks[3], (c, c), jnp.float32) * s, 'bk': jnp.zeros((c,), jnp.float32), 'Wv': jax.random.normal(ks[4], (c, c), jnp.float32) * s, 'bv': jnp.zeros((c,), jnp.float32)}
    _L0_xattn_all = _L0_xattn_setup()
    _L0_xattn_in = {k: v for k, v in _L0_xattn_all.items() if k in ('Wq', 'bq', 'Wk', 'bk', 'Wv', 'bv')}
    del _L0_xattn_all

    def _L1_xattn_setup():
        import jax, jax.numpy as jnp
        import numpy as np
        B, P, K, H, NH = (4, 512, 64, 512, 16)
        DH = H // NH
        EPS = 1e-06

        def rmsnorm(x, w):
            var = jnp.mean(jnp.square(x), axis=-1, keepdims=True)
            return x * jax.lax.rsqrt(var + EPS) * w
        key = jax.random.key(seed)
        ks = jax.random.split(key, 12)
        s = 0.02
        return {'x': jax.random.normal(ks[0], (B, P, H), jnp.float32), 'latents': jax.random.normal(ks[1], (B, K, H), jnp.float32), 'attention_mask': jax.random.randint(ks[2], (B, P), 0, 2, jnp.int32), 'q_w': s * jax.random.normal(ks[3], (H, H), jnp.float32), 'q_b': jnp.zeros((H,), jnp.float32), 'kv_w': s * jax.random.normal(ks[4], (H, 2 * H), jnp.float32), 'kv_b': jnp.zeros((2 * H,), jnp.float32), 'out_w': s * jax.random.normal(ks[5], (H, H), jnp.float32), 'out_b': jnp.zeros((H,), jnp.float32), 'postnorm_w': jnp.ones((H,), jnp.float32), 'mlp_w1': s * jax.random.normal(ks[6], (H, 4 * H), jnp.float32), 'mlp_b1': jnp.zeros((4 * H,), jnp.float32), 'mlp_w2': s * jax.random.normal(ks[7], (4 * H, H), jnp.float32), 'mlp_b2': jnp.zeros((H,), jnp.float32)}
    _L1_xattn_all = _L1_xattn_setup()
    _L1_xattn_in = {k: v for k, v in _L1_xattn_all.items() if k in ('q_w', 'q_b', 'kv_w', 'kv_b', 'out_w', 'out_b', 'postnorm_w', 'mlp_w1', 'mlp_b1', 'mlp_w2', 'mlp_b2')}
    del _L1_xattn_all

    def _L2_xattn_setup():
        import jax, jax.numpy as jnp
        import numpy as np
        H = 512
        NH = 32
        KVH = 8
        HD = H // NH
        GROUPS = NH // KVH
        EPS = 1e-06
        B, L, S = (4, 256, 256)

        def _gqa_forward(hidden_state, encoder_hidden_state, encoder_attention_mask, Wq, bq, Wk, bk, Wv, bv, Wo, bo, gamma, beta):
            b, l, _ = hidden_state.shape
            s = encoder_hidden_state.shape[1]
            q = hidden_state @ Wq + bq
            k = encoder_hidden_state @ Wk + bk
            v = encoder_hidden_state @ Wv + bv
            q = q.reshape(b, l, KVH, GROUPS, HD).transpose(0, 2, 3, 1, 4)
            k = k.reshape(b, s, KVH, HD).transpose(0, 2, 1, 3)
            v = v.reshape(b, s, KVH, HD).transpose(0, 2, 1, 3)
            scale = 1.0 / jnp.sqrt(jnp.asarray(HD, q.dtype))
            scores = jnp.einsum('bkgld,bksd->bkgls', q, k) * scale
            scores = scores + encoder_attention_mask[:, :, None, :, :]
            attn = jax.nn.softmax(scores, axis=-1)
            out = jnp.einsum('bkgls,bksd->bkgld', attn, v)
            out = out.transpose(0, 3, 1, 2, 4).reshape(b, l, H)
            out = out @ Wo + bo
            x = out + hidden_state
            mu = jnp.mean(x, axis=-1, keepdims=True)
            var = jnp.var(x, axis=-1, keepdims=True)
            return (x - mu) * jax.lax.rsqrt(var + EPS) * gamma + beta
        key = jax.random.key(seed)
        ks = jax.random.split(key, 12)
        sd = 0.02
        return {'hidden_state': jax.random.normal(ks[0], (B, L, H), jnp.float32), 'encoder_hidden_state': jax.random.normal(ks[1], (B, S, H), jnp.float32), 'encoder_attention_mask': jnp.zeros((B, 1, L, S), jnp.float32), 'Wq': jax.random.normal(ks[2], (H, H), jnp.float32) * sd, 'bq': jnp.zeros((H,), jnp.float32), 'Wk': jax.random.normal(ks[3], (H, KVH * HD), jnp.float32) * sd, 'bk': jnp.zeros((KVH * HD,), jnp.float32), 'Wv': jax.random.normal(ks[4], (H, KVH * HD), jnp.float32) * sd, 'bv': jnp.zeros((KVH * HD,), jnp.float32), 'Wo': jax.random.normal(ks[5], (H, H), jnp.float32) * sd, 'bo': jnp.zeros((H,), jnp.float32), 'gamma': jnp.ones((H,), jnp.float32), 'beta': jnp.zeros((H,), jnp.float32)}
    _L2_xattn_all = _L2_xattn_setup()
    _L2_xattn_in = {k: v for k, v in _L2_xattn_all.items() if k in ('Wq', 'bq', 'Wk', 'bk', 'Wv', 'bv', 'Wo', 'bo', 'gamma', 'beta')}
    del _L2_xattn_all

    def _L3_xattn_setup():
        import math
        import jax, jax.numpy as jnp
        import numpy as np
        C = 256
        H = 16
        DH = C // H
        EPS = 1e-05

        def pos_enc(c, T, dtype):
            pos = jnp.arange(T, dtype=jnp.float32)[:, None]
            div = jnp.exp(jnp.arange(0, c, 2, dtype=jnp.float32) * (-math.log(10000.0) / c))
            ang = pos * div
            pe = jnp.zeros((T, c), dtype=jnp.float32)
            pe = pe.at[:, 0::2].set(jnp.sin(ang)).at[:, 1::2].set(jnp.cos(ang))
            return pe.T.astype(dtype)

        def layer_norm(x, g, b):
            mu = jnp.mean(x, axis=-1, keepdims=True)
            var = jnp.mean(jnp.square(x - mu), axis=-1, keepdims=True)
            return (x - mu) * jax.lax.rsqrt(var + EPS) * g + b
        key = jax.random.key(seed)
        ks = jax.random.split(key, 16)
        s = 1.0 / math.sqrt(C)
        inp = {'zt_prev': jax.random.normal(ks[0], (2, C, 512), jnp.float32), 'za': jax.random.normal(ks[1], (2, C, 512), jnp.float32), 'Wq': jax.random.normal(ks[2], (C, C), jnp.float32) * s, 'Wk': jax.random.normal(ks[3], (C, C), jnp.float32) * s, 'Wv': jax.random.normal(ks[4], (C, C), jnp.float32) * s, 'Wo': jax.random.normal(ks[5], (C, C), jnp.float32) * s, 'ln_q_g': jnp.ones((C,), jnp.float32), 'ln_q_b': jnp.zeros((C,), jnp.float32), 'ln_kv_g': jnp.ones((C,), jnp.float32), 'ln_kv_b': jnp.zeros((C,), jnp.float32), 'ffn_ln_g': jnp.ones((C,), jnp.float32), 'ffn_ln_b': jnp.zeros((C,), jnp.float32), 'W1': jax.random.normal(ks[6], (C, 2 * C), jnp.float32) * s, 'b1': jnp.zeros((2 * C,), jnp.float32), 'W2': jax.random.normal(ks[7], (2 * C, C), jnp.float32) * (1.0 / math.sqrt(2 * C)), 'b2': jnp.zeros((C,), jnp.float32)}
        return inp
    _L3_xattn_all = _L3_xattn_setup()
    _L3_xattn_in = {k: v for k, v in _L3_xattn_all.items() if k in ('Wq', 'Wk', 'Wv', 'Wo', 'ln_q_g', 'ln_q_b', 'ln_kv_g', 'ln_kv_b', 'ffn_ln_g', 'ffn_ln_b', 'W1', 'b1', 'W2', 'b2')}
    del _L3_xattn_all
    return {'x': x, 'ctx_2048': ctx_2048, 'mask_Bx1x2048_bf1': mask_Bx1x2048_bf1, 'mask_BxS2_ik0': mask_BxS2_ik0, 'mask_Bx1xSxS2_ff0': mask_Bx1xSxS2_ff0, 'L0_xattn_Wq': _L0_xattn_in['Wq'], 'L0_xattn_bq': _L0_xattn_in['bq'], 'L0_xattn_Wk': _L0_xattn_in['Wk'], 'L0_xattn_bk': _L0_xattn_in['bk'], 'L0_xattn_Wv': _L0_xattn_in['Wv'], 'L0_xattn_bv': _L0_xattn_in['bv'], 'L1_xattn_q_w': _L1_xattn_in['q_w'], 'L1_xattn_q_b': _L1_xattn_in['q_b'], 'L1_xattn_kv_w': _L1_xattn_in['kv_w'], 'L1_xattn_kv_b': _L1_xattn_in['kv_b'], 'L1_xattn_out_w': _L1_xattn_in['out_w'], 'L1_xattn_out_b': _L1_xattn_in['out_b'], 'L1_xattn_postnorm_w': _L1_xattn_in['postnorm_w'], 'L1_xattn_mlp_w1': _L1_xattn_in['mlp_w1'], 'L1_xattn_mlp_b1': _L1_xattn_in['mlp_b1'], 'L1_xattn_mlp_w2': _L1_xattn_in['mlp_w2'], 'L1_xattn_mlp_b2': _L1_xattn_in['mlp_b2'], 'L2_xattn_Wq': _L2_xattn_in['Wq'], 'L2_xattn_bq': _L2_xattn_in['bq'], 'L2_xattn_Wk': _L2_xattn_in['Wk'], 'L2_xattn_bk': _L2_xattn_in['bk'], 'L2_xattn_Wv': _L2_xattn_in['Wv'], 'L2_xattn_bv': _L2_xattn_in['bv'], 'L2_xattn_Wo': _L2_xattn_in['Wo'], 'L2_xattn_bo': _L2_xattn_in['bo'], 'L2_xattn_gamma': _L2_xattn_in['gamma'], 'L2_xattn_beta': _L2_xattn_in['beta'], 'L3_xattn_Wq': _L3_xattn_in['Wq'], 'L3_xattn_Wk': _L3_xattn_in['Wk'], 'L3_xattn_Wv': _L3_xattn_in['Wv'], 'L3_xattn_Wo': _L3_xattn_in['Wo'], 'L3_xattn_ln_q_g': _L3_xattn_in['ln_q_g'], 'L3_xattn_ln_q_b': _L3_xattn_in['ln_q_b'], 'L3_xattn_ln_kv_g': _L3_xattn_in['ln_kv_g'], 'L3_xattn_ln_kv_b': _L3_xattn_in['ln_kv_b'], 'L3_xattn_ffn_ln_g': _L3_xattn_in['ffn_ln_g'], 'L3_xattn_ffn_ln_b': _L3_xattn_in['ffn_ln_b'], 'L3_xattn_W1': _L3_xattn_in['W1'], 'L3_xattn_b1': _L3_xattn_in['b1'], 'L3_xattn_W2': _L3_xattn_in['W2'], 'L3_xattn_b2': _L3_xattn_in['b2']}

def reference(x, ctx_2048, mask_Bx1x2048_bf1, mask_BxS2_ik0, mask_Bx1xSxS2_ff0, L0_xattn_Wq, L0_xattn_bq, L0_xattn_Wk, L0_xattn_bk, L0_xattn_Wv, L0_xattn_bv, L1_xattn_q_w, L1_xattn_q_b, L1_xattn_kv_w, L1_xattn_kv_b, L1_xattn_out_w, L1_xattn_out_b, L1_xattn_postnorm_w, L1_xattn_mlp_w1, L1_xattn_mlp_b1, L1_xattn_mlp_w2, L1_xattn_mlp_b2, L2_xattn_Wq, L2_xattn_bq, L2_xattn_Wk, L2_xattn_bk, L2_xattn_Wv, L2_xattn_bv, L2_xattn_Wo, L2_xattn_bo, L2_xattn_gamma, L2_xattn_beta, L3_xattn_Wq, L3_xattn_Wk, L3_xattn_Wv, L3_xattn_Wo, L3_xattn_ln_q_g, L3_xattn_ln_q_b, L3_xattn_ln_kv_g, L3_xattn_ln_kv_b, L3_xattn_ffn_ln_g, L3_xattn_ffn_ln_b, L3_xattn_W1, L3_xattn_b1, L3_xattn_W2, L3_xattn_b2):
    import jax
    import jax.numpy as jnp

    def _L0_xattn_ref(x, mask, kv, kv_mask, Wq, bq, Wk, bk, Wv, bv):
        import jax, jax.numpy as jnp
        import numpy as np
        import math
        N_HEADS = 16
        EPS = 1e-05

        def _masked_instance_norm(x, mask):
            m = mask.astype(x.dtype)
            x = x * m
            n_valid = jnp.sum(m, axis=-1, keepdims=True)
            mean = jnp.sum(x, axis=-1, keepdims=True) / n_valid
            var = jnp.sum(x * x, axis=-1, keepdims=True) / n_valid - mean * mean
            x = (x - mean) / jnp.sqrt(jax.nn.relu(var) + EPS)
            return x * m
        bs, c, t1 = x.shape
        h = N_HEADS
        d = c // h
        scale = 1.0 / math.sqrt(d)
        q = jnp.einsum('oc,bct->bot', Wq, x) + bq[None, :, None]
        k = jnp.einsum('oc,bct->bot', Wk, kv) + bk[None, :, None]
        v = jnp.einsum('oc,bct->bot', Wv, kv) + bv[None, :, None]
        q = q.reshape(bs, h, d, t1).transpose(0, 1, 3, 2)
        k = k.reshape(bs, h, d, -1)
        v = v.reshape(bs, h, d, -1).transpose(0, 1, 3, 2)
        attn = jnp.einsum('bhqd,bhdk->bhqk', q * scale, k)
        attn = jnp.where(kv_mask[:, :, None, :], attn, -jnp.inf)
        attn = jax.nn.softmax(attn, axis=-1)
        mean = jnp.einsum('bhqk,bhkd->bhqd', attn, v)
        ex2 = jnp.einsum('bhqk,bhkd->bhqd', attn, v * v)
        std = jnp.sqrt(jax.nn.relu(ex2 - mean * mean))
        mean = mean.transpose(0, 1, 3, 2).reshape(bs, c, t1)
        std = std.transpose(0, 1, 3, 2).reshape(bs, c, t1)
        xn = _masked_instance_norm(x, mask)
        out = (xn * std + mean) * mask.astype(x.dtype)
        return out

    def _L1_xattn_ref(x, latents, attention_mask, q_w, q_b, kv_w, kv_b, out_w, out_b, postnorm_w, mlp_w1, mlp_b1, mlp_w2, mlp_b2):
        import jax, jax.numpy as jnp
        import numpy as np
        B, P, K, H, NH = (4, 512, 64, 512, 16)
        DH = H // NH
        EPS = 1e-06

        def rmsnorm(x, w):
            var = jnp.mean(jnp.square(x), axis=-1, keepdims=True)
            return x * jax.lax.rsqrt(var + EPS) * w
        b, p, _ = x.shape
        k_len = latents.shape[1]
        residual = latents
        h = jnp.concatenate([x, latents], axis=1)
        q = (latents @ q_w + q_b).reshape(b, k_len, NH, DH)
        kv = (h @ kv_w + kv_b).reshape(b, p + k_len, NH, DH, 2)
        kmat, v = (kv[..., 0], kv[..., 1])
        attn = jnp.einsum('bkhd,bnhd->bhkn', q, kmat) / DH
        full_mask = jnp.concatenate([attention_mask.astype(bool), jnp.ones((b, k_len), bool)], axis=-1)
        attn = jnp.where(full_mask[:, None, None, :], attn, -jnp.inf)
        attn = jax.nn.softmax(attn.astype(jnp.float32), axis=-1).astype(q.dtype)
        attn_out = jnp.einsum('bhkn,bnhd->bkhd', attn, v).reshape(b, k_len, H)
        attn_out = attn_out @ out_w + out_b + residual
        out = rmsnorm(attn_out, postnorm_w)
        out = jax.nn.gelu(out @ mlp_w1 + mlp_b1) @ mlp_w2 + mlp_b2
        return out + residual

    def _L2_xattn_ref(hidden_state, encoder_hidden_state, encoder_attention_mask, Wq, bq, Wk, bk, Wv, bv, Wo, bo, gamma, beta):
        import jax, jax.numpy as jnp
        import numpy as np
        H = 512
        NH = 32
        KVH = 8
        HD = H // NH
        GROUPS = NH // KVH
        EPS = 1e-06
        B, L, S = (4, 256, 256)

        def _gqa_forward(hidden_state, encoder_hidden_state, encoder_attention_mask, Wq, bq, Wk, bk, Wv, bv, Wo, bo, gamma, beta):
            b, l, _ = hidden_state.shape
            s = encoder_hidden_state.shape[1]
            q = hidden_state @ Wq + bq
            k = encoder_hidden_state @ Wk + bk
            v = encoder_hidden_state @ Wv + bv
            q = q.reshape(b, l, KVH, GROUPS, HD).transpose(0, 2, 3, 1, 4)
            k = k.reshape(b, s, KVH, HD).transpose(0, 2, 1, 3)
            v = v.reshape(b, s, KVH, HD).transpose(0, 2, 1, 3)
            scale = 1.0 / jnp.sqrt(jnp.asarray(HD, q.dtype))
            scores = jnp.einsum('bkgld,bksd->bkgls', q, k) * scale
            scores = scores + encoder_attention_mask[:, :, None, :, :]
            attn = jax.nn.softmax(scores, axis=-1)
            out = jnp.einsum('bkgls,bksd->bkgld', attn, v)
            out = out.transpose(0, 3, 1, 2, 4).reshape(b, l, H)
            out = out @ Wo + bo
            x = out + hidden_state
            mu = jnp.mean(x, axis=-1, keepdims=True)
            var = jnp.var(x, axis=-1, keepdims=True)
            return (x - mu) * jax.lax.rsqrt(var + EPS) * gamma + beta
        return _gqa_forward(hidden_state, encoder_hidden_state, encoder_attention_mask, Wq, bq, Wk, bk, Wv, bv, Wo, bo, gamma, beta)

    def _L3_xattn_ref(zt_prev, za, Wq, Wk, Wv, Wo, ln_q_g, ln_q_b, ln_kv_g, ln_kv_b, ffn_ln_g, ffn_ln_b, W1, b1, W2, b2):
        import math
        import jax, jax.numpy as jnp
        import numpy as np
        C = 256
        H = 16
        DH = C // H
        EPS = 1e-05

        def pos_enc(c, T, dtype):
            pos = jnp.arange(T, dtype=jnp.float32)[:, None]
            div = jnp.exp(jnp.arange(0, c, 2, dtype=jnp.float32) * (-math.log(10000.0) / c))
            ang = pos * div
            pe = jnp.zeros((T, c), dtype=jnp.float32)
            pe = pe.at[:, 0::2].set(jnp.sin(ang)).at[:, 1::2].set(jnp.cos(ang))
            return pe.T.astype(dtype)

        def layer_norm(x, g, b):
            mu = jnp.mean(x, axis=-1, keepdims=True)
            var = jnp.mean(jnp.square(x - mu), axis=-1, keepdims=True)
            return (x - mu) * jax.lax.rsqrt(var + EPS) * g + b
        B, _, Tq = zt_prev.shape
        Tk = za.shape[-1]
        q = jnp.transpose(zt_prev + pos_enc(C, Tq, zt_prev.dtype)[None], (0, 2, 1))
        kv = jnp.transpose(za + pos_enc(C, Tk, za.dtype)[None], (0, 2, 1))
        q = layer_norm(q, ln_q_g, ln_q_b)
        kv = layer_norm(kv, ln_kv_g, ln_kv_b)

        def split(x):
            Bt, T, _ = x.shape
            return jnp.transpose(x.reshape(Bt, T, H, DH), (0, 2, 1, 3))
        Q = split(q @ Wq)
        K = split(kv @ Wk)
        V = split(kv @ Wv)
        attn = jnp.einsum('bhqd,bhkd->bhqk', Q, K) / math.sqrt(DH)
        ctx = jnp.einsum('bhqk,bhkd->bhqd', jax.nn.softmax(attn, axis=-1), V)
        ctx = jnp.transpose(ctx, (0, 2, 1, 3)).reshape(B, Tq, C)
        y = ctx @ Wo
        r = y + q
        h = layer_norm(r, ffn_ln_g, ffn_ln_b)
        h = jax.nn.gelu(h @ W1 + b1, approximate=False) @ W2 + b2
        out = h + r
        return jnp.transpose(out, (0, 2, 1))
    x = _L0_xattn_ref(x, mask_Bx1x2048_bf1, ctx_2048, mask_Bx1x2048_bf1, L0_xattn_Wq, L0_xattn_bq, L0_xattn_Wk, L0_xattn_bk, L0_xattn_Wv, L0_xattn_bv)
    x = _L1_xattn_ref(ctx_2048, x, mask_BxS2_ik0, L1_xattn_q_w, L1_xattn_q_b, L1_xattn_kv_w, L1_xattn_kv_b, L1_xattn_out_w, L1_xattn_out_b, L1_xattn_postnorm_w, L1_xattn_mlp_w1, L1_xattn_mlp_b1, L1_xattn_mlp_w2, L1_xattn_mlp_b2)
    x = _L2_xattn_ref(x, ctx_2048, mask_Bx1xSxS2_ff0, L2_xattn_Wq, L2_xattn_bq, L2_xattn_Wk, L2_xattn_bk, L2_xattn_Wv, L2_xattn_bv, L2_xattn_Wo, L2_xattn_bo, L2_xattn_gamma, L2_xattn_beta)
    x = _L3_xattn_ref(x, ctx_2048, L3_xattn_Wq, L3_xattn_Wk, L3_xattn_Wv, L3_xattn_Wo, L3_xattn_ln_q_g, L3_xattn_ln_q_b, L3_xattn_ln_kv_g, L3_xattn_ln_kv_b, L3_xattn_ffn_ln_g, L3_xattn_ffn_ln_b, L3_xattn_W1, L3_xattn_b1, L3_xattn_W2, L3_xattn_b2)
    return x

_drawn_inputs = setup_inputs


def setup_inputs(seed=0):
    import zlib

    import numpy as np

    out = dict(_drawn_inputs(seed))
    spreads = {'L0_xattn_bq': (0.0, 0.8),
     'L0_xattn_bk': (0.0, 2.0),
     'L0_xattn_bv': (0.0, 0.368),
     'L1_xattn_q_b': (0.0, 0.8),
     'L1_xattn_kv_b': (0.0, 0.8),
     'L1_xattn_out_b': (0.0, 2.0),
     'L1_xattn_postnorm_w': (1.0, 0.2),
     'L1_xattn_mlp_b1': (0.0, 0.349),
     'L1_xattn_mlp_b2': (0.0, 0.518),
     'L2_xattn_bq': (0.0, 0.8),
     'L2_xattn_bk': (0.0, 2.0),
     'L2_xattn_bv': (0.0, 0.8),
     'L2_xattn_bo': (0.0, 2.0),
     'L2_xattn_gamma': (1.0, 0.2),
     'L2_xattn_beta': (0.0, 2.0),
     'L3_xattn_ln_q_g': (1.0, 0.2),
     'L3_xattn_ln_q_b': (0.0, 0.1),
     'L3_xattn_ln_kv_g': (1.0, 0.2),
     'L3_xattn_ln_kv_b': (0.0, 0.1),
     'L3_xattn_ffn_ln_g': (1.0, 0.2),
     'L3_xattn_ffn_ln_b': (0.0, 0.1),
     'L3_xattn_b1': (0.0, 0.1),
     'L3_xattn_b2': (0.0, 0.1)}
    factors = {'L1_xattn_q_w': 8.0,
     'L1_xattn_kv_w': 8.0,
     'L1_xattn_out_w': 8.0,
     'L2_xattn_Wq': 8.0,
     'L2_xattn_Wk': 8.0,
     'L2_xattn_Wv': 3.159,
     'L2_xattn_Wo': 3.012}
    for name, (base, spread) in spreads.items():
        noise = np.random.default_rng([zlib.crc32(name.encode()), seed]).standard_normal(out[name].shape)
        drawn = base * np.exp(spread * noise) if base else spread * noise
        out[name] = jnp.asarray(drawn.astype(out[name].dtype))
    for name, factor in factors.items():
        out[name] = (out[name] * factor).astype(out[name].dtype)
    return out
```

```python
import numpy as np
import concourse.bass as bass
from concourse import mybir
from contextlib import ExitStack

COLS = [("bq0", 2), ("bk0", 2), ("qb1", 4), ("kb1", 4), ("pn1", 4), ("mb1", 16), ("bq2", 4), ("bk2", 1),
        ("gkv3", 2), ("bkv3", 2), ("gf3", 2), ("bf3", 2), ("b13", 4), ("b23", 2)]
ROWS = [("bv0", 256), ("vb1", 512), ("ob1", 512), ("mb2", 512), ("bv2", 128), ("bo2", 512), ("g2", 512), ("be2", 512),
        ("gq3", 256), ("bq3", 256)]
B, HALVES = 8, 2
NEG = 1e30


class Engine:

    def __init__(self, sem):
        self.ops, self.sem, self.n, self.seen = [], sem, 0, {}

    def wait(self, *tokens):
        for t in tokens:
            if t is None:
                continue
            if isinstance(t, list):
                self.wait(*t)
                continue
            sem, value = t
            if self.seen.get(id(sem), 0) < value:
                self.seen[id(sem)] = value
                self.ops.append(lambda e, s=sem, v=value: e.wait_ge(s, v))

    def do(self, f, *waits):
        self.wait(*waits)
        self.n += 1
        self.ops.append(lambda e: f(e).then_inc(self.sem, 1))
        return (self.sem, self.n)

    def quiet(self, f, *waits):
        self.wait(*waits)
        self.ops.append(f)

    def last(self):
        return (self.sem, self.n) if self.n else None

    def run(self, e):
        for f in self.ops:
            f(e)


class Dma(Engine):

    def __init__(self, sems):
        super().__init__(None)
        self.sems, self.count, self.k = sems, [0] * len(sems), 0

    def go(self, out, in_, *waits):
        i = self.k % len(self.sems)
        self.k += 1
        s = self.sems[i]
        if self.count[i]:
            self.wait((s, self.count[i]))
        self.wait(*waits)
        self.count[i] += 16
        self.ops.append(lambda e: e.dma_start(out, in_).then_inc(s, 16))
        return (s, self.count[i])

    def all(self):
        return [(s, c) for s, c in zip(self.sems, self.count) if c]


class Slot:

    def __init__(self, t):
        self.t, self.ready, self._free, self.taken = t, [], [], False

    @property
    def free(self):
        return self._free

    @free.setter
    def free(self, tokens):
        self._free, self.taken = tokens, False


class Ring:
    def __init__(self, slots):
        self.slots, self.k = slots, 0

    def next(self):
        s = self.slots[self.k % len(self.slots)]
        self.k += 1
        assert not s.taken, "the slot's last reader isn't queued yet"
        s.taken = True
        return s


def merge(*lists):
    placed = []
    for n, (steps, start, end) in enumerate(lists):
        for i, f in enumerate(steps):
            placed.append((start + (end - start) * (i + 0.5) / len(steps), n, i, f))
    for _, _, _, f in sorted(placed, key=lambda x: x[:3]):
        f()


def build_program(nc, I, out, batches=B):
    fp32, bf16, u8, i32 = mybir.dt.float32, mybir.dt.bfloat16, mybir.dt.uint8, mybir.dt.int32
    ALU, ACT, AX = mybir.AluOpType, mybir.ActivationFunctionType, mybir.AxisListType
    ctx = ExitStack()
    with ctx:
        sem = lambda n: ctx.enter_context(nc.semaphore(n))
        pe, act, dve, pool = Engine(sem("s_pe")), Engine(sem("s_act")), Engine(sem("s_dve")), Engine(sem("s_pool"))
        sp = Dma([sem(f"s_dma{i}") for i in range(48)])
        PS = ctx.enter_context(nc.psum_tensor("PS", [128, 8, 512], fp32))
        bankA = Ring([Slot(PS[:, i, :]) for i in (0, 1)])
        pairC = Ring([Slot(PS[:, i:i + 2, :]) for i in (2, 4)])
        bankV, bankS = Slot(PS[:, 6, :]), Slot(PS[:, 7, :])

        x1 = nc.dram_tensor("x1_scratch", [B, 256, 512], fp32, kind="Internal").ap()
        y1 = nc.dram_tensor("y1_scratch", [B, 256, 512], fp32, kind="Internal").ap()
        x2 = nc.dram_tensor("x2_scratch", [B, 256, 512], fp32, kind="Internal").ap()
        x3 = nc.dram_tensor("x3_scratch", [B, 256, 512], fp32, kind="Internal").ap()
        NSCR = 4
        scrq = Ring([Slot(nc.dram_tensor(f"q_scratch{i}", [128 * 3 * 512], bf16, kind="Internal").ap()) for i in range(NSCR)])
        scrk = Ring([Slot(nc.dram_tensor(f"k_scratch{i}", [128 * 3 * 1024], bf16, kind="Internal").ap()) for i in range(NSCR)])

        sb_of = lambda c, layer="": (lambda n, shape, dt=fp32: c.enter_context(nc.sbuf_tensor(layer + n, shape, dt)))
        sbg = sb_of(ctx)
        cols = sbg("cols", [128, sum(n for _, n in COLS)])
        col, at = {}, 0
        for n, w in COLS:
            col[n] = cols[:, at:at + w]
            at += w
        row_at, at = {}, 0
        for n, w in ROWS:
            row_at[n] = (at, w)
            at += w
        ident = sbg("ident", [128, 128])
        ones = sbg("ones", [128, 32])
        t_cols = sp.go(cols[:, :], I["cols"])
        t_id0 = pool.do(lambda e: e.memset(ident[:, :], 0.0))
        t_id = pool.do(lambda e: e.affine_select(out=ident[:, :], in_=ident[:, :], compare_op=ALU.not_equal, fill=1.0,
                                                 base=0, pattern=[[-1, 128]], channel_multiplier=1), t_id0)
        t_ones = pool.do(lambda e: e.memset(ones[:, :], 1.0))
        for e in (act, dve):
            e.wait(t_cols)
        pe.wait(t_id, t_ones)

        def barrier():
            tokens = [x.last() for x in (pe, act, dve, pool)] + sp.all()
            for x in (pe, act, dve, pool, sp):
                x.wait(*tokens)

        def load_rows(sb, names):
            r = {}
            for n in names:
                a, w = row_at[n]
                t = sb("row_" + n, [128, w])
                r[n] = t
                dve.wait(sp.go(t[:, :], I["rows"][0:1, a:a + w].broadcast_to([128, w])))
            return r

        def load_w(sb, name, k, n):
            t = sb("w_" + name, [128, k, n])
            pe.wait(sp.go(t[:, :, :], I[name].rearrange("(k p) n -> p k n", p=128)))
            return t

        def project(bank, lo, hi, pairs, *waits):
            pe.wait(bank.free, *waits)
            for i, (l, r) in enumerate(pairs[:-1]):
                pe.quiet(lambda e, l=l, r=r, i=i: e.matmul(bank.t[:, lo:hi], l, r, start=(i == 0), stop=False,
                                                           skip_group_check=True))
            l, r = pairs[-1]
            return pe.do(lambda e: e.matmul(bank.t[:, lo:hi], l, r, start=(len(pairs) == 1), stop=True,
                                            skip_group_check=True))

        def split3(src, n_part, t_src, T, tmp, bias=None, sign=1.0):
            r = tmp.t
            b = 0.0 if bias is None else bias
            a0 = act.do(lambda e: e.activation(T[0], src, ACT.Identity, bias=b, scale=sign), t_src)
            if bias is None:
                d0 = dve.do(lambda e: e.scalar_tensor_tensor(out=r, in0=src, scalar=sign, in1=T[0], op0=ALU.mult,
                                                             op1=ALU.subtract), a0, tmp.free)
            else:
                d0 = dve.do(lambda e: e.scalar_tensor_tensor(out=r, in0=src, scalar=bias, in1=T[0], op0=ALU.add,
                                                             op1=ALU.subtract), a0, tmp.free)
            d1 = dve.do(lambda e: e.tensor_copy(T[1], r), d0)
            d2 = dve.do(lambda e: e.tensor_tensor(T[2], r, T[1], ALU.subtract), d1)
            tmp.free = [d2]
            return [a0, d1, d2], d0

        def stack(dst, free, T, t_T, scr, parts, nt, d, cols_):
            view = scr.t[0:128 * 3 * nt * cols_].rearrange("(i n p q) -> i n p q", i=3, n=nt, p=128)
            w = sp.go(view.rearrange("i n p q -> p i n q"), T, t_T, scr.free)
            ready = []
            for rows, i in parts:
                ready.append(sp.go(rows, view[i].rearrange("n (h d) q -> d (n h) q", d=d), w, free))
            scr.free = ready
            return w, ready

        def transposes(dsts, srcs, bank, *waits):
            pe.wait(bank.free, *waits)
            for d, s in list(zip(dsts, srcs))[:-1]:
                pe.quiet(lambda e, d=d, s=s: e.transpose(d, s, ident[0:s.shape[0], 0:s.shape[0]]))
            return pe.do(lambda e: e.transpose(dsts[-1], srcs[-1], ident[0:srcs[-1].shape[0], 0:srcs[-1].shape[0]]))

        def maxima_rows(M, t_M, nh, nqt, MT, tmp, Q, extra=None):
            bank = bankA.next()
            w = nqt * 128
            t = transposes([bank.t[0:nh, q * 128:(q + 1) * 128] for q in range(nqt)],
                           [M.t[:, q, 0:nh] for q in range(nqt)], bank, t_M)
            M.free = [t]
            act.wait(MT.free)
            dve.wait(MT.free)
            tmpv = Slot(tmp.t[0:nh, 0:w])
            tmpv.free = tmp.free
            tk, rd = split3(bank.t[0:nh, 0:w], nh, t, [MT.t[0:nh, i, 0:w] for i in range(3)], tmpv, sign=-1.0)
            tmp.free = tmpv.free
            bank.free = [rd, tk[0]]
            r = [sp.go(Q[97 + i:98 + i, :, :], MT.t[0:nh, i, 0:w], tk) for i in range(3)]
            MT.free = r
            return r

        def rstd_of(ms, var, eps, scale, *waits):
            a = dve.do(lambda e: e.tensor_scalar(ms, var, scale, eps, ALU.mult, ALU.add), *waits)
            s = act.do(lambda e: e.activation(ms, ms, ACT.Sqrt), a)
            return dve.do(lambda e: e.reciprocal(ms, ms), s)

        class Item:
            pass

        def pipeline(items, a1, a2, c, p, spans=((0.0, 0.9), (0.0, 0.75), (0.0, 1.0), (0.0, 1.0))):
            n = len(items)
            stages = (a1, a2, c, p)
            for i in range(-2, n + 1):
                lists = []
                for s, (f, span) in enumerate(zip(stages, spans)):
                    k = i + 2 - s
                    if 0 <= k < n:
                        steps = f(items[k])
                        if steps:
                            lists.append((steps, *span))
                merge(*lists)

        def items_of():
            out_ = []
            for b in range(batches):
                shared = Item()
                for h in range(HALVES):
                    it = Item()
                    it.b, it.h, it.s = b, h, shared
                    out_.append(it)
            return out_

        def attend(it, heads, nkt, w, scale, Pring, lhs, vones, spread=4):
            steps = []
            pend = []

            def scores(h):
                def f():
                    P = Pring.next()
                    P.ready = []
                    per = 1024 // w
                    for c0 in range(0, nkt, per):
                        pair = pairC.next()
                        pe.wait(pair.free, it.t_rows, it.st.ready, it.t_stack)
                        flat = pair.t.rearrange("p a b -> p (a b)")
                        for i in range(per):
                            mm = lhs(h, c0 + i)
                            for m, (l, r) in enumerate(mm):
                                o = flat[:, i * w:(i + 1) * w]
                                g = lambda e, o=o, l=l, r=r, m=m, k=len(mm): e.matmul(
                                    o, l, r, start=(m == 0), stop=(m == k - 1), skip_group_check=True)
                                if i == per - 1 and m == len(mm) - 1:
                                    t = pe.do(g)
                                else:
                                    pe.quiet(g)
                        po = P.t[:, c0 * w:(c0 + per) * w]
                        a = act.do(lambda e, po=po, flat=flat: e.activation(po, flat, ACT.Exp, scale=scale), t, P.free)
                        pair.free = [a]
                        P.ready.append(a)
                    pend.append((h, P))
                    it.last_st = t
                return f

            def values(g, kt):
                def f():
                    four = pend[4 * g:4 * g + 4]
                    pe.wait(*[P.ready for _, P in four], it.t_V)
                    pe.wait(bankV.free if kt == 0 else None)
                    if vones:
                        pe.wait(bankS.free if kt == 0 else None)
                    for j, (h, P) in enumerate(four):
                        o = bankV.t[32 * j:32 * j + 32, 0:w]
                        r = P.t[:, kt * w:(kt + 1) * w]
                        pe.quiet(lambda e, o=o, r=r, l=it.V(kt, h), j=j: e.matmul(
                            o, l, r, start=(kt == 0), stop=(kt == nkt - 1), tile_position=(0, 32 * j), skip_group_check=True))
                    if vones:
                        for j, (h, P) in enumerate(four):
                            o = bankS.t[32 * j:32 * j + 32, 0:w]
                            r = P.t[:, kt * w:(kt + 1) * w]
                            pe.quiet(lambda e, o=o, r=r, j=j: e.matmul(
                                o, ones[:, :], r, start=(kt == 0), stop=(kt == nkt - 1), tile_position=(0, 32 * j),
                                skip_group_check=True))
                    f_last = pe.ops.pop()
                    t = pe.do(f_last)
                    if kt == nkt - 1:
                        for _, P in four:
                            P.free = [t]
                        it.group_done(g, t)
                return f

            ng = len(heads) // 4
            for i, h in enumerate(heads):
                steps.append(scores(h))
                if i >= 4 and (i - 4) % 4 < spread:
                    for kt in range((i - 4) % 4 * nkt // spread, ((i - 4) % 4 + 1) * nkt // spread):
                        steps.append(values((i - 4) // 4, kt))
            for kt in range(nkt):
                steps.append(values(ng - 1, kt))
            return steps

        def mask_row(dst, msk, t_m, ne, nh, free):
            return sp.go(dst, msk[0:1, None, 0:ne].broadcast_to([1, nh, ne]), t_m, free)

        def layer0():
            with ExitStack() as lc:
                sb = sb_of(lc, "l0_")
                rows = load_rows(sb, ["bv0"])
                wq, wk, wv = (load_w(sb, n, 2, 256) for n in ("WqT0", "WkT0", "WvT0"))
                X = Ring([Slot(sb(f"X{i}", [128, 2, 512])) for i in range(3)])
                C = Ring([Slot(sb(f"C{i}", [128, 2, 512])) for i in range(2)])
                MK8 = Ring([Slot(sb(f"MK8{i}", [128, 512], u8)) for i in range(3)])
                MK = Ring([Slot(sb(f"MK{i}", [128, 512])) for i in range(3)])
                MB = Ring([Slot(sb(f"MB{i}", [1, 512], bf16)) for i in range(2)])
                ST = Ring([Slot((sb(f"QS{i}", [128, 8, 512], bf16), sb(f"KS{i}", [128, 8, 512], bf16))) for i in range(3)])
                T = Ring([Slot(sb(f"T{i}", [128, 3, 1, 512], bf16)) for i in range(2)])
                tmp = Ring([Slot(sb(f"tmp{i}", [128, 512])) for i in range(2)])
                VV = Ring([Slot(sb(f"V{i}", [128, 4, 8, 32])) for i in range(3)])
                M = Ring([Slot(sb(f"M{i}", [128, 4, 8])) for i in range(2)])
                MT = Slot(sb("MT", [8, 3, 512], bf16))
                P = Ring([Slot(sb(f"P{i}", [128, 2048])) for i in range(8)])
                R = Ring([Slot(sb(f"R{i}", [128, 512])) for i in range(1)])
                E = Ring([Slot(sb(f"E{i}", [128, 512])) for i in range(2)])
                ME = Ring([Slot((sb(f"ME{i}", [128, 2, 512]), sb(f"EX{i}", [128, 2, 512]))) for i in range(2)])
                OUT = Slot(sb("OUT", [128, 2, 512]))
                sm = sb("sm", [128, 16])
                smj = Slot(sb("smj", [128, 512]))
                for s in ST.slots:
                    s.ready = [dve.do(lambda e, t=t: e.memset(t[96:100, :, :], 1.0)) for t in s.t]

                def a1(it):
                    s = it.s
                    it.st, it.vv, it.m = ST.next(), VV.next(), M.next()
                    QS, KS = it.st.t
                    steps = []

                    def load():
                        s.X, s.C, s.mk8, s.mk, s.mb = X.next(), C.next(), MK8.next(), MK.next(), MB.next()
                        s.tX = sp.go(s.X.t[:, :, :], I["x"][it.b].rearrange("(n p) t -> p n t", p=128), s.X.free)
                        s.tC = sp.go(s.C.t[:, :, :], I["ctx"][it.b].rearrange("(n p) t -> p n t", p=128), s.C.free)
                        t8 = sp.go(s.mk8.t[:, :], I["mask0"][it.b].broadcast_to([128, 512]), s.mk8.free)
                        s.tmk = dve.do(lambda e: e.tensor_copy(s.mk.t[:, :], s.mk8.t[:, :]), t8, s.mk.free)
                        s.tmb = dve.do(lambda e: e.tensor_scalar(s.mb.t[:, :], s.mk.t[0:1, :], -1.0, NEG, ALU.add, ALU.mult),
                                       s.tmk, s.mb.free)
                        s.mk8.free = [s.tmk]
                        s.mb.free = []

                    def qk(w, src, tsrc, bias, dst, scr, order):
                        def f():
                            bank, Tn, tm = bankA.next(), T.next(), tmp.next()
                            t = project(bank, 0, 512, [(w[:, c, it.h * 128:it.h * 128 + 128], src()[:, c, :]) for c in range(2)],
                                        tsrc())
                            act.wait(Tn.free)
                            dve.wait(Tn.free)
                            tv = Slot(tm.t[:, :])
                            tv.free = tm.free
                            tk, rd = split3(bank.t[:, :], 128, t, [Tn.t[:, i, 0, :] for i in range(3)], tv,
                                            bias=bias[:, it.h:it.h + 1])
                            tm.free = tv.free
                            bank.free = [rd, tk[0]]
                            wr, ready = stack(dst, it.st.free, Tn.t[:, :, :, :], tk, scr.next(),
                                              [(dst[16 * r:16 * r + 16, :, :], i) for r, i in enumerate(order)], 1, 16, 512)
                            Tn.free = [wr]
                            it.t_stack += ready
                        return f

                    def vproj(tp):
                        def f():
                            bank = bankA.next()
                            for k in range(2):
                                tt = 2 * tp + k
                                t = project(bank, 128 * k, 128 * k + 128,
                                            [(s.C.t[:, c, tt * 128:tt * 128 + 128], wv[:, c, it.h * 128:it.h * 128 + 128])
                                             for c in range(2)], s.tC)
                                bank.free = []
                            Vt = it.vv.t
                            br = rows["bv0"][:, it.h * 128:it.h * 128 + 128].rearrange("p (h d) -> p h d", d=16)
                            dv = []
                            for k in range(2):
                                src = bank.t[:, 128 * k:128 * k + 128].rearrange("p (h d) -> p h d", d=16)
                                dv.append(dve.do(lambda e, k=k, src=src: e.tensor_tensor(
                                    Vt[:, 2 * tp + k, :, 0:16], src, br, ALU.add), t, it.vv.free))
                            bank.free = dv
                            it.t_V += dv
                            for k in range(2):
                                v = Vt[:, 2 * tp + k, :, 0:16]
                                it.t_V.append(pool.do(lambda e, k=k, v=v: e.tensor_tensor(
                                    Vt[:, 2 * tp + k, :, 16:32], v, v, ALU.mult), dv[k], it.vv.free))
                            s.C.free = [t]
                        return f

                    def mrow():
                        it.t_stack.append(mask_row(KS[96:97, :, :], s.mb.t, s.tmb, 512, 8, [it.st.free, it.st.ready]))
                        s.mb.free = s.mb.free + [it.t_stack[-1]]

                    it.t_stack, it.t_V = [], []
                    if it.h == 0:
                        steps.append(load)
                    steps.append(qk(wq, lambda: s.X.t, lambda: s.tX, col["bq0"], QS, scrq, [0, 0, 1, 0, 1, 2]))
                    steps.append(qk(wk, lambda: s.C.t, lambda: s.tC, col["bk0"], KS, scrk, [0, 1, 0, 2, 1, 0]))
                    steps.append(mrow)
                    steps += [vproj(0), vproj(1)]
                    it.V = lambda kt, h: it.vv.t[:, kt, h, :]
                    return steps

                def a2(it):
                    QS, KS = it.st.t
                    steps = []
                    tk = []

                    def smax(h, qt):
                        def f():
                            bank = bankA.next()
                            t = pe.do(lambda e: e.matmul(bank.t[:, :], QS[0:97, h, qt * 128:qt * 128 + 128], KS[0:97, h, :],
                                                         start=True, stop=True), bank.free, it.t_stack, it.st.ready)
                            d = dve.do(lambda e: e.tensor_reduce(it.m.t[:, qt, h:h + 1], bank.t[:, :], AX.X, ALU.max), t, it.m.free)
                            bank.free = [d]
                            tk.append(d)
                            it.last_s = t
                        return f
                    for qt in range(4):
                        for h in range(8):
                            steps.append(smax(h, qt))

                    def rows_():
                        tm = tmp.next()
                        it.t_rows = maxima_rows(it.m, [tk[-1]], 8, 4, MT, tm, QS)
                    steps.append(rows_)
                    return steps

                def c(it):
                    QS, KS = it.st.t

                    def group_done(g, t):
                        if g == 0 and it.h == 0:
                            it.s.me = ME.next()
                            it.s.t_me = []
                        r, E_ = R.next(), E.next()
                        me, ex = it.s.me.t
                        d = dve.do(lambda e: e.reciprocal(r.t[:, :], bankS.t[:, :]), t, r.free)
                        d2 = dve.do(lambda e: e.tensor_tensor(E_.t[:, :], bankV.t[:, :], r.t[:, :], ALU.mult), d, E_.free)
                        bankS.free, bankV.free, r.free = [d], [d2], [d2]
                        E_.free = []
                        for j in range(4):
                            for k, dst in enumerate((me, ex)):
                                p0 = 16 * (4 * g + j)
                                E_.free.append(sp.go(dst[p0:p0 + 16, it.h, :], E_.t[32 * j + 16 * k:32 * j + 16 * k + 16, :],
                                                     d2, it.s.me.free))
                        it.s.t_me += E_.free
                        if g == 1:
                            it.st.free = [t]
                            it.vv.free = [t]
                    it.group_done = group_done
                    return attend(it, list(range(8)), 4, 512, 0.25, P,
                                  lambda h, kt: [(KS[0:100, h, kt * 128:kt * 128 + 128], QS[0:100, h, :])], True)

                def p(it):
                    if it.h == 0:
                        return []
                    s = it.s
                    me, ex = s.me.t
                    Xt, mk = s.X.t, s.mk.t
                    o = OUT.t

                    def f1():
                        s.d = []
                        for n in range(2):
                            a = dve.do(lambda e, n=n: e.tensor_tensor_reduce(
                                out=Xt[:, n, :], in0=Xt[:, n, :], in1=mk[:, :], scale=1.0, scalar=0.0, op0=ALU.mult,
                                op1=ALU.add, accum_out=sm[:, n:n + 1]), s.tX, s.tmk, dve.last(), act.last(), pool.last(), s.xread)
                            b_ = act.do(lambda e, n=n: e.activation(o[:, n, :], Xt[:, n, :], ACT.Square,
                                                                    accum_out=sm[:, 2 + n:3 + n]), a, OUT.free, act.last())
                            s.d.append(b_)
                        s.n = dve.do(lambda e: e.tensor_reduce(sm[:, 4:5], mk[:, :], AX.X, ALU.add))

                    def f2():
                        t = dve.do(lambda e: e.reciprocal(sm[:, 5:6], sm[:, 4:5]), s.n)
                        t = dve.do(lambda e: e.tensor_scalar(sm[:, 6:10], sm[:, 0:4], sm[:, 5:6], None, ALU.mult), t, s.d)
                        t1 = dve.do(lambda e: e.tensor_tensor(sm[:, 10:12], sm[:, 6:8], sm[:, 6:8], ALU.mult), t)
                        t2 = dve.do(lambda e: e.tensor_tensor(sm[:, 12:14], sm[:, 8:10], sm[:, 10:12], ALU.subtract), t1)
                        t3 = dve.do(lambda e: e.tensor_scalar(sm[:, 12:14], sm[:, 12:14], 0.0, 1e-5, ALU.max, ALU.add), t2)
                        s.t3 = t3

                    def f3():
                        t = pool.do(lambda e: e.tensor_tensor(o[:, :, :], me[:, :, :], me[:, :, :], ALU.mult), s.t_me, s.d)
                        t = dve.do(lambda e: e.tensor_tensor(ex[:, :, :], ex[:, :, :], o[:, :, :], ALU.subtract), t)
                        t = dve.do(lambda e: e.tensor_scalar(ex[:, :, :], ex[:, :, :], 0.0, None, ALU.max), t)
                        s.t4 = act.do(lambda e: e.activation(ex[:, :, :], ex[:, :, :], ACT.Sqrt), t)
                        s.t5 = act.do(lambda e: e.activation(sm[:, 14:16], sm[:, 12:14], ACT.Sqrt), s.t3)

                    def f4():
                        t = dve.do(lambda e: e.reciprocal(sm[:, 12:14], sm[:, 14:16]), s.t5)
                        last = []
                        for n in range(2):
                            a = dve.do(lambda e, n=n: e.tensor_scalar(Xt[:, n, :], Xt[:, n, :], sm[:, 6 + n:7 + n],
                                                                      sm[:, 12 + n:13 + n], ALU.subtract, ALU.mult), t)
                            a = dve.do(lambda e, n=n: e.tensor_tensor(Xt[:, n, :], Xt[:, n, :], mk[:, :], ALU.mult), a)
                            a = dve.do(lambda e, n=n: e.tensor_tensor(Xt[:, n, :], Xt[:, n, :], ex[:, n, :], ALU.mult), a, s.t4)
                            a = dve.do(lambda e, n=n: e.tensor_tensor(Xt[:, n, :], Xt[:, n, :], me[:, n, :], ALU.add), a)
                            a = dve.do(lambda e, n=n: e.tensor_tensor(o[:, n, :], Xt[:, n, :], mk[:, :], ALU.mult), a)
                            last.append(a)
                        s.X.free = s.mk.free = s.me.free = last
                        OUT.free = [sp.go(x1[it.b].rearrange("(n p) t -> p n t", p=128), o[:, :, :], last)]
                    s.xread = it.t_xread
                    return [f1, f2, f3, f4]

                its = items_of()

                def a2w(it):
                    return a2(it)

                def cw(it):
                    it.t_xread = it.t_stack
                    return c(it)
                pipeline(its, a1, a2w, cw, p)
                barrier()

        def layer1a():
            with ExitStack() as lc:
                sb = sb_of(lc, "l1a_")
                rows = load_rows(sb, ["vb1", "ob1"])
                wq = load_w(sb, "q_w1", 4, 512)
                wk = load_w(sb, "k_w1", 4, 512)
                wv = load_w(sb, "v_w1", 4, 512)
                wo = load_w(sb, "out_w1", 4, 512)
                LAT = Ring([Slot(sb(f"LAT{i}", [128, 2, 512])) for i in range(3)])
                HT = Ring([Slot(sb(f"HT{i}", [128, 4, 512])) for i in range(1)])
                MI = Ring([Slot(sb(f"MI{i}", [1, 256], i32)) for i in range(1)])
                MF = Ring([Slot(sb(f"MF{i}", [1, 256])) for i in range(1)])
                MB = Ring([Slot(sb(f"MB{i}", [1, 512], bf16)) for i in range(2)])
                ST = Ring([Slot((sb(f"QA{i}", [128, 8, 256], bf16), sb(f"QB{i}", [96, 8, 256], bf16),
                                 sb(f"KA{i}", [128, 8, 512], bf16), sb(f"KB{i}", [96, 8, 512], bf16))) for i in range(3)])
                T = Ring([Slot(sb(f"T{i}", [128, 3, 2, 512], bf16)) for i in range(1)])
                tmp = Ring([Slot(sb(f"tmp{i}", [128, 512])) for i in range(1)])
                VV = Ring([Slot(sb(f"V{i}", [128, 4, 256])) for i in range(3)])
                M = Ring([Slot(sb(f"M{i}", [128, 2, 8])) for i in range(2)])
                MT = Slot(sb("MT", [8, 3, 256], bf16))
                P = Ring([Slot(sb(f"P{i}", [128, 1024])) for i in range(8)])
                R = Ring([Slot(sb(f"R{i}", [128, 256])) for i in range(1)])
                AT = Ring([Slot(sb(f"AT{i}", [128, 4, 256])) for i in range(2)])
                Y = Slot(sb("Y", [128, 2, 512]))
                sm = sb("sm", [128, 4])
                for s in ST.slots:
                    s.ready = [dve.do(lambda e, t=t: e.memset(t[96:100, :, :], 1.0)) for t in (s.t[0], s.t[2])]
                for s in MB.slots:
                    s.ready = [dve.do(lambda e, s=s: e.memset(s.t[:, 256:512], 0.0))]

                def a1(it):
                    s = it.s
                    it.st, it.vv, it.m = ST.next(), VV.next(), M.next()
                    QA, QB, KA, KB = it.st.t
                    it.t_stack, it.t_V = [], []
                    steps = []

                    def load():
                        s.L, s.H, s.mb = LAT.next(), HT.next(), MB.next()
                        mi, mf = MI.next(), MF.next()
                        s.tL = sp.go(s.L.t[:, :, :], x1[it.b].rearrange("(n p) t -> p n t", p=128), s.L.free)
                        s.tH = [sp.go(s.H.t[:, :, 0:256], I["ctxT"][it.b].rearrange("(n p) t -> p n t", p=128), s.H.free)]
                        t8 = sp.go(mi.t[:, :], I["mask1"][it.b:it.b + 1, :], mi.free)
                        a = dve.do(lambda e: e.tensor_scalar(mf.t[:, :], mi.t[:, :], 0.0, None, ALU.not_equal), t8, mf.free)
                        mi.free = [a]
                        s.tmb = dve.do(lambda e: e.tensor_scalar(s.mb.t[:, 0:256], mf.t[:, :], -1.0, NEG, ALU.add, ALU.mult),
                                       a, s.mb.free, s.mb.ready)
                        mf.free = [s.tmb]
                        s.mb.free = []

                    def lat_t(tt):
                        def f():
                            bank = bankA.next()
                            t = transposes([bank.t[:, q * 128:q * 128 + 128] for q in range(4)],
                                           [s.L.t[:, tt, q * 128:q * 128 + 128] for q in range(4)], bank, s.tL)
                            a = act.do(lambda e: e.activation(s.H.t[:, :, 256 + tt * 128:384 + tt * 128],
                                                              bank.t[:, :].rearrange("p (a b) -> p a b", a=4), ACT.Copy),
                                       t, s.H.free)
                            bank.free = [a]
                            s.tH.append(a)
                        return f

                    def qk(w, bias, dsts, scr, nc_, lo, which):
                        def f():
                            Tn = T.next()
                            act.wait(Tn.free)
                            dve.wait(Tn.free)
                            tks = []
                            for o in range(2):
                                og = 2 * it.h + o
                                bank, tm = bankA.next(), tmp.next()
                                t = project(bank, 0, nc_, [(w[:, c, og * 128:og * 128 + 128], s.H.t[:, c, lo:lo + nc_])
                                                           for c in range(4)], s.tH)
                                tv = Slot(tm.t[:, 0:nc_])
                                tv.free = tm.free
                                tk, rd = split3(bank.t[:, 0:nc_], 128, t, [Tn.t[:, i, o, 0:nc_] for i in range(3)], tv,
                                                bias=bias[:, og:og + 1])
                                tm.free = tv.free
                                bank.free = [rd, tk[0]]
                                tks += tk
                            wr, ready = stack(None, it.st.free, Tn.t[:, :, :, 0:nc_], tks, scr.next(),
                                              [(d[32 * r:32 * r + 32, :, :], i) for d, order in dsts for r, i in enumerate(order)],
                                              2, 32, nc_)
                            Tn.free = [wr]
                            it.t_stack += ready
                            if which:
                                s.H.free = [t]
                        return f

                    def vproj(tt):
                        def f():
                            bank = bankA.next()
                            t = project(bank, 0, 256, [(s.H.t[:, c, tt * 128:tt * 128 + 128],
                                                        wv[:, c, it.h * 256:it.h * 256 + 256]) for c in range(4)], s.tH)
                            d = dve.do(lambda e: e.tensor_tensor(it.vv.t[:, tt, :], bank.t[:, 0:256],
                                                                 rows["vb1"][:, it.h * 256:it.h * 256 + 256], ALU.add),
                                       t, it.vv.free)
                            bank.free = [d]
                            it.t_V.append(d)
                            s.H.free = [t]
                        return f

                    def mrow():
                        it.t_stack.append(mask_row(KA[96:97, :, :], s.mb.t, s.tmb, 512, 8, [it.st.free, it.st.ready]))
                        s.mb.free = s.mb.free + [it.t_stack[-1]]

                    if it.h == 0:
                        steps += [load, lat_t(0), lat_t(1)]
                    steps.append(qk(wq, col["qb1"], [(QA, [0, 0, 1]), (QB, [0, 1, 2])], scrq, 256, 256, False))
                    steps.append(qk(wk, col["kb1"], [(KA, [0, 1, 0]), (KB, [2, 1, 0])], scrk, 512, 0, True))
                    steps.append(mrow)
                    steps += [vproj(i) for i in range(4)]
                    it.V = lambda kt, h: it.vv.t[:, kt, h * 32:h * 32 + 32]
                    return steps

                def a2(it):
                    QA, QB, KA, KB = it.st.t
                    tk = []

                    def smax(h, qt):
                        def f():
                            bank = bankA.next()
                            t = pe.do(lambda e: e.matmul(bank.t[:, :], QA[0:97, h, qt * 128:qt * 128 + 128], KA[0:97, h, :],
                                                         start=True, stop=True), bank.free, it.t_stack, it.st.ready)
                            d = dve.do(lambda e: e.tensor_reduce(it.m.t[:, qt, h:h + 1], bank.t[:, :], AX.X, ALU.max), t, it.m.free)
                            bank.free = [d]
                            tk.append(d)
                        return f

                    def rows_():
                        it.t_rows = maxima_rows(it.m, [tk[-1]], 8, 2, MT, tmp.next(), QA)
                    return [smax(h, qt) for qt in range(2) for h in range(8)] + [rows_]

                def c(it):
                    QA, QB, KA, KB = it.st.t

                    def group_done(g, t):
                        if g == 0 and it.h == 0:
                            it.s.at = AT.next()
                            it.s.t_at = []
                        r = R.next()
                        d = dve.do(lambda e: e.reciprocal(r.t[:, :], bankS.t[:, 0:256]), t, r.free)
                        d2 = dve.do(lambda e: e.tensor_tensor(it.s.at.t[:, 2 * it.h + g, :], bankV.t[:, 0:256], r.t[:, :],
                                                              ALU.mult), d, it.s.at.free)
                        bankS.free, bankV.free, r.free = [d], [d2], [d2]
                        it.s.t_at.append(d2)
                        if g == 1:
                            it.st.free = [t]
                            it.vv.free = [t]
                    it.group_done = group_done
                    return attend(it, list(range(8)), 4, 256, 1.0 / 32, P,
                                  lambda h, kt: [(KA[0:100, h, kt * 128:kt * 128 + 128], QA[0:100, h, :]),
                                                 (KB[0:96, h, kt * 128:kt * 128 + 128], QB[0:96, h, :])], True)

                def p(it):
                    if it.h == 0:
                        return []
                    s = it.s

                    def f1():
                        s.sq = []
                        for tt in range(2):
                            bank = bankA.next()
                            t = project(bank, 0, 512, [(s.at.t[:, g, tt * 128:tt * 128 + 128], wo[:, g, :]) for g in range(4)],
                                        s.t_at)
                            a = dve.do(lambda e, tt=tt, bank=bank: e.tensor_tensor(Y.t[:, tt, :], bank.t[:, :], rows["ob1"][:, :],
                                                                                 ALU.add), t, Y.free)
                            bank.free = [a]
                            b_ = dve.do(lambda e, tt=tt: e.tensor_tensor(Y.t[:, tt, :], Y.t[:, tt, :], s.L.t[:, tt, :], ALU.add), a)
                            s.L.free = [b_]
                            j = s.L.t[:, tt, :]
                            c_ = act.do(lambda e, tt=tt, j=j: e.activation(j, Y.t[:, tt, :], ACT.Square,
                                                                           accum_out=sm[:, tt:tt + 1]), b_, dve.last(), act.last())
                            s.sq.append(c_)
                        s.at.free = [t]
                        s.L.free = s.L.free + [c_]

                    def f2():
                        t = rstd_of(sm[:, 0:2], sm[:, 0:2], 1e-6, 1.0 / 512, s.sq)
                        last = []
                        for tt in range(2):
                            last.append(dve.do(lambda e, tt=tt: e.tensor_scalar(Y.t[:, tt, :], Y.t[:, tt, :], sm[:, tt:tt + 1],
                                                                                None, ALU.mult), t))
                        Y.free = [sp.go(y1[it.b].rearrange("(n p) t -> p n t", p=128), Y.t[:, :, :], last)]
                    return [f1, f2]
                pipeline(items_of(), a1, a2, c, p)
                barrier()

        def layer1b():
            with ExitStack() as lc:
                sb = sb_of(lc, "l1b_")
                rows = load_rows(sb, ["mb2"])
                w1 = load_w(sb, "mlp_w1", 4, 2048)
                w2 = load_w(sb, "mlp_w2", 16, 512)
                YN = Ring([Slot(sb(f"YN{i}", [128, 4, 512])) for i in range(2)])
                YT = Slot(sb("YT", [128, 4, 512]))
                LT = Ring([Slot(sb(f"LT{i}", [128, 4, 512])) for i in range(2)])
                H1 = Slot(sb("H1", [128, 16, 512]))
                banks = Ring([Slot(PS[:, i, :]) for i in range(8)])
                for b in range(0, batches, 2):
                    nb = min(2, batches - b)
                    n4, w = 2 * nb, 256 * nb
                    yn, lt = YN.next(), LT.next()
                    ty = sp.go(yn.t[:, 0:n4, :], y1[b:b + nb].rearrange("b (n p) t -> p (b n) t", p=128), yn.free)
                    tl = sp.go(lt.t[:, 0:n4, :], x1[b:b + nb].rearrange("b (n p) t -> p (b n) t", p=128), lt.free)
                    ev = []
                    for f in range(4):
                        bank = banks.next()
                        t = transposes([bank.t[:, q * 128:q * 128 + 128] for q in range(n4)],
                                       [yn.t[:, q, f * 128:f * 128 + 128] for q in range(n4)], bank, ty)
                        d = dve.do(lambda e, f=f, bank=bank: e.tensor_scalar(YT.t[:, f, 0:w], bank.t[:, 0:w],
                                                                             col["pn1"][:, f:f + 1], None, ALU.mult), t, YT.free)
                        bank.free = [d]
                        ev.append(d)
                    yn.free = [t]
                    hs = []
                    for o in range(16):
                        bank = banks.next()
                        t = project(bank, 0, w, [(w1[:, c, o * 128:o * 128 + 128], YT.t[:, c, 0:w]) for c in range(4)], ev)
                        a = act.do(lambda e, o=o, bank=bank: e.activation(H1.t[:, o, 0:w], bank.t[:, 0:w], ACT.Gelu_apprx_tanh,
                                                                          bias=col["mb1"][:, o:o + 1]), t, H1.free)
                        bank.free = [a]
                        hs.append(a)
                    YT.free = [t]
                    last = []
                    for tt in range(n4):
                        bank = banks.next()
                        t = project(bank, 0, 512, [(H1.t[:, o, tt * 128:tt * 128 + 128], w2[:, o, :]) for o in range(16)], hs)
                        d = dve.do(lambda e, tt=tt, bank=bank, lt=lt: e.tensor_tensor(lt.t[:, tt, :], bank.t[:, :], lt.t[:, tt, :],
                                                                                      ALU.add), t, tl)
                        bank.free = [d]
                        last.append(dve.do(lambda e, tt=tt, lt=lt: e.tensor_tensor(lt.t[:, tt, :], lt.t[:, tt, :], rows["mb2"][:, :],
                                                                            ALU.add), d))
                    H1.free = [t]
                    lt.free = [sp.go(x2[b:b + nb].rearrange("b (n p) t -> p (b n) t", p=128), lt.t[:, 0:n4, :], last)]
                for s in bankA.slots + pairC.slots + [bankV, bankS]:
                    s.free = []
                barrier()

        def compact_normalize(it, R, NC, SC, DST, w, part, tk_in, dst_free):
            t = dve.do(lambda e: e.reciprocal(SC[:, part, 0:w], SC[:, part, 0:w]), tk_in)
            return dve.do(lambda e: e.tensor_tensor(DST, NC[:, part, 0:w], SC[:, part, 0:w], ALU.mult), t, dst_free)

        def layer2():
            with ExitStack() as lc:
                sb = sb_of(lc, "l2_")
                rows = load_rows(sb, ["bv2", "bo2", "g2", "be2"])
                wq = load_w(sb, "Wq2", 4, 512)
                wk = load_w(sb, "Wk2", 4, 128)
                wv = load_w(sb, "Wv2", 4, 128)
                wo = load_w(sb, "Wo2", 4, 512)
                X = Ring([Slot(sb(f"X{i}", [128, 2, 512])) for i in range(3)])
                XT = Ring([Slot(sb(f"XT{i}", [128, 4, 256])) for i in range(2)])
                CT = Ring([Slot(sb(f"CT{i}", [128, 4, 256])) for i in range(2)])
                MK = Ring([Slot((sb(f"MK{i}", [128, 2, 256]), sb(f"MKT{i}", [128, 2, 256]))) for i in range(3)])
                QSR = Ring([Slot(sb(f"QS{i}", [128, 16, 256], bf16)) for i in range(3)])
                KSR = Ring([Slot(sb(f"KS{i}", [128, 8, 256], bf16)) for i in range(3)])
                T = Ring([Slot(sb(f"T{i}", [128, 3, 2, 256], bf16)) for i in range(2)])
                tmp = Ring([Slot(sb(f"tmp{i}", [128, 256])) for i in range(2)])
                VV = Ring([Slot(sb(f"V{i}", [128, 2, 8, 32])) for i in range(3)])
                M = Ring([Slot(sb(f"M{i}", [128, 2, 16])) for i in range(2)])
                MT = Slot(sb("MT", [16, 3, 256], bf16))
                P = Ring([Slot(sb(f"P{i}", [128, 2, 4, 256])) for i in range(4)])
                JK = Ring([Slot(sb(f"JK{i}", [128, 256])) for i in range(2)])
                E = Ring([Slot(sb(f"E{i}", [128, 512])) for i in range(2)])
                NCR = Ring([Slot((sb(f"NC{i}", [128, 4, 256]), sb(f"SC{i}", [128, 4, 256]))) for i in range(2)])
                AT = Ring([Slot(sb(f"AT{i}", [128, 4, 256])) for i in range(2)])
                Y = Slot(sb("Y", [128, 2, 512]))
                st_ = sb("st", [128, 2, 6])
                mv = sb("mv", [128, 2, 2])
                rs = sb("rs", [128, 2])
                banksV = Ring([bankV, bankS])
                for s in QSR.slots:
                    s.ready = [dve.do(lambda e, s=s: e.memset(s.t[96:100, :, :], 1.0))]
                for s in KSR.slots:
                    a = dve.do(lambda e, s=s: e.memset(s.t[96:100, :, :], 1.0))
                    s.ready = [dve.do(lambda e, s=s: e.memset(s.t[96:97, :, :], 0.0), a)]
                for s in VV.slots:
                    s.ready = [dve.do(lambda e, s=s: e.memset(s.t[:, :, :, 16:32], 1.0))]

                def a1(it):
                    s = it.s
                    it.qs, it.m = QSR.next(), M.next()
                    it.st = it.qs
                    it.t_stack = []
                    steps = []

                    def load():
                        s.X, s.XT, s.C, s.mk, s.ks, s.vv = X.next(), XT.next(), CT.next(), MK.next(), KSR.next(), VV.next()
                        s.t_k, s.t_V = [], []
                        s.tX = sp.go(s.X.t[:, :, :], x2[it.b].rearrange("(n p) t -> p n t", p=128), s.X.free)
                        s.tC = sp.go(s.C.t[:, :, :], I["ctxT"][it.b].rearrange("(n p) t -> p n t", p=128), s.C.free)
                        s.tmk = []
                        for t, name in zip(s.mk.t, ("mask2", "mask2T")):
                            a = sp.go(t[:, :, :], I[name][it.b].rearrange("(n p) t -> p n t", p=128), s.mk.free)
                            s.tmk.append(dve.do(lambda e, t=t: e.tensor_scalar(t[:, :, :], t[:, :, :], 4.0, None, ALU.mult), a))

                    def xt(tt):
                        def f():
                            bank = bankA.next()
                            t = transposes([bank.t[:, q * 128:q * 128 + 128] for q in range(4)],
                                           [s.X.t[:, tt, q * 128:q * 128 + 128] for q in range(4)], bank, s.tX)
                            a = act.do(lambda e: e.activation(s.XT.t[:, :, tt * 128:tt * 128 + 128],
                                                              bank.t[:, :].rearrange("p (a b) -> p a b", a=4), ACT.Copy),
                                       t, s.XT.free)
                            bank.free = [a]
                            s.tXT = [a] if tt == 0 else s.tXT + [a]
                        return f

                    def q():
                        Tn = T.next()
                        act.wait(Tn.free)
                        dve.wait(Tn.free)
                        tks = []
                        for o in range(2):
                            og = 2 * it.h + o
                            bank, tm = bankA.next(), tmp.next()
                            t = project(bank, 0, 256, [(wq[:, c, og * 128:og * 128 + 128], s.XT.t[:, c, :]) for c in range(4)], s.tXT)
                            tv = Slot(tm.t[:, :])
                            tv.free = tm.free
                            tk, rd = split3(bank.t[:, 0:256], 128, t, [Tn.t[:, i, o, :] for i in range(3)], tv,
                                            bias=col["bq2"][:, og:og + 1])
                            tm.free = tv.free
                            bank.free = [rd, tk[0]]
                            tks += tk
                        s.XT.free = [t]
                        Q = it.qs.t
                        wr, ready = stack(None, it.qs.free, Tn.t[:, :, :, :], tks, scrq.next(),
                                          [(Q[16 * r:16 * r + 16, :, :], i) for r, i in enumerate([0, 0, 1, 0, 1, 2])], 2, 16, 256)
                        Tn.free = [wr]
                        it.t_stack += ready + s.t_k

                    def k():
                        Tn, bank, tm = T.next(), bankA.next(), tmp.next()
                        act.wait(Tn.free)
                        dve.wait(Tn.free)
                        t = project(bank, 0, 256, [(wk[:, c, :], s.C.t[:, c, :]) for c in range(4)], s.tC)
                        tv = Slot(tm.t[:, :])
                        tv.free = tm.free
                        tk, rd = split3(bank.t[:, 0:256], 128, t, [Tn.t[:, i, 0, :] for i in range(3)], tv, bias=col["bk2"][:, 0:1])
                        tm.free = tv.free
                        bank.free = [rd, tk[0]]
                        K = s.ks.t
                        wr, ready = stack(None, s.ks.free, Tn.t[:, :, 0:1, :], tk, scrk.next(),
                                          [(K[16 * r:16 * r + 16, :, :], i) for r, i in enumerate([0, 1, 0, 2, 1, 0])], 1, 16, 256)
                        Tn.free = [wr]
                        s.t_k = ready + s.ks.ready

                    def v():
                        bank = bankA.next()
                        for tt in range(2):
                            t = project(bank, 128 * tt, 128 * tt + 128,
                                        [(s.C.t[:, c, tt * 128:tt * 128 + 128], wv[:, c, :]) for c in range(4)], s.tC)
                            bank.free = []
                        br = rows["bv2"][:, :].rearrange("p (h d) -> p h d", d=16)
                        for tt in range(2):
                            s.t_V.append(dve.do(lambda e, tt=tt: e.tensor_tensor(
                                s.vv.t[:, tt, :, 0:16], bank.t[:, 128 * tt:128 * tt + 128].rearrange("p (h d) -> p h d", d=16),
                                br, ALU.add), t, s.vv.free, s.vv.ready))
                        bank.free = s.t_V[-2:]
                        s.C.free = [t]

                    if it.h == 0:
                        steps += [load, xt(0), xt(1), k, v]
                    steps.append(q)
                    return steps

                def a2(it):
                    s, Q = it.s, it.qs.t
                    tk = []

                    def smax(hp, qt):
                        def f():
                            bank = bankA.next()
                            pe.wait(bank.free, it.t_stack, it.qs.ready)
                            for i in range(2):
                                h = 2 * hp + i
                                g = lambda e, i=i, h=h: e.matmul(
                                    bank.t[:, 256 * i:256 * i + 256], Q[0:97, h, qt * 128:qt * 128 + 128],
                                    s.ks.t[0:97, 4 * it.h + h // 4, :], start=True, stop=True, skip_group_check=True)
                                if i:
                                    t = pe.do(g)
                                else:
                                    pe.quiet(g)
                            for i in range(2):
                                jk = JK.next()
                                d = dve.do(lambda e, i=i, jk=jk: e.tensor_tensor_reduce(
                                    out=jk.t[:, :], in0=bank.t[:, 256 * i:256 * i + 256], in1=s.mk.t[0][:, qt, :], scale=1.0,
                                    scalar=-3.0e38, op0=ALU.add, op1=ALU.max,
                                    accum_out=it.m.t[:, qt, 2 * hp + i:2 * hp + i + 1]), t, it.m.free, jk.free, s.tmk)
                                jk.free = [d]
                            bank.free = [d]
                            tk.append(d)
                        return f

                    def rows_():
                        it.t_rows = maxima_rows(it.m, [tk[-1]], 16, 2, MT, Slot2(tmp), it.qs.t)
                    return [smax(hp, qt) for qt in range(2) for hp in range(8)] + [rows_]

                def c(it):
                    s, Q = it.s, it.qs.t
                    pend, steps = [], []

                    def scores(kv):
                        def f():
                            Pk = P.next()
                            Pk.ready = []
                            for kt in range(2):
                                pair = pairC.next()
                                pe.wait(pair.free, it.t_rows, it.t_stack, it.qs.ready)
                                for i in range(2):
                                    g = lambda e, i=i, kt=kt, pair=pair: e.matmul(
                                        pair.t[:, i, :], s.ks.t[0:100, 4 * it.h + kv, kt * 128:kt * 128 + 128],
                                        Q[0:100, 4 * kv + 2 * i:4 * kv + 2 * i + 2, :], start=True, stop=True,
                                        skip_group_check=True)
                                    if i:
                                        t = pe.do(g)
                                    else:
                                        pe.quiet(g)
                                src = pair.t.rearrange("p a (b q) -> p (a b) q", b=2)
                                mk = s.mk.t[1][:, kt:kt + 1, :].broadcast_to([128, 4, 256])
                                d = dve.do(lambda e, kt=kt, src=src, mk=mk: e.tensor_tensor(Pk.t[:, kt, :, :], src, mk, ALU.add),
                                           t, Pk.free, s.tmk)
                                pair.free = [d]
                                Pk.ready.append(act.do(lambda e, kt=kt: e.activation(Pk.t[:, kt, :, :], Pk.t[:, kt, :, :], ACT.Exp,
                                                                                   scale=0.25), d))
                            pend.append(Pk)
                        return f

                    def values(g, kt):
                        def f():
                            two = pend[2 * g:2 * g + 2]
                            if kt == 0:
                                it.bv = banksV.next()
                                pe.wait(it.bv.free)
                            pe.wait(*[x.ready for x in two], s.t_V)
                            bv = it.bv
                            for j in range(4):
                                kv = 2 * g + j // 2
                                l = s.vv.t[:, kt, 4 * it.h + kv, :]
                                r = two[j // 2].t[:, kt, 2 * (j % 2):2 * (j % 2) + 2, :]
                                h = lambda e, j=j, l=l, r=r: e.matmul(
                                    bv.t[32 * j:32 * j + 32, :], l, r, start=(kt == 0), stop=(kt == 1),
                                    tile_position=(0, 32 * j), skip_group_check=True)
                                if j == 3:
                                    t = pe.do(h)
                                else:
                                    pe.quiet(h)
                            if kt == 1:
                                for x in two:
                                    x.free = [t]
                                if g == 0 and it.h == 0:
                                    s.nc = NCR.next()
                                    s.t_nc = []
                                E_ = E.next()
                                a = dve.do(lambda e: e.tensor_copy(E_.t[:, :], bv.t[:, :]), t, E_.free)
                                bv.free = [a]
                                E_.free = []
                                for j in range(4):
                                    for i in range(2):
                                        h = 16 * it.h + 4 * (2 * g + j // 2) + 2 * (j % 2) + i
                                        p0 = 16 * (h % 8)
                                        for k_, dst in enumerate(s.nc.t):
                                            E_.free.append(sp.go(dst[p0:p0 + 16, h // 8, :],
                                                                 E_.t[32 * j + 16 * k_:32 * j + 16 * k_ + 16, 256 * i:256 * i + 256],
                                                                 a, s.nc.free))
                                s.t_nc += E_.free
                                if g == 1:
                                    it.qs.free = [t]
                                    if it.h == 1:
                                        s.ks.free = [t]
                                        s.vv.free = [t]
                                        s.mk.free = [dve.last()]
                        return f
                    steps = [scores(0), scores(1), scores(2), values(0, 0), scores(3), values(0, 1), values(1, 0), values(1, 1)]
                    return steps

                def p(it):
                    if it.h == 0:
                        return []
                    s = it.s

                    def f0():
                        s.at = AT.next()
                        s.t_at = []
                        for i in range(4):
                            s.t_at.append(compact_normalize(it, None, s.nc.t[0], s.nc.t[1], s.at.t[:, i, :], 256, i, s.t_nc, s.at.free))
                        s.nc.free = [s.t_at[-1]]

                    def f1():
                        s.a = []
                        for tt in range(2):
                            bank = bankA.next()
                            t = project(bank, 0, 512, [(s.at.t[:, g, tt * 128:tt * 128 + 128], wo[:, g, :]) for g in range(4)], s.t_at)
                            a = dve.do(lambda e, tt=tt, bank=bank: e.tensor_tensor(Y.t[:, tt, :], bank.t[:, :], s.X.t[:, tt, :],
                                                                                 ALU.add), t, Y.free)
                            bank.free = [a]
                            a = dve.do(lambda e, tt=tt: e.tensor_tensor(Y.t[:, tt, :], Y.t[:, tt, :], rows["bo2"][:, :], ALU.add), a)
                            a = dve.do(lambda e, tt=tt: e.bn_stats(st_[:, tt, :], Y.t[:, tt, :]), a)
                            a = dve.do(lambda e, tt=tt: e.bn_aggr(mv[:, tt, :], st_[:, tt, :]), a)
                            s.a.append(a)
                        s.at.free = [t]
                        s.X.free = [a]

                    def f2():
                        t = rstd_of(rs[:, :], mv[:, :, 1], 1e-6, 1.0, s.a)
                        last = []
                        for tt in range(2):
                            a = dve.do(lambda e, tt=tt: e.tensor_scalar(Y.t[:, tt, :], Y.t[:, tt, :], mv[:, tt, 0:1],
                                                                        rs[:, tt:tt + 1], ALU.subtract, ALU.mult), t)
                            a = dve.do(lambda e, tt=tt: e.tensor_tensor(Y.t[:, tt, :], Y.t[:, tt, :], rows["g2"][:, :], ALU.mult), a)
                            last.append(dve.do(lambda e, tt=tt: e.tensor_tensor(Y.t[:, tt, :], Y.t[:, tt, :], rows["be2"][:, :],
                                                                                ALU.add), a))
                        Y.free = [sp.go(x3[it.b].rearrange("(n p) t -> p n t", p=128), Y.t[:, :, :], last)]
                    return [f0, f1, f2]

                class Slot2:
                    def __init__(self, ring):
                        self.s = ring.next()
                        self.t = self.s.t

                    @property
                    def free(self):
                        return self.s.free

                    @free.setter
                    def free(self, v):
                        self.s.free = v
                pipeline(items_of(), a1, a2, c, p)
                barrier()

        def layer3():
            with ExitStack() as lc:
                sb = sb_of(lc, "l3_")
                rows = load_rows(sb, ["gq3", "bq3"])
                wq, wk, wv, wo = (load_w(sb, n, 2, 256) for n in ("Wq3", "Wk3", "Wv3", "Wo3"))
                w1 = load_w(sb, "W13", 2, 512)
                w2 = load_w(sb, "W23", 4, 256)
                pos = sb("pos", [128, 4, 256])
                dve.wait(sp.go(pos[:, :, :], I["pos"].rearrange("(n p) c -> p n c", p=128)))
                X = Ring([Slot(sb(f"X{i}", [128, 2, 512])) for i in range(1)])
                QN = Ring([Slot(sb(f"QN{i}", [128, 4, 256])) for i in range(3)])
                KN = Ring([Slot(sb(f"KN{i}", [128, 4, 256])) for i in range(1)])
                QT = Ring([Slot((sb(f"QT{i}", [128, 2, 512]), sb(f"KT{i}", [128, 2, 512]))) for i in range(1)])
                ST = Ring([Slot((sb(f"QS{i}", [128, 8, 512], bf16), sb(f"KS{i}", [128, 8, 512], bf16))) for i in range(3)])
                T = Ring([Slot(sb(f"T{i}", [128, 3, 1, 512], bf16)) for i in range(1)])
                tmp = Ring([Slot(sb(f"tmp{i}", [128, 512])) for i in range(1)])
                VV = Ring([Slot(sb(f"V{i}", [128, 4, 8, 32])) for i in range(3)])
                M = Ring([Slot(sb(f"M{i}", [128, 4, 8])) for i in range(2)])
                MT = Slot(sb("MT", [8, 3, 512], bf16))
                P = Ring([Slot(sb(f"P{i}", [128, 2048])) for i in range(6)])
                E = Ring([Slot(sb(f"E{i}", [128, 512])) for i in range(1)])
                NCR = Ring([Slot((sb(f"NC{i}", [128, 2, 512]), sb(f"SC{i}", [128, 2, 512]))) for i in range(1)])
                HH = Slot(sb("HH", [128, 4, 256]))
                HTT = Slot(sb("HTT", [128, 2, 512]))
                RT = Slot(sb("RT", [128, 2, 512]))
                G = Slot(sb("G", [128, 4, 512]))
                st_ = sb("st", [128, 8, 6])
                mv = sb("mv", [128, 8, 2])
                rs = sb("rs", [128, 8])
                st2 = sb("st2", [128, 4, 6])
                mv2 = sb("mv2", [128, 4, 2])
                rs2 = sb("rs2", [128, 4])
                for s in ST.slots:
                    a = [dve.do(lambda e, t=t: e.memset(t[96:100, :, :], 1.0)) for t in s.t]
                    s.ready = [a[0], dve.do(lambda e, s=s: e.memset(s.t[1][96:97, :, :], 0.0), a)]
                for s in VV.slots:
                    s.ready = [dve.do(lambda e, s=s: e.memset(s.t[:, :, :, 16:32], 1.0))]

                def a1(it):
                    s = it.s
                    it.st, it.vv, it.m = ST.next(), VV.next(), M.next()
                    QS, KS = it.st.t
                    it.t_stack, it.t_V = [], []
                    steps = []

                    def load():
                        s.X, s.qn, s.kn, s.qt = X.next(), QN.next(), KN.next(), QT.next()
                        s.tX = sp.go(s.X.t[:, :, :], x3[it.b].rearrange("(n p) t -> p n t", p=128), s.X.free)
                        s.tC = sp.go(s.kn.t[:, :, :], I["ctxT"][it.b].rearrange("(n p) t -> p n t", p=128), s.kn.free)
                        s.ln = []

                    def kn():
                        a = dve.do(lambda e: e.tensor_tensor(s.kn.t[:, :, :], s.kn.t[:, :, :], pos[:, :, :], ALU.add), s.tC)
                        for tt in range(4):
                            b_ = dve.do(lambda e, tt=tt: e.bn_stats(st_[:, 4 + tt, :], s.kn.t[:, tt, :]), a)
                            s.ln.append(dve.do(lambda e, tt=tt: e.bn_aggr(mv[:, 4 + tt, :], st_[:, 4 + tt, :]), b_))

                    def qn(tp):
                        def f():
                            bank = bankA.next()
                            t = transposes([bank.t[:, (2 * k + cc) * 128:(2 * k + cc) * 128 + 128] for k in range(2) for cc in range(2)],
                                           [s.X.t[:, cc, (2 * tp + k) * 128:(2 * tp + k) * 128 + 128] for k in range(2) for cc in range(2)],
                                           bank, s.tX)
                            d = dve.do(lambda e: e.tensor_tensor(s.qn.t[:, 2 * tp:2 * tp + 2, :],
                                                                 bank.t[:, :].rearrange("p (a b) -> p a b", a=2),
                                                                 pos[:, 2 * tp:2 * tp + 2, :], ALU.add), t, s.qn.free)
                            bank.free = [d]
                            s.X.free = [t]
                            for k in range(2):
                                tt = 2 * tp + k
                                b_ = dve.do(lambda e, tt=tt: e.bn_stats(st_[:, tt, :], s.qn.t[:, tt, :]), d)
                                s.ln.append(dve.do(lambda e, tt=tt: e.bn_aggr(mv[:, tt, :], st_[:, tt, :]), b_))
                        return f

                    def norm():
                        t = rstd_of(rs[:, :], mv[:, :, 1], 1e-5, 1.0, s.ln)
                        s.tq, s.tk = [], []
                        for tt in range(4):
                            q = s.qn.t[:, tt, :]
                            a = dve.do(lambda e, tt=tt, q=q: e.tensor_scalar(q, q, mv[:, tt, 0:1], rs[:, tt:tt + 1],
                                                                             ALU.subtract, ALU.mult), t)
                            a = dve.do(lambda e, q=q: e.tensor_tensor(q, q, rows["gq3"][:, :], ALU.mult), a)
                            s.tq.append(dve.do(lambda e, q=q: e.tensor_tensor(q, q, rows["bq3"][:, :], ALU.add), a))
                            k = s.kn.t[:, tt, :]
                            s.tk.append(dve.do(lambda e, tt=tt, k=k: e.tensor_scalar(k, k, mv[:, 4 + tt, 0:1], rs[:, 4 + tt:5 + tt],
                                                                                     ALU.subtract, ALU.mult), t))

                    def tr(cc):
                        def f():
                            QTt, KTt = s.qt.t
                            if cc == 0:
                                s.t_qt, s.t_kt = [], []
                            bank = bankA.next()
                            t = transposes([bank.t[:, tt * 128:tt * 128 + 128] for tt in range(4)],
                                           [s.qn.t[:, tt, cc * 128:cc * 128 + 128] for tt in range(4)], bank, s.tq)
                            a = act.do(lambda e, bank=bank: e.activation(QTt[:, cc, :], bank.t[:, :], ACT.Copy), t, s.qt.free)
                            bank.free = [a]
                            s.t_qt.append(a)
                            bank = bankA.next()
                            t = transposes([bank.t[:, tt * 128:tt * 128 + 128] for tt in range(4)],
                                           [s.kn.t[:, tt, cc * 128:cc * 128 + 128] for tt in range(4)], bank, s.tk)
                            a = act.do(lambda e, bank=bank: e.activation(KTt[:, cc, :], bank.t[:, :], ACT.Identity,
                                                                         bias=col["bkv3"][:, cc:cc + 1],
                                                                         scale=col["gkv3"][:, cc:cc + 1]), t, s.qt.free)
                            bank.free = [a]
                            s.t_kt.append(a)
                            s.kn.free = [t]
                        return f

                    def qk(w, k_, dst, scr, order):
                        def f():
                            src, ts = s.qt.t[k_], (s.t_kt if k_ else s.t_qt)
                            bank, Tn, tm = bankA.next(), T.next(), tmp.next()
                            t = project(bank, 0, 512, [(w[:, c, it.h * 128:it.h * 128 + 128], src[:, c, :]) for c in range(2)], ts)
                            act.wait(Tn.free)
                            dve.wait(Tn.free)
                            tv = Slot(tm.t[:, :])
                            tv.free = tm.free
                            tk, rd = split3(bank.t[:, :], 128, t, [Tn.t[:, i, 0, :] for i in range(3)], tv)
                            tm.free = tv.free
                            bank.free = [rd, tk[0]]
                            wr, ready = stack(dst, it.st.free, Tn.t[:, :, :, :], tk, scr.next(),
                                              [(dst[16 * r:16 * r + 16, :, :], i) for r, i in enumerate(order)], 1, 16, 512)
                            Tn.free = [wr]
                            it.t_stack += ready
                        return f

                    def vproj(tp):
                        def f():
                            bank = bankA.next()
                            for k in range(2):
                                tt = 2 * tp + k
                                t = project(bank, 128 * k, 128 * k + 128,
                                            [(s.qt.t[1][:, c, tt * 128:tt * 128 + 128], wv[:, c, it.h * 128:it.h * 128 + 128])
                                             for c in range(2)], s.t_kt)
                                bank.free = []
                            d = dve.do(lambda e: e.tensor_copy(
                                it.vv.t[:, 2 * tp:2 * tp + 2, :, 0:16],
                                bank.t[:, 0:256].rearrange("p (a h d) -> p a h d", a=2, d=16)), t, it.vv.free, it.vv.ready)
                            bank.free = [d]
                            it.t_V.append(d)
                            s.qt.free = [t]
                        return f

                    if it.h == 0:
                        steps += [load, kn, qn(0), qn(1), norm, tr(0), tr(1)]
                    steps.append(qk(wq, 0, QS, scrq, [0, 0, 1, 0, 1, 2]))
                    steps.append(qk(wk, 1, KS, scrk, [0, 1, 0, 2, 1, 0]))
                    steps += [vproj(0), vproj(1)]
                    it.V = lambda kt, h: it.vv.t[:, kt, h, :]
                    return steps

                def a2(it):
                    QS, KS = it.st.t
                    tk = []

                    def smax(h, qt):
                        def f():
                            bank = bankA.next()
                            t = pe.do(lambda e: e.matmul(bank.t[:, :], QS[0:97, h, qt * 128:qt * 128 + 128], KS[0:97, h, :],
                                                         start=True, stop=True), bank.free, it.t_stack, it.st.ready)
                            d = dve.do(lambda e: e.tensor_reduce(it.m.t[:, qt, h:h + 1], bank.t[:, :], AX.X, ALU.max), t, it.m.free)
                            bank.free = [d]
                            tk.append(d)
                        return f

                    def rows_():
                        it.t_rows = maxima_rows(it.m, [tk[-1]], 8, 4, MT, tmp.next(), QS)
                    return [smax(h, qt) for qt in range(4) for h in range(8)] + [rows_]

                def c(it):
                    QS, KS = it.st.t

                    def group_done(g, t):
                        s = it.s
                        if g == 0 and it.h == 0:
                            s.nc = NCR.next()
                            s.t_nc = []
                        E_ = E.next()
                        a = dve.do(lambda e: e.tensor_copy(E_.t[:, :], bankV.t[:, :]), t, E_.free)
                        bankV.free = [a]
                        E_.free = []
                        for j in range(4):
                            p0 = 16 * (4 * g + j)
                            for k_, dst in enumerate(s.nc.t):
                                E_.free.append(sp.go(dst[p0:p0 + 16, it.h, :], E_.t[32 * j + 16 * k_:32 * j + 16 * k_ + 16, :],
                                                     a, s.nc.free))
                        s.t_nc += E_.free
                        if g == 1:
                            it.st.free = [t]
                            it.vv.free = [t]
                    it.group_done = group_done
                    return attend3(it)

                def attend3(it):
                    QS, KS = it.st.t
                    return attend(it, list(range(8)), 4, 512, 0.25, P,
                                  lambda h, kt: [(KS[0:100, h, kt * 128:kt * 128 + 128], QS[0:100, h, :])], False, 2)

                def p(it):
                    if it.h == 0:
                        return []
                    s = it.s

                    def f0():
                        s.t_at = [compact_normalize(it, None, s.nc.t[0], s.nc.t[1], s.nc.t[0][:, i, :], 512, i, s.t_nc, None)
                                  for i in range(2)]

                    def f1():
                        s.a = []
                        for tt in range(4):
                            bank = bankA.next()
                            t = project(bank, 0, 256, [(s.nc.t[0][:, c, tt * 128:tt * 128 + 128], wo[:, c, :]) for c in range(2)],
                                        s.t_at)
                            q = s.qn.t[:, tt, :]
                            a = dve.do(lambda e, q=q, bank=bank: e.tensor_tensor(q, bank.t[:, 0:256], q, ALU.add), t)
                            bank.free = [a]
                            a = dve.do(lambda e, tt=tt, q=q: e.bn_stats(st2[:, tt, :], q), a)
                            s.a.append(dve.do(lambda e, tt=tt: e.bn_aggr(mv2[:, tt, :], st2[:, tt, :]), a))
                        s.nc.free = [t]

                    def f2():
                        t = rstd_of(rs2[:, :], mv2[:, :, 1], 1e-5, 1.0, s.a)
                        s.th = []
                        for tt in range(4):
                            s.th.append(dve.do(lambda e, tt=tt: e.tensor_scalar(HH.t[:, tt, :], s.qn.t[:, tt, :], mv2[:, tt, 0:1],
                                                                                rs2[:, tt:tt + 1], ALU.subtract, ALU.mult),
                                               t, HH.free))

                    def f3(cc):
                        def f():
                            if cc == 0:
                                s.t_ht, s.t_rt = [], []
                            bank = bankA.next()
                            t = transposes([bank.t[:, tt * 128:tt * 128 + 128] for tt in range(4)],
                                           [HH.t[:, tt, cc * 128:cc * 128 + 128] for tt in range(4)], bank, s.th)
                            a = act.do(lambda e, bank=bank: e.activation(HTT.t[:, cc, :], bank.t[:, :], ACT.Identity,
                                                                         bias=col["bf3"][:, cc:cc + 1],
                                                                         scale=col["gf3"][:, cc:cc + 1]), t, HTT.free)
                            bank.free = [a]
                            HH.free = [t]
                            s.t_ht.append(a)
                            bank = bankA.next()
                            t = transposes([bank.t[:, tt * 128:tt * 128 + 128] for tt in range(4)],
                                           [s.qn.t[:, tt, cc * 128:cc * 128 + 128] for tt in range(4)], bank)
                            a = act.do(lambda e, bank=bank: e.activation(RT.t[:, cc, :], bank.t[:, :], ACT.Copy), t, RT.free)
                            bank.free = [a]
                            s.t_rt.append(a)
                            s.qn.free = [t]
                        return f

                    def f4(o):
                        def f():
                            if o == 0:
                                s.tg = []
                            bank = bankA.next()
                            t = project(bank, 0, 512, [(w1[:, c, o * 128:o * 128 + 128], HTT.t[:, c, :]) for c in range(2)], s.t_ht)
                            s.tg.append(act.do(lambda e: e.activation(G.t[:, o, :], bank.t[:, :], ACT.Gelu,
                                                                      bias=col["b13"][:, o:o + 1]), t, G.free))
                            bank.free = [s.tg[-1]]
                            if o == 3:
                                HTT.free = [t]
                        return f

                    def f5():
                        last = []
                        for cc in range(2):
                            bank = bankA.next()
                            t = project(bank, 0, 512, [(w2[:, o, cc * 128:cc * 128 + 128], G.t[:, o, :]) for o in range(4)], s.tg)
                            d = dve.do(lambda e, cc=cc, bank=bank: e.scalar_tensor_tensor(
                                out=RT.t[:, cc, :], in0=bank.t[:, :], scalar=col["b23"][:, cc:cc + 1], in1=RT.t[:, cc, :],
                                op0=ALU.add, op1=ALU.add), t, s.t_rt)
                            bank.free = [d]
                            last.append(d)
                        G.free = [t]
                        RT.free = [sp.go(out[it.b].rearrange("(n p) t -> p n t", p=128), RT.t[:, :, :], last)]
                    return [f0, f1, f2, f3(0), f3(1), f4(0), f4(1), f4(2), f4(3), f5]
                pipeline(items_of(), a1, a2, c, p)
                barrier()

        layer0()
        layer1a()
        layer1b()
        layer2()
        layer3()

        block = ctx.enter_context(nc.Block())

        @block.sync
        def _(e):
            sp.run(e)

        @block.gpsimd
        def _(e):
            pool.run(e)

        @block.scalar
        def _(e):
            act.run(e)

        @block.vector
        def _(e):
            dve.run(e)

        @block.tensor
        def _(e):
            pe.run(e)


def lay_out(i):
    a = {k: np.asarray(v) for k, v in i.items()}
    C = np.ascontiguousarray
    colv = lambda v: C(v.reshape(-1, 128).T)
    kvw = a["L1_xattn_kv_w"].reshape(512, 512, 2)
    kvb = a["L1_xattn_kv_b"].reshape(512, 2)
    cols = {"bq0": a["L0_xattn_bq"], "bk0": a["L0_xattn_bk"], "qb1": a["L1_xattn_q_b"], "kb1": kvb[:, 0],
            "pn1": a["L1_xattn_postnorm_w"], "mb1": a["L1_xattn_mlp_b1"], "bq2": a["L2_xattn_bq"], "bk2": a["L2_xattn_bk"],
            "gkv3": a["L3_xattn_ln_kv_g"], "bkv3": a["L3_xattn_ln_kv_b"], "gf3": a["L3_xattn_ffn_ln_g"],
            "bf3": a["L3_xattn_ffn_ln_b"], "b13": a["L3_xattn_b1"], "b23": a["L3_xattn_b2"]}
    rows = {"bv0": a["L0_xattn_bv"], "vb1": kvb[:, 1], "ob1": a["L1_xattn_out_b"], "mb2": a["L1_xattn_mlp_b2"],
            "bv2": a["L2_xattn_bv"], "bo2": a["L2_xattn_bo"], "g2": a["L2_xattn_gamma"], "be2": a["L2_xattn_beta"],
            "gq3": a["L3_xattn_ln_q_g"], "bq3": a["L3_xattn_ln_q_b"]}
    t = np.arange(512, dtype=np.float32)[:, None]
    div = np.exp(np.arange(0, 256, 2, dtype=np.float32) * np.float32(-np.log(10000.0) / 256))
    ang = (t * div).astype(np.float32)
    pos = np.zeros((512, 256), np.float32)
    pos[:, 0::2] = np.sin(ang)
    pos[:, 1::2] = np.cos(ang)
    mask0 = a["mask_Bx1x2048_bf1"]
    return {
        "x": a["x"], "ctx": a["ctx_2048"], "ctxT": C(a["ctx_2048"].transpose(0, 2, 1)),
        "mask0": C(mask0).view(np.uint8), "mask1": a["mask_BxS2_ik0"],
        "mask2": C(a["mask_Bx1xSxS2_ff0"][:, 0]), "mask2T": C(a["mask_Bx1xSxS2_ff0"][:, 0].transpose(0, 2, 1)),
        "cols": C(np.concatenate([colv(cols[n]) for n, _ in COLS], axis=1)),
        "rows": C(np.concatenate([rows[n] for n, _ in ROWS])[None, :]),
        "pos": pos,
        "WqT0": C(a["L0_xattn_Wq"].T), "WkT0": C(a["L0_xattn_Wk"].T), "WvT0": C(a["L0_xattn_Wv"].T),
        "q_w1": a["L1_xattn_q_w"], "k_w1": C(kvw[:, :, 0]), "v_w1": C(kvw[:, :, 1]), "out_w1": a["L1_xattn_out_w"],
        "mlp_w1": a["L1_xattn_mlp_w1"], "mlp_w2": a["L1_xattn_mlp_w2"],
        "Wq2": a["L2_xattn_Wq"], "Wk2": a["L2_xattn_Wk"], "Wv2": a["L2_xattn_Wv"], "Wo2": a["L2_xattn_Wo"],
        "Wq3": a["L3_xattn_Wq"], "Wk3": a["L3_xattn_Wk"], "Wv3": a["L3_xattn_Wv"], "Wo3": a["L3_xattn_Wo"],
        "W13": a["L3_xattn_W1"], "W23": a["L3_xattn_W2"],
    }


def kernel(**inputs):
    import concourse.bacc as _bacc
    from concourse.bass_utils import run_bass_kernel_spmd as _run

    nc = _bacc.Bacc("TRN2", target_bir_lowering=False, num_devices=1)
    arrays, aps = {}, {}
    for name, v in lay_out(inputs).items():
        arrays[f"in_{name}"] = v
        aps[name] = nc.dram_tensor(f"in_{name}", v.shape, mybir.dt.from_np(v.dtype), kind="ExternalInput").ap()
    out = nc.dram_tensor("out_0", [8, 256, 512], mybir.dt.float32, kind="ExternalOutput").ap()
    build_program(nc, aps, out)
    r = _run(nc, [arrays], core_ids=[0])
    return r.results[0]["out_0"]
```

```python
import numpy as np
import concourse.bass as bass
from concourse import mybir
from contextlib import ExitStack

COLS = [("bq0", 2), ("bk0", 2), ("qb1", 4), ("kb1", 4), ("pn1", 4), ("mb1", 16), ("bq2", 4), ("bk2", 1),
        ("gkv3", 2), ("bkv3", 2), ("gf3", 2), ("bf3", 2), ("b13", 4), ("b23", 2)]
ROWS = [("bv0", 256), ("vb1", 512), ("ob1", 512), ("mb2", 512), ("bv2", 128), ("bo2", 512), ("g2", 512), ("be2", 512),
        ("gq3", 256), ("bq3", 256)]
B, HALVES = 8, 2
NEG = 1e30


class Engine:

    def __init__(self, sem):
        self.ops, self.sem, self.n, self.seen = [], sem, 0, {}

    def wait(self, *tokens):
        for t in tokens:
            if t is None:
                continue
            if isinstance(t, list):
                self.wait(*t)
                continue
            sem, value = t
            if self.seen.get(id(sem), 0) < value:
                self.seen[id(sem)] = value
                self.ops.append(lambda e, s=sem, v=value: e.wait_ge(s, v))

    def do(self, f, *waits):
        self.wait(*waits)
        self.n += 1
        self.ops.append(lambda e: f(e).then_inc(self.sem, 1))
        return (self.sem, self.n)

    def quiet(self, f, *waits):
        self.wait(*waits)
        self.ops.append(f)

    def last(self):
        return (self.sem, self.n) if self.n else None

    def run(self, e):
        for f in self.ops:
            f(e)


class Dma(Engine):

    def __init__(self, sems, engine=None):
        super().__init__(None)
        self.sems, self.count, self.k = sems, [0] * len(sems), 0
        if engine:
            self.ops, self.seen = engine.ops, engine.seen

    def go(self, out, in_, *waits):
        i = self.k % len(self.sems)
        self.k += 1
        s = self.sems[i]
        if self.count[i]:
            self.wait((s, self.count[i]))
        self.wait(*waits)
        self.count[i] += 16
        self.ops.append(lambda e: e.dma_start(out, in_).then_inc(s, 16))
        return (s, self.count[i])

    def all(self):
        return [(s, c) for s, c in zip(self.sems, self.count) if c]


class Slot:

    def __init__(self, t):
        self.t, self.ready, self._free, self.taken = t, [], [], False

    @property
    def free(self):
        return self._free

    @free.setter
    def free(self, tokens):
        self._free, self.taken = tokens, False


class Ring:
    def __init__(self, slots):
        self.slots, self.k = slots, 0

    def next(self):
        s = self.slots[self.k % len(self.slots)]
        self.k += 1
        assert not s.taken, "the slot's last reader isn't queued yet"
        s.taken = True
        return s


def merge(*lists):
    placed = []
    for n, (steps, start, end) in enumerate(lists):
        for i, f in enumerate(steps):
            f, delay = f if isinstance(f, tuple) else (f, 0.0)
            placed.append((start + (end - start) * (i + 0.5) / len(steps) + delay, n, i, f))
    for _, _, _, f in sorted(placed, key=lambda x: x[:3]):
        f()


def build_program(nc, I, out, batches=B):
    fp32, bf16, u8, i32 = mybir.dt.float32, mybir.dt.bfloat16, mybir.dt.uint8, mybir.dt.int32
    ALU, ACT, AX = mybir.AluOpType, mybir.ActivationFunctionType, mybir.AxisListType
    ctx = ExitStack()
    with ctx:
        sem = lambda n: ctx.enter_context(nc.semaphore(n))
        pe, act, dve, pool = Engine(sem("s_pe")), Engine(sem("s_act")), Engine(sem("s_dve")), Engine(sem("s_pool"))
        sp = Dma([sem(f"s_dma{i}") for i in range(48)])
        pq = Dma([sem(f"s_pdma{i}") for i in range(16)], pool)
        PS = ctx.enter_context(nc.psum_tensor("PS", [128, 8, 512], fp32))
        bankA = Ring([Slot(PS[:, i, :]) for i in (0, 1, 2)])
        bankC = Ring([Slot(PS[:, i, :]) for i in (3, 4, 5)])
        bankV, bankS = Slot(PS[:, 6, :]), Slot(PS[:, 7, :])
        bankVV = Ring([bankV, bankS])

        x1 = nc.dram_tensor("x1_scratch", [B, 256, 512], fp32, kind="Internal").ap()
        y1 = nc.dram_tensor("y1_scratch", [B, 256, 512], fp32, kind="Internal").ap()
        x2 = nc.dram_tensor("x2_scratch", [B, 256, 512], fp32, kind="Internal").ap()
        x3 = nc.dram_tensor("x3_scratch", [B, 256, 512], fp32, kind="Internal").ap()
        NSCR = 4
        scrq = Ring([Slot(nc.dram_tensor(f"q_scratch{i}", [128 * 3 * 512], bf16, kind="Internal").ap()) for i in range(NSCR)])
        scrk = Ring([Slot(nc.dram_tensor(f"k_scratch{i}", [128 * 3 * 1024], bf16, kind="Internal").ap()) for i in range(NSCR)])

        sb_of = lambda c, layer="": (lambda n, shape, dt=fp32: c.enter_context(nc.sbuf_tensor(layer + n, shape, dt)))
        sbg = sb_of(ctx)
        cols = sbg("cols", [128, sum(n for _, n in COLS)])
        col, at = {}, 0
        for n, w in COLS:
            col[n] = cols[:, at:at + w]
            at += w
        row_at, at = {}, 0
        for n, w in ROWS:
            row_at[n] = (at, w)
            at += w
        ident = sbg("ident", [128, 128])
        identb = sbg("identb", [128, 128], bf16)
        onerow = sbg("onerow", [4, 512], bf16)
        zrow = sbg("zrow", [1, 512], bf16)
        ones = sbg("ones", [128, 32])
        t_cols = sp.go(cols[:, :], I["cols"])
        t_id0 = pool.do(lambda e: e.memset(ident[:, :], 0.0))
        t_id = pool.do(lambda e: e.affine_select(out=ident[:, :], in_=ident[:, :], compare_op=ALU.not_equal, fill=1.0,
                                                 base=0, pattern=[[-1, 128]], channel_multiplier=1), t_id0)
        t_ones = pool.do(lambda e: e.memset(ones[:, :], 1.0))
        t_idb = pool.do(lambda e: e.tensor_copy(identb[:, :], ident[:, :]), t_id)
        t_1r = pool.do(lambda e: e.memset(onerow[:, :], 1.0))
        t_0r = pool.do(lambda e: e.memset(zrow[:, :], 0.0))
        for e in (act, dve):
            e.wait(t_cols)
        pe.wait(t_id, t_ones, t_idb)

        def set_rows(t, nh, w, key):
            r = [sp.go(t[96:100, :, :], onerow[:, None, 0:w].broadcast_to([4, nh, w]), t_1r)]
            if key:
                r = [sp.go(t[96:97, :, :], zrow[:, None, 0:w].broadcast_to([1, nh, w]), t_0r, r)]
            return r

        def barrier():
            tokens = [x.last() for x in (pe, act, dve, pool)] + sp.all() + pq.all()
            for x in (pe, act, dve, pool, sp):
                x.wait(*tokens)

        def load_rows(sb, names):
            r = {}
            for n in names:
                a, w = row_at[n]
                t = sb("row_" + n, [128, w])
                r[n] = t
                dve.wait(sp.go(t[:, :], I["rows"][0:1, a:a + w].broadcast_to([128, w])))
            return r

        def load_w(sb, name, k, n):
            t = sb("w_" + name, [128, k, n])
            pe.wait(sp.go(t[:, :, :], I[name].rearrange("(k p) n -> p k n", p=128)))
            return t

        def project(bank, lo, hi, pairs, *waits):
            pe.wait(bank.free, *waits)
            for i, (l, r) in enumerate(pairs[:-1]):
                pe.quiet(lambda e, l=l, r=r, i=i: e.matmul(bank.t[:, lo:hi], l, r, start=(i == 0), stop=False,
                                                           skip_group_check=True))
            l, r = pairs[-1]
            return pe.do(lambda e: e.matmul(bank.t[:, lo:hi], l, r, start=(len(pairs) == 1), stop=True,
                                            skip_group_check=True))

        def evacuate(src, t_src, T0, F, bias=None):
            b = 0.0 if bias is None else bias
            a0 = act.do(lambda e: e.activation(T0, src, ACT.Identity, bias=b), t_src)
            return a0, act.do(lambda e: e.activation(F.t, src, ACT.Identity, bias=b), F.free)

        def split3(T, F, t_F):
            f = F.t
            d0 = dve.do(lambda e: e.tensor_tensor(f, f, T[0], ALU.subtract), t_F)
            d1 = dve.do(lambda e: e.tensor_copy(T[1], f), d0)
            d2 = pool.do(lambda e: e.tensor_tensor(T[2], f, T[1], ALU.subtract), d1)
            F.free = [d2]
            return [t_F, d1, d2]

        def stack(dst, free, T, t_T, scr, parts, nt, d, cols_):
            view = scr.t[0:128 * 3 * nt * cols_].rearrange("(i n p q) -> i n p q", i=3, n=nt, p=128)
            w = sp.go(view.rearrange("i n p q -> p i n q"), T, t_T, scr.free)
            ready = []
            for rows, i in parts:
                ready.append(sp.go(rows, view[i].rearrange("n (h d) q -> d (n h) q", d=d), w, free))
            scr.free = ready
            return w, ready

        def stack_rows(free, T, t_T, scr, parts):
            view = scr.t[0:128 * 3 * 512].rearrange("(i d h q) -> i d h q", i=3, d=16, h=8)
            w = [sp.go(view[i].rearrange("d h q -> h d q"), T[:, i, :], t_T[i], scr.free) for i in range(3)]
            ready = []
            for rows, i, n, same in parts:
                src = view[i:i + 1].broadcast_to([n, 16, 8, 512]) if same else view[i:i + n].rearrange("i d h q -> (i d) h q")
                ready.append(sp.go(rows, src, w, free))
            scr.free = ready
            return w, ready

        def transposes(dsts, srcs, bank, *waits):
            pe.wait(bank.free, *waits)
            for d, s in list(zip(dsts, srcs))[:-1]:
                pe.quiet(lambda e, d=d, s=s: e.transpose(d, s, ident[0:s.shape[0], 0:s.shape[0]]))
            return pe.do(lambda e: e.transpose(dsts[-1], srcs[-1], ident[0:srcs[-1].shape[0], 0:srcs[-1].shape[0]]))

        def maxima_rows(M, t_M, nh, nqt, SP, MT, Q):
            w = nqt * 128
            m, (s3, r) = M.t, SP.t
            m3 = s3[:, :, :].rearrange("p q (i h) -> p i q h", i=3)
            a = dve.do(lambda e: e.tensor_scalar(m3[:, 0], m[:, :, :], -1.0, None, ALU.mult), t_M, SP.free)
            b_ = dve.do(lambda e: e.scalar_tensor_tensor(out=r[:, :, :], in0=m[:, :, :], scalar=-1.0, in1=m3[:, 0], op0=ALU.mult,
                                                         op1=ALU.subtract), a)
            c_ = dve.do(lambda e: e.tensor_copy(m3[:, 1], r[:, :, :]), b_)
            d_ = dve.do(lambda e: e.tensor_tensor(m3[:, 2], r[:, :, :], m3[:, 1], ALU.subtract), c_)
            M.free = [b_]
            bank = bankA.next()
            pe.wait(bank.free, d_)
            for q in range(nqt):
                f = lambda e, q=q: e.matmul(bank.t[0:3 * nh, q * 128:(q + 1) * 128], s3[:, q, :], identb[:, :], start=True,
                                            stop=True, skip_group_check=True)
                if q == nqt - 1:
                    t = pe.do(f)
                else:
                    pe.quiet(f)
            SP.free = [t]
            v = act.do(lambda e: e.activation(MT.t[0:3 * nh, 0:w], bank.t[0:3 * nh, 0:w], ACT.Copy), t, MT.free)
            bank.free = [v]
            rr = [sp.go(Q[97 + i:98 + i, :, :], MT.t[nh * i:nh * i + nh, 0:w], v) for i in range(3)]
            MT.free = rr
            return rr

        class Sums:

            def __init__(self, sb, name, rows_, w, n):
                self.dram = Ring([Slot((nc.dram_tensor(f"{name}_sums{i}", [rows_, w], fp32, kind="Internal").ap(),
                                        nc.dram_tensor(f"{name}_recs{i}", [rows_, w], fp32, kind="Internal").ap()))
                                  for i in range(n)])
                self.small = Ring([Slot(sb(f"{name}r{i}", [128, rows_ * w // 128])) for i in range(2)])
                self.w = w

            def take(self):
                d = self.dram.next()
                d.tokens = []
                return d

            def put(self, d, at, src, t):
                x = sp.go(d.t[0][at[0]:at[1], at[2]:at[3]], src, t, d.free)
                d.tokens.append(x)
                return x

            def invert(self, d):
                f = lambda x: x.rearrange("a b -> (a b)").rearrange("(p f) -> p f", p=128)
                s = self.small.next()
                a = sp.go(s.t[:, :], f(d.t[0]), d.tokens, s.free)
                b_ = dve.do(lambda e: e.reciprocal(s.t[:, :], s.t[:, :]), a)
                c_ = sp.go(f(d.t[1]), s.t[:, :], b_)
                s.free = [c_]
                d.tokens = [c_]

            def spread(self, d, dst, lo, hi, rep, free):
                x = sp.go(dst, d.t[1][lo:hi, None, :].broadcast_to([hi - lo, rep, self.w]), d.tokens, free)
                return x

        magic = sbg("magic", [128, 3, 8])

        def rstd_of(ms, var, eps, scale, *waits):
            n = ms.shape[1]
            x, y, z = (magic[:, i, 0:n] for i in range(3))
            t = dve.do(lambda e: e.tensor_scalar(x, var, scale, eps, ALU.mult, ALU.add), *waits, dve.last())
            t = dve.do(lambda e: e.tensor_scalar(z.bitcast(i32), x.bitcast(i32), 1, None, ALU.arith_shift_right), t)
            t = dve.do(lambda e: e.tensor_scalar(y.bitcast(i32), z.bitcast(i32), -1.0, float(0x5f3759df), ALU.mult, ALU.add), t)
            for k in range(4):
                t = dve.do(lambda e: e.tensor_tensor(z, y, y, ALU.mult), t)
                t = dve.do(lambda e: e.tensor_tensor(z, z, x, ALU.mult), t)
                t = dve.do(lambda e: e.tensor_scalar(z, z, -0.5, 1.5, ALU.mult, ALU.add), t)
                t = dve.do(lambda e, o=ms if k == 3 else y: e.tensor_tensor(o, y, z, ALU.mult), t)
            return t

        class Item:
            pass

        def nop():
            pass

        def pipeline(items, a1, a2, c, p, spans=((0.0, 0.9), (0.0, 0.75), (0.0, 1.0), (0.0, 1.0))):
            n = len(items)
            stages = (a1, a2, c, p)
            for i in range(-2, n + 1):
                lists = []
                for s, (f, span) in enumerate(zip(stages, spans)):
                    k = i + 2 - s
                    if 0 <= k < n:
                        steps = f(items[k])
                        if steps:
                            lists.append((steps, *span))
                merge(*lists)

        def items_of():
            out_ = []
            for b in range(batches):
                shared = Item()
                for h in range(HALVES):
                    it = Item()
                    it.b, it.h, it.s = b, h, shared
                    out_.append(it)
            return out_

        def attend(it, heads, nkt, w, scale, Pring, lhs, vones, spread=4):
            steps = []
            pend = []

            def scores(h):
                def f():
                    P = Pring.next()
                    P.ready = []
                    per = 512 // w
                    for c0 in range(0, nkt, per):
                        bank = bankC.next()
                        pe.wait(bank.free, it.t_rows, it.st.ready, it.t_stack)
                        for i in range(per):
                            mm = lhs(h, c0 + i)
                            for m, (l, r) in enumerate(mm):
                                o = bank.t[:, i * w:(i + 1) * w]
                                g = lambda e, o=o, l=l, r=r, m=m, k=len(mm): e.matmul(
                                    o, l, r, start=(m == 0), stop=(m == k - 1), skip_group_check=True)
                                if i == per - 1 and m == len(mm) - 1:
                                    t = pe.do(g)
                                else:
                                    pe.quiet(g)
                        po = P.t[:, c0 * w:(c0 + per) * w]
                        a = act.do(lambda e, po=po, bank=bank: e.activation(po, bank.t, ACT.Exp, scale=scale), t, P.free)
                        bank.free = [a]
                        P.ready.append(a)
                    pend.append((h, P))
                return f

            def values(g, kt):
                def f():
                    four = pend[4 * g:4 * g + 4]
                    if kt == 0:
                        it.bv = bankV if vones else bankVV.next()
                        pe.wait(it.bv.free)
                    bv = it.bv
                    pe.wait(*[P.ready for _, P in four], it.t_V)
                    if vones:
                        pe.wait(bankS.free if kt == 0 else None)
                    for j, (h, P) in enumerate(four):
                        l = it.V(kt, h)
                        o = bv.t[32 * j:32 * j + l.shape[1], 0:w]
                        r = P.t[:, kt * w:(kt + 1) * w]
                        pe.quiet(lambda e, o=o, r=r, l=l, j=j: e.matmul(
                            o, l, r, start=(kt == 0), stop=(kt == nkt - 1), tile_position=(0, 32 * j), skip_group_check=True))
                    if vones:
                        for j, (h, P) in enumerate(four):
                            o = bankS.t[32 * j:32 * j + 32, 0:w]
                            r = P.t[:, kt * w:(kt + 1) * w]
                            pe.quiet(lambda e, o=o, r=r, j=j: e.matmul(
                                o, ones[:, :], r, start=(kt == 0), stop=(kt == nkt - 1), tile_position=(0, 32 * j),
                                skip_group_check=True))
                    f_last = pe.ops.pop()
                    t = pe.do(f_last)
                    if kt == nkt - 1:
                        for _, P in four:
                            P.free = [t]
                        it.group_done(g, t)
                return f

            ng = len(heads) // 4
            for i, h in enumerate(heads):
                steps.append(scores(h))
                if i >= 4 and (i - 4) % 4 < spread:
                    for kt in range((i - 4) % 4 * nkt // spread, ((i - 4) % 4 + 1) * nkt // spread):
                        steps.append(values((i - 4) // 4, kt))
            for kt in range(nkt):
                steps.append(values(ng - 1, kt))
            return steps

        q_parts = lambda Q: [(Q[0:48, :, :], 0, 3, False), (Q[48:80, :, :], 0, 2, False), (Q[80:96, :, :], 0, 1, False)]
        k_parts = lambda K: [(K[0:48, :, :], 0, 3, True), (K[48:80, :, :], 1, 2, True), (K[80:96, :, :], 2, 1, False)]

        def mask_row(dst, msk, t_m, ne, nh, free):
            return sp.go(dst, msk[0:1, None, 0:ne].broadcast_to([1, nh, ne]), t_m, free)

        def layer0():
            with ExitStack() as lc:
                sb = sb_of(lc, "l0_")
                rows = load_rows(sb, ["bv0"])
                wq, wk, wv = (load_w(sb, n, 2, 256) for n in ("WqT0", "WkT0", "WvT0"))
                X = Ring([Slot(sb(f"X{i}", [128, 2, 512])) for i in range(3)])
                C = Ring([Slot(sb(f"C{i}", [128, 2, 512])) for i in range(2)])
                MK8 = Ring([Slot(sb(f"MK8{i}", [128, 512], u8)) for i in range(3)])
                MK = Ring([Slot(sb(f"MK{i}", [128, 512])) for i in range(3)])
                MB = Ring([Slot(sb(f"MB{i}", [1, 512], bf16)) for i in range(2)])
                ST = Ring([Slot((sb(f"QS{i}", [128, 8, 512], bf16), sb(f"KS{i}", [128, 8, 512], bf16))) for i in range(3)])
                T = Ring([Slot(sb(f"T{i}", [128, 3, 512], bf16)) for i in range(2)])
                F = Ring([Slot(sb(f"F{i}", [128, 512])[:, :]) for i in range(2)])
                VV = Ring([Slot(sb(f"V{i}", [128, 4, 8, 32])) for i in range(3)])
                M = Ring([Slot(sb(f"M{i}", [128, 4, 8])) for i in range(2)])
                SP = Slot((sb("M3", [128, 4, 24], bf16), sb("Mr", [128, 4, 8])))
                MT = Slot(sb("MT", [24, 512], bf16))
                P = Ring([Slot(sb(f"P{i}", [128, 2048])) for i in range(8)])
                RB = Slot(sb("RB", [128, 2, 512]))
                sums = Sums(sb, "l0", 8, 512, 4)
                SS = Slot(sb("SS", [128, 512]))
                E = Ring([Slot(sb(f"E{i}", [128, 512])) for i in range(2)])
                ME = Ring([Slot((sb(f"ME{i}", [128, 2, 512]), sb(f"EX{i}", [128, 2, 512]))) for i in range(2)])
                OUT = Slot(sb("OUT", [128, 2, 512]))
                sm = sb("sm", [128, 16])
                for s in ST.slots:
                    s.ready = [set_rows(t, 8, 512, False) for t in s.t]

                def a1(it):
                    s = it.s
                    it.st, it.vv, it.m = ST.next(), VV.next(), M.next()
                    QS, KS = it.st.t
                    steps = []

                    def load():
                        s.X, s.C, s.mk8, s.mk, s.mb = X.next(), C.next(), MK8.next(), MK.next(), MB.next()
                        s.tX = pq.go(s.X.t[:, :, :], I["x"][it.b].rearrange("(n p) t -> p n t", p=128), s.X.free)
                        s.tC = pq.go(s.C.t[:, :, :], I["ctx"][it.b].rearrange("(n p) t -> p n t", p=128), s.C.free)
                        t8 = pq.go(s.mk8.t[:, :], I["mask0"][it.b].broadcast_to([128, 512]), s.mk8.free)
                        s.tmk = dve.do(lambda e: e.tensor_copy(s.mk.t[:, :], s.mk8.t[:, :]), t8, s.mk.free)
                        s.tmb = dve.do(lambda e: e.tensor_scalar(s.mb.t[:, :], s.mk.t[0:1, :], -1.0, NEG, ALU.add, ALU.mult),
                                       s.tmk, s.mb.free)
                        s.mk8.free = [s.tmk]
                        s.mb.free = []

                    def qk(w, src, tsrc, bias, scr, parts):
                        hold = {}

                        def f():
                            bank, Tn, Fn = bankA.next(), T.next(), F.next()
                            t = project(bank, 0, 512, [(w[:, c, it.h * 128:it.h * 128 + 128], src()[:, c, :]) for c in range(2)],
                                        tsrc())
                            act.wait(Tn.free)
                            a0, a1_ = evacuate(bank.t[:, :], t, Tn.t[:, 0, :], Fn, bias[:, it.h:it.h + 1])
                            bank.free = [a1_]
                            hold["x"] = (Tn, Fn, a1_)

                        def g():
                            Tn, Fn, a = hold["x"]
                            tk = split3([Tn.t[:, i, :] for i in range(3)], Fn, a)
                            wr, ready = stack_rows(it.st.free, Tn.t, tk, scr.next(), parts)
                            Tn.free = wr
                            it.t_stack += ready
                        return [f, (g, 0.04)]

                    def vproj(tp):
                        def f():
                            bank = bankA.next()
                            for k in range(2):
                                tt = 2 * tp + k
                                t = project(bank, 128 * k, 128 * k + 128,
                                            [(s.C.t[:, c, tt * 128:tt * 128 + 128], wv[:, c, it.h * 128:it.h * 128 + 128])
                                             for c in range(2)], s.tC)
                                bank.free = []
                            Vt = it.vv.t
                            br = rows["bv0"][:, it.h * 128:it.h * 128 + 128].rearrange("p (h d) -> p h d", d=16)
                            dv = []
                            for k in range(2):
                                src = bank.t[:, 128 * k:128 * k + 128].rearrange("p (h d) -> p h d", d=16)
                                dv.append(dve.do(lambda e, k=k, src=src: e.tensor_tensor(
                                    Vt[:, 2 * tp + k, :, 0:16], src, br, ALU.add), t, it.vv.free))
                            bank.free = dv
                            it.t_V += dv
                            for k in range(2):
                                v = Vt[:, 2 * tp + k, :, 0:16]
                                it.t_V.append(pool.do(lambda e, k=k, v=v: e.tensor_tensor(
                                    Vt[:, 2 * tp + k, :, 16:32], v, v, ALU.mult), dv[k], it.vv.free))
                            s.C.free = [t]
                        return f

                    def mrow():
                        it.t_stack.append(mask_row(KS[96:97, :, :], s.mb.t, s.tmb, 512, 8, [it.st.free, it.st.ready]))
                        s.mb.free = s.mb.free + [it.t_stack[-1]]

                    it.t_stack, it.t_V = [], []
                    if it.h == 0:
                        steps.append(load)
                    steps += qk(wq, lambda: s.X.t, lambda: s.tX, col["bq0"], scrq, q_parts(QS))
                    steps += qk(wk, lambda: s.C.t, lambda: s.tC, col["bk0"], scrk, k_parts(KS))
                    steps.append(mrow)
                    steps += [vproj(0), vproj(1)]
                    it.V = lambda kt, h: it.vv.t[:, kt, h, :]
                    return steps

                def a2(it):
                    QS, KS = it.st.t
                    steps = []
                    tk = []

                    def smax(h, qt):
                        def f():
                            bank = bankA.next()
                            t = pe.do(lambda e: e.matmul(bank.t[:, :], QS[0:97, h, qt * 128:qt * 128 + 128], KS[0:97, h, :],
                                                         start=True, stop=True), bank.free, it.t_stack, it.st.ready)
                            d = dve.do(lambda e: e.tensor_reduce(it.m.t[:, qt, h:h + 1], bank.t[:, :], AX.X, ALU.max), t, it.m.free)
                            bank.free = [d]
                            tk.append(d)
                            it.last_s = t
                        return f
                    for qt in range(4):
                        for h in range(8):
                            steps.append(smax(h, qt))

                    def rows_():
                        it.t_rows = maxima_rows(it.m, [tk[-1]], 8, 4, SP, MT, QS)
                    steps.append(rows_)
                    return steps

                def c(it):
                    QS, KS = it.st.t

                    def group_done(g, t):
                        if g == 0 and it.h == 0:
                            it.s.me = ME.next()
                            it.s.t_me = []
                        E_ = E.next()
                        me, ex = it.s.me.t
                        if g == 0:
                            it.sums = sums.take()
                        d = act.do(lambda e: e.activation(SS.t[:, :], bankS.t[:, :], ACT.Copy), t, SS.free)
                        d2 = act.do(lambda e: e.activation(E_.t[:, :], bankV.t[:, :], ACT.Copy), t, E_.free)
                        bankS.free, bankV.free = [d], [d2]
                        SS.free = [sums.put(it.sums, (4 * g, 4 * g + 4, 0, 512), SS.t[0:97:32, :], d)]
                        fr = []
                        for j in range(4):
                            for k, dst in enumerate((me, ex)):
                                p0 = 16 * (4 * g + j)
                                fr.append(sp.go(dst[p0:p0 + 16, it.h, :], E_.t[32 * j + 16 * k:32 * j + 16 * k + 16, :],
                                                d2, it.s.me.free))
                        E_.free = fr
                        it.s.t_me += fr
                        if g == 1:
                            it.st.free = [t]
                            it.vv.free = [t]
                    it.group_done = group_done
                    return attend(it, list(range(8)), 4, 512, 0.25, P,
                                  lambda h, kt: [(KS[0:100, h, kt * 128:kt * 128 + 128], QS[0:100, h, :])], True)

                def p(it):
                    s = it.s

                    def inv():
                        sums.invert(it.sums)

                    def spread():
                        if it.h == 0:
                            s.t_rb = []
                            s.rbfree = RB.free
                        x = sums.spread(it.sums, RB.t[:, it.h, :], 0, 8, 16, s.rbfree)
                        it.sums.free = [x]
                        s.t_rb.append(x)
                    if it.h == 0:
                        return [inv, nop, nop, spread, nop, nop]
                    me, ex = s.me.t
                    Xt, mk = s.X.t, s.mk.t
                    o = OUT.t

                    def f1():
                        s.d = []
                        for n in range(2):
                            a = dve.do(lambda e, n=n: e.tensor_tensor_reduce(
                                out=Xt[:, n, :], in0=Xt[:, n, :], in1=mk[:, :], scale=1.0, scalar=0.0, op0=ALU.mult,
                                op1=ALU.add, accum_out=sm[:, n:n + 1]), s.tX, s.tmk, dve.last(), act.last(), pool.last(), s.xread)
                            b_ = act.do(lambda e, n=n: e.activation(o[:, n, :], Xt[:, n, :], ACT.Square,
                                                                    accum_out=sm[:, 2 + n:3 + n]), a, OUT.free, act.last())
                            s.d.append(b_)
                        s.n = dve.do(lambda e: e.tensor_reduce(sm[:, 4:5], mk[:, :], AX.X, ALU.add))

                    def f2():
                        t = dve.do(lambda e: e.reciprocal(sm[:, 5:6], sm[:, 4:5]), s.n)
                        t = dve.do(lambda e: e.tensor_scalar(sm[:, 6:10], sm[:, 0:4], sm[:, 5:6], None, ALU.mult), t, s.d)
                        t1 = dve.do(lambda e: e.tensor_tensor(sm[:, 10:12], sm[:, 6:8], sm[:, 6:8], ALU.mult), t)
                        t2 = dve.do(lambda e: e.tensor_tensor(sm[:, 12:14], sm[:, 8:10], sm[:, 10:12], ALU.subtract), t1)
                        t3 = dve.do(lambda e: e.tensor_scalar(sm[:, 12:14], sm[:, 12:14], 0.0, 1e-5, ALU.max, ALU.add), t2)
                        s.t3 = t3

                    def f3():
                        t = dve.do(lambda e: e.tensor_tensor(me[:, :, :], me[:, :, :], RB.t[:, :, :], ALU.mult), s.t_me, s.t_rb)
                        t2 = pool.do(lambda e: e.tensor_tensor(ex[:, :, :], ex[:, :, :], RB.t[:, :, :], ALU.mult), s.t_me, s.t_rb)
                        RB.free = [t, t2]
                        t = dve.do(lambda e: e.tensor_tensor(o[:, :, :], me[:, :, :], me[:, :, :], ALU.mult), t, s.d)
                        t = dve.do(lambda e: e.tensor_tensor(ex[:, :, :], ex[:, :, :], o[:, :, :], ALU.subtract), t, t2)
                        t = dve.do(lambda e: e.tensor_scalar(ex[:, :, :], ex[:, :, :], 0.0, None, ALU.max), t)
                        s.t4 = act.do(lambda e: e.activation(ex[:, :, :], ex[:, :, :], ACT.Sqrt), t)
                        s.t5 = act.do(lambda e: e.activation(sm[:, 14:16], sm[:, 12:14], ACT.Sqrt), s.t3)

                    def f4():
                        t = dve.do(lambda e: e.reciprocal(sm[:, 12:14], sm[:, 14:16]), s.t5)
                        last = []
                        for n in range(2):
                            a = dve.do(lambda e, n=n: e.tensor_scalar(Xt[:, n, :], Xt[:, n, :], sm[:, 6 + n:7 + n],
                                                                      sm[:, 12 + n:13 + n], ALU.subtract, ALU.mult), t)
                            a = (pool if n else dve).do(lambda e, n=n: e.tensor_tensor(Xt[:, n, :], Xt[:, n, :], mk[:, :], ALU.mult), a)
                            a = (pool if n else dve).do(lambda e, n=n: e.tensor_tensor(Xt[:, n, :], Xt[:, n, :], ex[:, n, :], ALU.mult), a, s.t4)
                            a = (pool if n else dve).do(lambda e, n=n: e.tensor_tensor(Xt[:, n, :], Xt[:, n, :], me[:, n, :], ALU.add), a)
                            a = (pool if n else dve).do(lambda e, n=n: e.tensor_tensor(o[:, n, :], Xt[:, n, :], mk[:, :], ALU.mult), a)
                            last.append(a)
                        s.X.free = s.mk.free = s.me.free = last
                        OUT.free = [pq.go(x1[it.b].rearrange("(n p) t -> p n t", p=128), o[:, :, :], last)]
                    s.xread = it.t_xread
                    return [inv, nop, f1, f2, spread, nop, f3, f4]

                its = items_of()

                def a2w(it):
                    return a2(it)

                def cw(it):
                    it.t_xread = it.t_stack
                    return c(it)
                pipeline(its, a1, a2w, cw, p)
                barrier()

        def layer1a():
            with ExitStack() as lc:
                sb = sb_of(lc, "l1a_")
                rows = load_rows(sb, ["vb1", "ob1"])
                wq = load_w(sb, "q_w1", 4, 512)
                wk = load_w(sb, "k_w1", 4, 512)
                wv = load_w(sb, "v_w1", 4, 512)
                wo = load_w(sb, "out_w1", 4, 512)
                LAT = Ring([Slot(sb(f"LAT{i}", [128, 2, 512])) for i in range(3)])
                HT = Ring([Slot(sb(f"HT{i}", [128, 4, 512])) for i in range(1)])
                MI = Ring([Slot(sb(f"MI{i}", [1, 256], i32)) for i in range(1)])
                MF = Ring([Slot(sb(f"MF{i}", [1, 256])) for i in range(1)])
                MB = Ring([Slot(sb(f"MB{i}", [1, 512], bf16)) for i in range(2)])
                ST = Ring([Slot((sb(f"QA{i}", [128, 8, 256], bf16), sb(f"QB{i}", [96, 8, 256], bf16),
                                 sb(f"KA{i}", [128, 8, 512], bf16), sb(f"KB{i}", [96, 8, 512], bf16))) for i in range(3)])
                TQ = Ring([Slot(sb(f"TQ{i}", [128, 3, 2, 256], bf16)) for i in range(1)])
                TK = Ring([Slot(sb(f"TK{i}", [128, 3, 2, 512], bf16)) for i in range(1)])
                F = Ring([Slot(sb(f"F{i}", [128, 512])) for i in range(2)])
                VV = Ring([Slot(sb(f"V{i}", [128, 4, 256])) for i in range(3)])
                M = Ring([Slot(sb(f"M{i}", [128, 2, 8])) for i in range(2)])
                SP = Slot((sb("M3", [128, 2, 24], bf16), sb("Mr", [128, 2, 8])))
                MT = Slot(sb("MT", [24, 256], bf16))
                P = Ring([Slot(sb(f"P{i}", [128, 1024])) for i in range(8)])
                RB = Slot(sb("RB", [128, 4, 256]))
                sums = Sums(sb, "l1", 8, 256, 4)
                SS = Slot(sb("SS", [128, 256]))
                AT = Ring([Slot(sb(f"AT{i}", [128, 4, 256])) for i in range(2)])
                sm = sb("sm", [128, 4])
                for s in ST.slots:
                    s.ready = [set_rows(s.t[0], 8, 256, False), set_rows(s.t[2], 8, 512, False)]
                for s in MB.slots:
                    s.ready = [dve.do(lambda e, s=s: e.memset(s.t[:, 256:512], 0.0))]

                def a1(it):
                    s = it.s
                    it.st, it.vv, it.m = ST.next(), VV.next(), M.next()
                    QA, QB, KA, KB = it.st.t
                    it.t_stack, it.t_V = [], []
                    steps = []

                    def load():
                        s.L, s.H, s.mb = LAT.next(), HT.next(), MB.next()
                        mi, mf = MI.next(), MF.next()
                        s.tL = pq.go(s.L.t[:, :, :], x1[it.b].rearrange("(n p) t -> p n t", p=128), s.L.free)
                        s.tH = [pq.go(s.H.t[:, :, 0:256], I["ctxT"][it.b].rearrange("(n p) t -> p n t", p=128), s.H.free)]
                        t8 = pq.go(mi.t[:, :], I["mask1"][it.b:it.b + 1, :], mi.free)
                        a = dve.do(lambda e: e.tensor_scalar(mf.t[:, :], mi.t[:, :], 0.0, None, ALU.not_equal), t8, mf.free)
                        mi.free = [a]
                        s.tmb = dve.do(lambda e: e.tensor_scalar(s.mb.t[:, 0:256], mf.t[:, :], -1.0, NEG, ALU.add, ALU.mult),
                                       a, s.mb.free, s.mb.ready)
                        mf.free = [s.tmb]
                        s.mb.free = []

                    def lat_t(tt):
                        def f():
                            bank = bankA.next()
                            t = transposes([bank.t[:, q * 128:q * 128 + 128] for q in range(4)],
                                           [s.L.t[:, tt, q * 128:q * 128 + 128] for q in range(4)], bank, s.tL)
                            a = act.do(lambda e: e.activation(s.H.t[:, :, 256 + tt * 128:384 + tt * 128],
                                                              bank.t[:, :].rearrange("p (a b) -> p a b", a=4), ACT.Copy),
                                       t, s.H.free)
                            bank.free = [a]
                            s.tH.append(a)
                        return f

                    def qk(w, bias, dsts, T, scr, nc_, lo):
                        hold = {"tk": []}

                        def f(o):
                            og = 2 * it.h + o
                            if o == 0:
                                hold["T"] = T.next()
                                for x in (act, dve, pool):
                                    x.wait(hold["T"].free)
                            Tn = hold["T"]
                            bank, Fn = bankA.next(), F.next()
                            t = project(bank, 0, nc_, [(w[:, c, og * 128:og * 128 + 128], s.H.t[:, c, lo:lo + nc_])
                                                       for c in range(4)], s.tH)
                            Fv = Slot(Fn.t[:, 0:nc_])
                            Fv.free = Fn.free
                            a0, a1_ = evacuate(bank.t[:, 0:nc_], t, Tn.t[:, 0, o, :], Fv, bias[:, og:og + 1])
                            bank.free = [a1_]
                            s.H.free = [t]
                            hold[o] = (Fn, Fv, a1_)

                        def g(o):
                            Tn, (Fn, Fv, a) = hold["T"], hold[o]
                            hold["tk"].append(split3([Tn.t[:, i, o, :] for i in range(3)], Fv, a))
                            Fn.free = Fv.free
                            if o == 1:
                                wr, ready = stack(None, it.st.free, Tn.t[:, :, :, :], hold["tk"], scr.next(),
                                                  [(d[32 * r:32 * r + 32, :, :], i) for d, order in dsts for r, i in enumerate(order)],
                                                  2, 32, nc_)
                                Tn.free = [wr]
                                it.t_stack += ready
                        return [lambda: f(0), (lambda: g(0), 0.04), lambda: f(1), (lambda: g(1), 0.04)]

                    def vproj(tt):
                        def f():
                            bank = bankA.next()
                            t = project(bank, 0, 256, [(s.H.t[:, c, tt * 128:tt * 128 + 128],
                                                        wv[:, c, it.h * 256:it.h * 256 + 256]) for c in range(4)], s.tH)
                            d = dve.do(lambda e: e.tensor_tensor(it.vv.t[:, tt, :], bank.t[:, 0:256],
                                                                 rows["vb1"][:, it.h * 256:it.h * 256 + 256], ALU.add),
                                       t, it.vv.free)
                            bank.free = [d]
                            it.t_V.append(d)
                            s.H.free = [t]
                        return f

                    def mrow():
                        it.t_stack.append(mask_row(KA[96:97, :, :], s.mb.t, s.tmb, 512, 8, [it.st.free, it.st.ready]))
                        s.mb.free = s.mb.free + [it.t_stack[-1]]

                    if it.h == 0:
                        steps += [load, lat_t(0), lat_t(1)]
                    steps += qk(wk, col["kb1"], [(KA, [0, 1, 0]), (KB, [2, 1, 0])], TK, scrk, 512, 0)
                    steps += qk(wq, col["qb1"], [(QA, [0, 0, 1]), (QB, [0, 1, 2])], TQ, scrq, 256, 256)
                    steps.append(mrow)
                    steps += [vproj(i) for i in range(4)]
                    it.V = lambda kt, h: it.vv.t[:, kt, h * 32:h * 32 + 32]
                    return steps

                def a2(it):
                    QA, QB, KA, KB = it.st.t
                    tk = []

                    def smax(h, qt):
                        def f():
                            bank = bankA.next()
                            t = pe.do(lambda e: e.matmul(bank.t[:, :], QA[0:97, h, qt * 128:qt * 128 + 128], KA[0:97, h, :],
                                                         start=True, stop=True), bank.free, it.t_stack, it.st.ready)
                            d = dve.do(lambda e: e.tensor_reduce(it.m.t[:, qt, h:h + 1], bank.t[:, :], AX.X, ALU.max), t, it.m.free)
                            bank.free = [d]
                            tk.append(d)
                        return f

                    def rows_():
                        it.t_rows = maxima_rows(it.m, [tk[-1]], 8, 2, SP, MT, QA)
                    return [smax(h, qt) for qt in range(2) for h in range(8)] + [rows_]

                def c(it):
                    QA, QB, KA, KB = it.st.t

                    def group_done(g, t):
                        if g == 0 and it.h == 0:
                            it.s.at = AT.next()
                            it.s.t_at = []
                        if g == 0:
                            it.sums = sums.take()
                        d = act.do(lambda e: e.activation(SS.t[:, :], bankS.t[:, 0:256], ACT.Copy), t, SS.free)
                        d2 = act.do(lambda e: e.activation(it.s.at.t[:, 2 * it.h + g, :], bankV.t[:, 0:256], ACT.Copy), t, it.s.at.free)
                        bankS.free, bankV.free = [d], [d2]
                        SS.free = [sums.put(it.sums, (4 * g, 4 * g + 4, 0, 256), SS.t[0:97:32, :], d)]
                        it.s.t_at.append(d2)
                        if g == 1:
                            it.st.free = [t]
                            it.vv.free = [t]
                    it.group_done = group_done
                    return attend(it, list(range(8)), 4, 256, 1.0 / 32, P,
                                  lambda h, kt: [(KA[0:100, h, kt * 128:kt * 128 + 128], QA[0:100, h, :]),
                                                 (KB[0:96, h, kt * 128:kt * 128 + 128], QB[0:96, h, :])], True)

                def p(it):
                    s = it.s

                    def inv():
                        sums.invert(it.sums)

                    def spread():
                        if it.h == 0:
                            s.t_rb = []
                            s.rbfree = RB.free
                        for g in range(2):
                            x = sums.spread(it.sums, RB.t[:, 2 * it.h + g, :], 4 * g, 4 * g + 4, 32, s.rbfree)
                            s.t_rb.append(x)
                        it.sums.free = s.t_rb[-2:]
                    if it.h == 0:
                        return [inv, nop, nop, spread, nop, nop]

                    def f0():
                        t = pool.do(lambda e: e.tensor_tensor(s.at.t[:, :, :], s.at.t[:, :, :], RB.t[:, :, :], ALU.mult), s.t_at, s.t_rb)
                        RB.free = [t]
                        s.t_at = [t]

                    def f1():
                        s.sq, s.banks = [], []
                        L, j = s.L.t, s.at.t.rearrange("p (a b) q -> p a (b q)", a=2)
                        for tt in range(2):
                            bank = bankA.next()
                            t = project(bank, 0, 512, [(s.at.t[:, g, tt * 128:tt * 128 + 128], wo[:, g, :]) for g in range(4)],
                                        s.t_at)
                            s.banks.append((bank, t))
                        for tt, (bank, t1) in enumerate(s.banks):
                            a = dve.do(lambda e, tt=tt, bank=bank: e.tensor_tensor(L[:, tt, :], bank.t[:, :], L[:, tt, :],
                                                                                 ALU.add), t1)
                            bank.free = [a]
                            b_ = dve.do(lambda e, tt=tt: e.tensor_tensor(L[:, tt, :], L[:, tt, :], rows["ob1"][:, :], ALU.add), a)
                            s.sq.append(act.do(lambda e, tt=tt: e.activation(j[:, tt, :], L[:, tt, :], ACT.Square,
                                                                             accum_out=sm[:, tt:tt + 1]), b_, t, dve.last()))
                        s.at.free = [t, s.sq[-1]]

                    def f2():
                        L = s.L.t
                        t = rstd_of(sm[:, 0:2], sm[:, 0:2], 1e-6, 1.0 / 512, s.sq)
                        last = [dve.do(lambda e, tt=tt: e.tensor_scalar(L[:, tt, :], L[:, tt, :], sm[:, tt:tt + 1],
                                                                        None, ALU.mult), t) for tt in range(2)]
                        s.L.free = [pq.go(y1[it.b].rearrange("(n p) t -> p n t", p=128), L[:, :, :], last)]
                    return [inv, nop, nop, spread, nop, f0, f1, f2]
                pipeline(items_of(), a1, a2, c, p)
                barrier()

        def layer1b():
            with ExitStack() as lc:
                sb = sb_of(lc, "l1b_")
                rows = load_rows(sb, ["mb2"])
                w1 = load_w(sb, "mlp_w1", 4, 2048)
                w2 = load_w(sb, "mlp_w2", 16, 512)
                YN = Ring([Slot(sb(f"YN{i}", [128, 4, 512])) for i in range(2)])
                YT = Slot(sb("YT", [128, 4, 512]))
                LT = Ring([Slot(sb(f"LT{i}", [128, 4, 512])) for i in range(2)])
                H1 = Slot(sb("H1", [128, 16, 512]))
                banks = Ring([Slot(PS[:, i, :]) for i in range(8)])
                for b in range(0, batches, 2):
                    nb = min(2, batches - b)
                    n4, w = 2 * nb, 256 * nb
                    yn, lt = YN.next(), LT.next()
                    ty = sp.go(yn.t[:, 0:n4, :], y1[b:b + nb].rearrange("b (n p) t -> p (b n) t", p=128), yn.free)
                    tl = sp.go(lt.t[:, 0:n4, :], x1[b:b + nb].rearrange("b (n p) t -> p (b n) t", p=128), lt.free)
                    ev = []
                    for f in range(4):
                        bank = banks.next()
                        t = transposes([bank.t[:, q * 128:q * 128 + 128] for q in range(n4)],
                                       [yn.t[:, q, f * 128:f * 128 + 128] for q in range(n4)], bank, ty)
                        d = dve.do(lambda e, f=f, bank=bank: e.tensor_scalar(YT.t[:, f, 0:w], bank.t[:, 0:w],
                                                                             col["pn1"][:, f:f + 1], None, ALU.mult), t, YT.free)
                        bank.free = [d]
                        ev.append(d)
                    yn.free = [t]
                    hs = []
                    for o in range(16):
                        bank = banks.next()
                        t = project(bank, 0, w, [(w1[:, c, o * 128:o * 128 + 128], YT.t[:, c, 0:w]) for c in range(4)], ev)
                        a = act.do(lambda e, o=o, bank=bank: e.activation(H1.t[:, o, 0:w], bank.t[:, 0:w], ACT.Gelu_apprx_tanh,
                                                                          bias=col["mb1"][:, o:o + 1]), t, H1.free)
                        bank.free = [a]
                        hs.append(a)
                    YT.free = [t]
                    last = []
                    for tt in range(n4):
                        bank = banks.next()
                        t = project(bank, 0, 512, [(H1.t[:, o, tt * 128:tt * 128 + 128], w2[:, o, :]) for o in range(16)], hs)
                        d = dve.do(lambda e, tt=tt, bank=bank, lt=lt: e.tensor_tensor(lt.t[:, tt, :], bank.t[:, :], lt.t[:, tt, :],
                                                                                      ALU.add), t, tl)
                        bank.free = [d]
                        last.append(dve.do(lambda e, tt=tt, lt=lt: e.tensor_tensor(lt.t[:, tt, :], lt.t[:, tt, :], rows["mb2"][:, :],
                                                                            ALU.add), d))
                    H1.free = [t]
                    lt.free = [sp.go(x2[b:b + nb].rearrange("b (n p) t -> p (b n) t", p=128), lt.t[:, 0:n4, :], last)]
                for s in bankA.slots + bankC.slots + [bankV, bankS]:
                    s.free = []
                barrier()

        def layer2():
            with ExitStack() as lc:
                sb = sb_of(lc, "l2_")
                rows = load_rows(sb, ["bv2", "bo2", "g2", "be2"])
                wq = load_w(sb, "Wq2", 4, 512)
                wk = load_w(sb, "Wk2", 4, 128)
                wv = load_w(sb, "Wv2", 4, 128)
                wo = load_w(sb, "Wo2", 4, 512)
                X = Ring([Slot(sb(f"X{i}", [128, 2, 512])) for i in range(3)])
                XT = Ring([Slot(sb(f"XT{i}", [128, 4, 256])) for i in range(2)])
                CT = Ring([Slot(sb(f"CT{i}", [128, 4, 256])) for i in range(2)])
                MK = Ring([Slot((sb(f"MK{i}", [128, 2, 256]), sb(f"MKT{i}", [128, 2, 256]))) for i in range(3)])
                QSR = Ring([Slot(sb(f"QS{i}", [128, 16, 256], bf16)) for i in range(3)])
                KSR = Ring([Slot(sb(f"KS{i}", [128, 8, 256], bf16)) for i in range(3)])
                T = Ring([Slot(sb(f"T{i}", [128, 3, 2, 256], bf16)) for i in range(2)])
                F = Ring([Slot(sb(f"F{i}", [128, 256])[:, :]) for i in range(2)])
                VV = Ring([Slot(sb(f"V{i}", [128, 2, 8, 17])) for i in range(3)])
                M = Ring([Slot(sb(f"M{i}", [128, 2, 16])) for i in range(2)])
                SP = Slot((sb("M3", [128, 2, 48], bf16), sb("Mr", [128, 2, 16])))
                MT = Slot(sb("MT", [48, 256], bf16))
                P = Ring([Slot(sb(f"P{i}", [128, 2, 4, 256])) for i in range(4)])
                JK = Ring([Slot(sb(f"JK{i}", [128, 256])) for i in range(2)])
                E = Ring([Slot(sb(f"E{i}", [128, 512])) for i in range(2)])
                AT = Ring([Slot(sb(f"AT{i}", [128, 4, 256])) for i in range(2)])
                RB = Slot(sb("RB", [128, 4, 256]))
                sums = Sums(sb, "l2", 16, 256, 4)
                Y = Slot(sb("Y", [128, 2, 512]))
                st_ = sb("st", [128, 2, 6])
                mv = sb("mv", [128, 2, 2])
                rs = sb("rs", [128, 2])
                for s in QSR.slots:
                    s.ready = set_rows(s.t, 16, 256, False)
                for s in KSR.slots:
                    s.ready = set_rows(s.t, 8, 256, True)
                for s in VV.slots:
                    s.ready = [pool.do(lambda e, s=s: e.memset(s.t[:, :, :, 16:17], 1.0))]

                def a1(it):
                    s = it.s
                    it.qs, it.m = QSR.next(), M.next()
                    it.st = it.qs
                    it.t_stack = []
                    steps = []

                    def load():
                        s.X, s.XT, s.C, s.mk, s.ks, s.vv = X.next(), XT.next(), CT.next(), MK.next(), KSR.next(), VV.next()
                        s.t_k, s.t_V = [], []
                        s.tX = pq.go(s.X.t[:, :, :], x2[it.b].rearrange("(n p) t -> p n t", p=128), s.X.free)
                        s.tC = pq.go(s.C.t[:, :, :], I["ctxT"][it.b].rearrange("(n p) t -> p n t", p=128), s.C.free)
                        s.tmk = []
                        for t, name in zip(s.mk.t, ("mask2", "mask2T")):
                            a = pq.go(t[:, :, :], I[name][it.b].rearrange("(n p) t -> p n t", p=128), s.mk.free)
                            s.tmk.append(pool.do(lambda e, t=t: e.tensor_scalar(t[:, :, :], t[:, :, :], 4.0, None, ALU.mult), a))

                    def xt(tt):
                        def f():
                            bank = bankA.next()
                            t = transposes([bank.t[:, q * 128:q * 128 + 128] for q in range(4)],
                                           [s.X.t[:, tt, q * 128:q * 128 + 128] for q in range(4)], bank, s.tX)
                            a = act.do(lambda e: e.activation(s.XT.t[:, :, tt * 128:tt * 128 + 128],
                                                              bank.t[:, :].rearrange("p (a b) -> p a b", a=4), ACT.Copy),
                                       t, s.XT.free)
                            bank.free = [a]
                            s.tXT = [a] if tt == 0 else s.tXT + [a]
                        return f

                    def project3(w, o, src, ts, bias, Tn, i_):
                        bank, Fn = bankA.next(), F.next()
                        t = project(bank, 0, 256, [(w[:, c, o:o + 128], src[:, c, :]) for c in range(4)], ts)
                        a0, a1_ = evacuate(bank.t[:, 0:256], t, Tn.t[:, 0, i_, :], Fn, bias)
                        bank.free = [a1_]
                        return t, Fn, a1_

                    def q():
                        hold = {"tk": []}

                        def f(o):
                            og = 2 * it.h + o
                            if o == 0:
                                hold["T"] = T.next()
                                for x in (act, dve, pool):
                                    x.wait(hold["T"].free)
                            t, *hold[o] = project3(wq, og * 128, s.XT.t, s.tXT, col["bq2"][:, og:og + 1], hold["T"], o)
                            s.XT.free = [t]

                        def g(o):
                            Tn, (Fn, a) = hold["T"], hold[o]
                            hold["tk"].append(split3([Tn.t[:, i, o, :] for i in range(3)], Fn, a))
                            if o == 1:
                                Q = it.qs.t
                                wr, ready = stack(None, it.qs.free, Tn.t[:, :, :, :], hold["tk"], scrq.next(),
                                                  [(Q[16 * r:16 * r + 16, :, :], i) for r, i in enumerate([0, 1, 2, 0, 1, 0])],
                                                  2, 16, 256)
                                Tn.free = [wr]
                                it.t_stack += ready + s.t_k
                        return [lambda: f(0), (lambda: g(0), 0.04), lambda: f(1), (lambda: g(1), 0.04)]

                    def k():
                        hold = {}

                        def f():
                            Tn = T.next()
                            for x in (act, dve, pool):
                                x.wait(Tn.free)
                            hold["x"] = (Tn, *project3(wk, 0, s.C.t, s.tC, col["bk2"][:, 0:1], Tn, 0)[1:])

                        def g():
                            Tn, Fn, a = hold["x"]
                            tk = split3([Tn.t[:, i, 0, :] for i in range(3)], Fn, a)
                            K = s.ks.t
                            wr, ready = stack(None, s.ks.free, Tn.t[:, :, 0:1, :], tk, scrk.next(),
                                              [(K[16 * r:16 * r + 16, :, :], i) for r, i in enumerate([0, 0, 0, 1, 1, 2])],
                                              1, 16, 256)
                            Tn.free = [wr]
                            s.t_k = ready + s.ks.ready
                        return [f, (g, 0.04)]

                    def v():
                        bank = bankA.next()
                        for tt in range(2):
                            t = project(bank, 128 * tt, 128 * tt + 128,
                                        [(s.C.t[:, c, tt * 128:tt * 128 + 128], wv[:, c, :]) for c in range(4)], s.tC)
                            bank.free = []
                        br = rows["bv2"][:, :].rearrange("p (h d) -> p h d", d=16)
                        for tt in range(2):
                            s.t_V.append(dve.do(lambda e, tt=tt: e.tensor_tensor(
                                s.vv.t[:, tt, :, 0:16], bank.t[:, 128 * tt:128 * tt + 128].rearrange("p (h d) -> p h d", d=16),
                                br, ALU.add), t, s.vv.free, s.vv.ready))
                        bank.free = s.t_V[-2:]
                        s.C.free = [t]

                    if it.h == 0:
                        steps += [load, xt(0), xt(1)] + k() + [v]
                    steps += q()
                    return steps

                def a2(it):
                    s, Q = it.s, it.qs.t
                    tk = []

                    def smax(hp, qt):
                        def f():
                            bank = bankA.next()
                            pe.wait(bank.free, it.t_stack, it.qs.ready)
                            for i in range(2):
                                h = 2 * hp + i
                                g = lambda e, i=i, h=h: e.matmul(
                                    bank.t[:, 256 * i:256 * i + 256], Q[0:97, h, qt * 128:qt * 128 + 128],
                                    s.ks.t[0:97, 4 * it.h + h // 4, :], start=True, stop=True, skip_group_check=True)
                                if i:
                                    t = pe.do(g)
                                else:
                                    pe.quiet(g)
                            for i in range(2):
                                jk = JK.next()
                                d = dve.do(lambda e, i=i, jk=jk: e.tensor_tensor_reduce(
                                    out=jk.t[:, :], in0=bank.t[:, 256 * i:256 * i + 256], in1=s.mk.t[0][:, qt, :], scale=1.0,
                                    scalar=-3.0e38, op0=ALU.add, op1=ALU.max,
                                    accum_out=it.m.t[:, qt, 2 * hp + i:2 * hp + i + 1]), t, it.m.free, jk.free, s.tmk)
                                jk.free = [d]
                            bank.free = [d]
                            tk.append(d)
                        return f

                    def rows_():
                        it.t_rows = maxima_rows(it.m, [tk[-1]], 16, 2, SP, MT, it.qs.t)
                    return [smax(hp, qt) for qt in range(2) for hp in range(8)] + [rows_]

                def c(it):
                    s, Q = it.s, it.qs.t
                    pend, steps = [], []

                    def scores(kv, kt):
                        def f():
                            if kt == 0:
                                Pk = P.next()
                                Pk.ready = []
                                pend.append(Pk)
                            Pk = pend[kv]
                            add = []
                            for i in range(2):
                                bank = bankC.next()
                                t = pe.do(lambda e, i=i, bank=bank: e.matmul(
                                    bank.t, s.ks.t[0:100, 4 * it.h + kv, kt * 128:kt * 128 + 128],
                                    Q[0:100, 4 * kv + 2 * i:4 * kv + 2 * i + 2, :], start=True, stop=True),
                                    bank.free, it.t_rows, it.t_stack, it.qs.ready)
                                mk = s.mk.t[1][:, kt:kt + 1, :].broadcast_to([128, 2, 256])
                                d = dve.do(lambda e, i=i, mk=mk, bank=bank: e.tensor_tensor(
                                    Pk.t[:, kt, 2 * i:2 * i + 2, :], bank.t.rearrange("p (b q) -> p b q", b=2), mk, ALU.add),
                                    t, Pk.free, s.tmk)
                                bank.free = [d]
                                add.append(d)
                            Pk.ready.append(act.do(lambda e: e.activation(Pk.t[:, kt, :, :], Pk.t[:, kt, :, :], ACT.Exp,
                                                                          scale=0.25), add))
                        return f

                    def values(g, kt):
                        def f():
                            two = pend[2 * g:2 * g + 2]
                            if kt == 0:
                                it.bv = bankVV.next()
                                pe.wait(it.bv.free)
                            pe.wait(*[x.ready for x in two], s.t_V)
                            bv = it.bv
                            for j in range(4):
                                kv = 2 * g + j // 2
                                l = s.vv.t[:, kt, 4 * it.h + kv, :]
                                r = two[j // 2].t[:, kt, 2 * (j % 2):2 * (j % 2) + 2, :]
                                h = lambda e, j=j, l=l, r=r: e.matmul(
                                    bv.t[32 * j:32 * j + 17, :], l, r, start=(kt == 0), stop=(kt == 1),
                                    tile_position=(0, 32 * j), skip_group_check=True)
                                if j == 3:
                                    t = pe.do(h)
                                else:
                                    pe.quiet(h)
                            if kt == 1:
                                for x in two:
                                    x.free = [t]
                                if g == 0 and it.h == 0:
                                    s.at = AT.next()
                                    s.t_at = []
                                if g == 0:
                                    it.sums = sums.take()
                                E_ = E.next()
                                a = act.do(lambda e: e.activation(E_.t[:, :], bv.t[:, :], ACT.Copy), t, E_.free)
                                bv.free = [a]
                                fr = [sums.put(it.sums, (8 * g, 8 * g + 8, 0, 256), E_.t[16:113:32, :], a)]
                                for j in range(4):
                                    fr.append(sp.go(s.at.t[64 * g + 16 * j:64 * g + 16 * j + 16, 2 * it.h:2 * it.h + 2, :],
                                                    E_.t[32 * j:32 * j + 16, :], a, s.at.free))
                                E_.free = fr
                                s.t_at += fr
                                if g == 1:
                                    it.qs.free = [t]
                                    if it.h == 1:
                                        s.ks.free = [t]
                                        s.vv.free = [t]
                                        s.mk.free = [dve.last()]
                        return f
                    steps = [scores(0, 0), scores(0, 1), scores(1, 0), scores(1, 1), scores(2, 0), values(0, 0), scores(2, 1),
                             values(0, 1), scores(3, 0), scores(3, 1), nop, values(1, 0), values(1, 1)]
                    return steps

                def p(it):
                    s = it.s

                    def inv():
                        sums.invert(it.sums)

                    def spread():
                        if it.h == 0:
                            s.t_rb = []
                            s.rbfree = RB.free
                        x = [sp.go(RB.t[64 * g:64 * g + 64, 2 * it.h + i, :],
                                   it.sums.t[1][8 * g:8 * g + 8, None, :].rearrange("(j i) r q -> i j r q", i=2)[i]
                                   .broadcast_to([4, 16, 256]), it.sums.tokens, s.rbfree) for g in range(2) for i in range(2)]
                        it.sums.free = x
                        s.t_rb += x
                    if it.h == 0:
                        return [inv, nop, nop, spread, nop, nop]

                    def f0():
                        t = pool.do(lambda e: e.tensor_tensor(s.at.t[:, :, :], s.at.t[:, :, :], RB.t[:, :, :], ALU.mult), s.t_at, s.t_rb)
                        RB.free = [t]
                        s.t_at = [t]

                    def f1():
                        s.a = []
                        for tt in range(2):
                            bank = bankA.next()
                            t = project(bank, 0, 512, [(s.at.t[:, g, tt * 128:tt * 128 + 128], wo[:, g, :]) for g in range(4)], s.t_at)
                            a = dve.do(lambda e, tt=tt, bank=bank: e.tensor_tensor(Y.t[:, tt, :], bank.t[:, :], s.X.t[:, tt, :],
                                                                                 ALU.add), t, Y.free)
                            bank.free = [a]
                            a = dve.do(lambda e, tt=tt: e.tensor_tensor(Y.t[:, tt, :], Y.t[:, tt, :], rows["bo2"][:, :], ALU.add), a)
                            a = dve.do(lambda e, tt=tt: e.bn_stats(st_[:, tt, :], Y.t[:, tt, :]), a)
                            a = dve.do(lambda e, tt=tt: e.bn_aggr(mv[:, tt, :], st_[:, tt, :]), a)
                            s.a.append(a)
                        s.at.free = [t]
                        s.X.free = [a]

                    def f2():
                        t = rstd_of(rs[:, :], mv[:, :, 1], 1e-6, 1.0, s.a)
                        last = []
                        for tt in range(2):
                            a = dve.do(lambda e, tt=tt: e.tensor_scalar(Y.t[:, tt, :], Y.t[:, tt, :], mv[:, tt, 0:1],
                                                                        rs[:, tt:tt + 1], ALU.subtract, ALU.mult), t)
                            a = dve.do(lambda e, tt=tt: e.tensor_tensor(Y.t[:, tt, :], Y.t[:, tt, :], rows["g2"][:, :], ALU.mult), a)
                            last.append(dve.do(lambda e, tt=tt: e.tensor_tensor(Y.t[:, tt, :], Y.t[:, tt, :], rows["be2"][:, :],
                                                                                ALU.add), a))
                        Y.free = [sp.go(x3[it.b].rearrange("(n p) t -> p n t", p=128), Y.t[:, :, :], last)]
                    return [inv, nop, nop, spread, nop, f0, f1, f2]

                pipeline(items_of(), a1, a2, c, p)
                barrier()

        def layer3():
            with ExitStack() as lc:
                sb = sb_of(lc, "l3_")
                rows = load_rows(sb, ["gq3", "bq3"])
                wq, wk, wv, wo = (load_w(sb, n, 2, 256) for n in ("Wq3", "Wk3", "Wv3", "Wo3"))
                w1 = load_w(sb, "W13", 2, 512)
                w2 = load_w(sb, "W23", 4, 256)
                pos = sb("pos", [128, 4, 256])
                dve.wait(sp.go(pos[:, :, :], I["pos"].rearrange("(n p) c -> p n c", p=128)))
                X = Ring([Slot(sb(f"X{i}", [128, 2, 512])) for i in range(1)])
                QN = Ring([Slot(sb(f"QN{i}", [128, 4, 256])) for i in range(3)])
                KN = Ring([Slot(sb(f"KN{i}", [128, 4, 256])) for i in range(1)])
                QT = Ring([Slot((sb(f"QT{i}", [128, 2, 512]), sb(f"KT{i}", [128, 2, 512]))) for i in range(1)])
                ST = Ring([Slot((sb(f"QS{i}", [128, 8, 512], bf16), sb(f"KS{i}", [128, 8, 512], bf16))) for i in range(3)])
                T = Ring([Slot(sb(f"T{i}", [128, 3, 512], bf16)) for i in range(2)])
                F = Ring([Slot(sb(f"F{i}", [128, 512])[:, :]) for i in range(1)])
                VV = Ring([Slot(sb(f"V{i}", [128, 4, 8, 17])) for i in range(3)])
                M = Ring([Slot(sb(f"M{i}", [128, 4, 8])) for i in range(2)])
                SP = Slot((sb("M3", [128, 4, 24], bf16), sb("Mr", [128, 4, 8])))
                MT = Slot(sb("MT", [24, 512], bf16))
                P = Ring([Slot(sb(f"P{i}", [128, 2048])) for i in range(6)])
                E = Ring([Slot(sb(f"E{i}", [128, 512])) for i in range(1)])
                NCR = Ring([Slot(sb(f"NC{i}", [128, 2, 512])) for i in range(1)])
                RB = Slot(sb("RB", [128, 2, 512]))
                sums = Sums(sb, "l3", 8, 512, 4)
                HH = Slot(sb("HH", [128, 4, 256]))
                HTT = Slot(sb("HTT", [128, 2, 512]))
                RT = Slot(sb("RT", [128, 2, 512]))
                G = Slot(sb("G", [128, 4, 512]))
                st_ = sb("st", [128, 8, 6])
                mv = sb("mv", [128, 8, 2])
                rs = sb("rs", [128, 8])
                st2 = sb("st2", [128, 4, 6])
                mv2 = sb("mv2", [128, 4, 2])
                rs2 = sb("rs2", [128, 4])
                for s in ST.slots:
                    s.ready = [set_rows(t, 8, 512, k == 1) for k, t in enumerate(s.t)]
                for s in VV.slots:
                    s.ready = [pool.do(lambda e, s=s: e.memset(s.t[:, :, :, 16:17], 1.0))]

                def a1(it):
                    s = it.s
                    it.st, it.vv, it.m = ST.next(), VV.next(), M.next()
                    QS, KS = it.st.t
                    it.t_stack, it.t_V = [], []
                    steps = []

                    def load():
                        s.X, s.qn, s.kn, s.qt = X.next(), QN.next(), KN.next(), QT.next()
                        s.tX = pq.go(s.X.t[:, :, :], x3[it.b].rearrange("(n p) t -> p n t", p=128), s.X.free)
                        s.tC = pq.go(s.kn.t[:, :, :], I["ctxT"][it.b].rearrange("(n p) t -> p n t", p=128), s.kn.free)
                        s.ln = []

                    def kn():
                        a = dve.do(lambda e: e.tensor_tensor(s.kn.t[:, :, :], s.kn.t[:, :, :], pos[:, :, :], ALU.add), s.tC)
                        for tt in range(4):
                            b_ = dve.do(lambda e, tt=tt: e.bn_stats(st_[:, 4 + tt, :], s.kn.t[:, tt, :]), a)
                            s.ln.append(dve.do(lambda e, tt=tt: e.bn_aggr(mv[:, 4 + tt, :], st_[:, 4 + tt, :]), b_))

                    def qn(tp):
                        def f():
                            bank = bankA.next()
                            t = transposes([bank.t[:, (2 * k + cc) * 128:(2 * k + cc) * 128 + 128] for k in range(2) for cc in range(2)],
                                           [s.X.t[:, cc, (2 * tp + k) * 128:(2 * tp + k) * 128 + 128] for k in range(2) for cc in range(2)],
                                           bank, s.tX)
                            d = dve.do(lambda e: e.tensor_tensor(s.qn.t[:, 2 * tp:2 * tp + 2, :],
                                                                 bank.t[:, :].rearrange("p (a b) -> p a b", a=2),
                                                                 pos[:, 2 * tp:2 * tp + 2, :], ALU.add), t, s.qn.free)
                            bank.free = [d]
                            s.X.free = [t]
                            for k in range(2):
                                tt = 2 * tp + k
                                b_ = dve.do(lambda e, tt=tt: e.bn_stats(st_[:, tt, :], s.qn.t[:, tt, :]), d)
                                s.ln.append(dve.do(lambda e, tt=tt: e.bn_aggr(mv[:, tt, :], st_[:, tt, :]), b_))
                        return f

                    def norm():
                        t = rstd_of(rs[:, :], mv[:, :, 1], 1e-5, 1.0, s.ln)
                        s.tq, s.tk = [], []
                        for tt in range(4):
                            q = s.qn.t[:, tt, :]
                            a = dve.do(lambda e, tt=tt, q=q: e.tensor_scalar(q, q, mv[:, tt, 0:1], rs[:, tt:tt + 1],
                                                                             ALU.subtract, ALU.mult), t)
                            a = dve.do(lambda e, q=q: e.tensor_tensor(q, q, rows["gq3"][:, :], ALU.mult), a)
                            s.tq.append(dve.do(lambda e, q=q: e.tensor_tensor(q, q, rows["bq3"][:, :], ALU.add), a))
                            k = s.kn.t[:, tt, :]
                            s.tk.append(dve.do(lambda e, tt=tt, k=k: e.tensor_scalar(k, k, mv[:, 4 + tt, 0:1], rs[:, 4 + tt:5 + tt],
                                                                                     ALU.subtract, ALU.mult), t))

                    def tr(cc):
                        def f():
                            QTt, KTt = s.qt.t
                            if cc == 0:
                                s.t_qt, s.t_kt = [], []
                            bank = bankA.next()
                            t = transposes([bank.t[:, tt * 128:tt * 128 + 128] for tt in range(4)],
                                           [s.qn.t[:, tt, cc * 128:cc * 128 + 128] for tt in range(4)], bank, s.tq)
                            a = act.do(lambda e, bank=bank: e.activation(QTt[:, cc, :], bank.t[:, :], ACT.Copy), t, s.qt.free)
                            bank.free = [a]
                            s.t_qt.append(a)
                            bank = bankA.next()
                            t = transposes([bank.t[:, tt * 128:tt * 128 + 128] for tt in range(4)],
                                           [s.kn.t[:, tt, cc * 128:cc * 128 + 128] for tt in range(4)], bank, s.tk)
                            a = act.do(lambda e, bank=bank: e.activation(KTt[:, cc, :], bank.t[:, :], ACT.Identity,
                                                                         bias=col["bkv3"][:, cc:cc + 1],
                                                                         scale=col["gkv3"][:, cc:cc + 1]), t, s.qt.free)
                            bank.free = [a]
                            s.t_kt.append(a)
                            s.kn.free = [t]
                        return f

                    def qk(w, k_, scr, parts):
                        hold = {}

                        def f():
                            src, ts = s.qt.t[k_], (s.t_kt if k_ else s.t_qt)
                            bank, Tn, Fn = bankA.next(), T.next(), F.next()
                            t = project(bank, 0, 512, [(w[:, c, it.h * 128:it.h * 128 + 128], src[:, c, :]) for c in range(2)], ts)
                            act.wait(Tn.free)
                            a0, a1_ = evacuate(bank.t[:, :], t, Tn.t[:, 0, :], Fn)
                            bank.free = [a1_]
                            hold["x"] = (Tn, Fn, a1_)

                        def g():
                            Tn, Fn, a = hold["x"]
                            tk = split3([Tn.t[:, i, :] for i in range(3)], Fn, a)
                            wr, ready = stack_rows(it.st.free, Tn.t, tk, scr.next(), parts)
                            Tn.free = wr
                            it.t_stack += ready
                        return [f, (g, 0.04)]

                    def vproj(tp):
                        def f():
                            bank = bankA.next()
                            for k in range(2):
                                tt = 2 * tp + k
                                t = project(bank, 128 * k, 128 * k + 128,
                                            [(s.qt.t[1][:, c, tt * 128:tt * 128 + 128], wv[:, c, it.h * 128:it.h * 128 + 128])
                                             for c in range(2)], s.t_kt)
                                bank.free = []
                            d = dve.do(lambda e: e.tensor_copy(
                                it.vv.t[:, 2 * tp:2 * tp + 2, :, 0:16],
                                bank.t[:, 0:256].rearrange("p (a h d) -> p a h d", a=2, d=16)), t, it.vv.free, it.vv.ready)
                            bank.free = [d]
                            it.t_V.append(d)
                            s.qt.free = [t]
                        return f

                    if it.h == 0:
                        steps += [load, kn, qn(0), qn(1), norm, tr(0), tr(1)]
                    steps += qk(wq, 0, scrq, q_parts(QS))
                    steps += qk(wk, 1, scrk, k_parts(KS))
                    steps += [vproj(0), vproj(1)]
                    it.V = lambda kt, h: it.vv.t[:, kt, h, :]
                    return steps

                def a2(it):
                    QS, KS = it.st.t
                    tk = []

                    def smax(h, qt):
                        def f():
                            bank = bankA.next()
                            t = pe.do(lambda e: e.matmul(bank.t[:, :], QS[0:97, h, qt * 128:qt * 128 + 128], KS[0:97, h, :],
                                                         start=True, stop=True), bank.free, it.t_stack, it.st.ready)
                            d = dve.do(lambda e: e.tensor_reduce(it.m.t[:, qt, h:h + 1], bank.t[:, :], AX.X, ALU.max), t, it.m.free)
                            bank.free = [d]
                            tk.append(d)
                        return f

                    def rows_():
                        it.t_rows = maxima_rows(it.m, [tk[-1]], 8, 4, SP, MT, QS)
                    return [smax(h, qt) for qt in range(4) for h in range(8)] + [rows_]

                def c(it):
                    QS, KS = it.st.t

                    def group_done(g, t):
                        s = it.s
                        if g == 0 and it.h == 0:
                            s.nc = NCR.next()
                            s.t_nc = []
                        if g == 0:
                            it.sums = sums.take()
                        E_ = E.next()
                        bv = it.bv
                        a = act.do(lambda e: e.activation(E_.t[:, :], bv.t[:, :], ACT.Copy), t, E_.free)
                        bv.free = [a]
                        fr = [sums.put(it.sums, (4 * g, 4 * g + 4, 0, 512), E_.t[16:113:32, :], a)]
                        for j in range(4):
                            p0 = 16 * (4 * g + j)
                            fr.append(sp.go(s.nc.t[p0:p0 + 16, it.h, :], E_.t[32 * j:32 * j + 16, :], a, s.nc.free))
                        E_.free = fr
                        s.t_nc += fr
                        if g == 1:
                            it.st.free = [t]
                            it.vv.free = [t]
                    it.group_done = group_done
                    return attend3(it)

                def attend3(it):
                    QS, KS = it.st.t
                    return attend(it, list(range(8)), 4, 512, 0.25, P,
                                  lambda h, kt: [(KS[0:100, h, kt * 128:kt * 128 + 128], QS[0:100, h, :])], False, 2)

                def p(it):
                    s = it.s

                    def inv():
                        sums.invert(it.sums)

                    def spread():
                        if it.h == 0:
                            s.t_rb = []
                            s.rbfree = RB.free
                        x = sums.spread(it.sums, RB.t[:, it.h, :], 0, 8, 16, s.rbfree)
                        it.sums.free = [x]
                        s.t_rb.append(x)
                    if it.h == 0:
                        return [inv, nop, nop, spread, nop, nop]

                    def f0():
                        t = pool.do(lambda e: e.tensor_tensor(s.nc.t[:, :, :], s.nc.t[:, :, :], RB.t[:, :, :], ALU.mult), s.t_nc, s.t_rb)
                        RB.free = [t]
                        s.t_at = [t]

                    def f1():
                        s.a = []
                        for tt in range(4):
                            bank = bankA.next()
                            t = project(bank, 0, 256, [(s.nc.t[:, c, tt * 128:tt * 128 + 128], wo[:, c, :]) for c in range(2)],
                                        s.t_at)
                            q = s.qn.t[:, tt, :]
                            a = dve.do(lambda e, q=q, bank=bank: e.tensor_tensor(q, bank.t[:, 0:256], q, ALU.add), t)
                            bank.free = [a]
                            a = dve.do(lambda e, tt=tt, q=q: e.bn_stats(st2[:, tt, :], q), a)
                            s.a.append(dve.do(lambda e, tt=tt: e.bn_aggr(mv2[:, tt, :], st2[:, tt, :]), a))
                        s.nc.free = [t]

                    def f2():
                        t = rstd_of(rs2[:, :], mv2[:, :, 1], 1e-5, 1.0, s.a)
                        s.th = []
                        for tt in range(4):
                            s.th.append(dve.do(lambda e, tt=tt: e.tensor_scalar(HH.t[:, tt, :], s.qn.t[:, tt, :], mv2[:, tt, 0:1],
                                                                                rs2[:, tt:tt + 1], ALU.subtract, ALU.mult),
                                               t, HH.free))

                    def f3(cc):
                        def f():
                            if cc == 0:
                                s.t_ht, s.t_rt = [], []
                            bank = bankA.next()
                            t = transposes([bank.t[:, tt * 128:tt * 128 + 128] for tt in range(4)],
                                           [HH.t[:, tt, cc * 128:cc * 128 + 128] for tt in range(4)], bank, s.th)
                            a = act.do(lambda e, bank=bank: e.activation(HTT.t[:, cc, :], bank.t[:, :], ACT.Identity,
                                                                         bias=col["bf3"][:, cc:cc + 1],
                                                                         scale=col["gf3"][:, cc:cc + 1]), t, HTT.free)
                            bank.free = [a]
                            HH.free = [t]
                            s.t_ht.append(a)
                            bank = bankA.next()
                            t = transposes([bank.t[:, tt * 128:tt * 128 + 128] for tt in range(4)],
                                           [s.qn.t[:, tt, cc * 128:cc * 128 + 128] for tt in range(4)], bank)
                            a = act.do(lambda e, bank=bank: e.activation(RT.t[:, cc, :], bank.t[:, :], ACT.Copy), t, RT.free)
                            bank.free = [a]
                            s.t_rt.append(a)
                            s.qn.free = [t]
                        return f

                    def f4(o):
                        def f():
                            if o == 0:
                                s.tg = []
                            bank = bankA.next()
                            t = project(bank, 0, 512, [(w1[:, c, o * 128:o * 128 + 128], HTT.t[:, c, :]) for c in range(2)], s.t_ht)
                            s.tg.append(dve.do(lambda e: e.tensor_scalar(G.t[:, o, :], bank.t[:, :], col["b13"][:, o:o + 1], None,
                                                                         ALU.add), t, G.free))
                            bank.free = [s.tg[-1]]
                            if o == 3:
                                HTT.free = [t]
                                s.tg = [act.do(lambda e: e.activation(G.t[:, :, :], G.t[:, :, :], ACT.Gelu), s.tg)]
                        return f

                    def f5():
                        last = []
                        for cc in range(2):
                            bank = bankA.next()
                            t = project(bank, 0, 512, [(w2[:, o, cc * 128:cc * 128 + 128], G.t[:, o, :]) for o in range(4)], s.tg)
                            d = dve.do(lambda e, cc=cc, bank=bank: e.scalar_tensor_tensor(
                                out=RT.t[:, cc, :], in0=bank.t[:, :], scalar=col["b23"][:, cc:cc + 1], in1=RT.t[:, cc, :],
                                op0=ALU.add, op1=ALU.add), t, s.t_rt)
                            bank.free = [d]
                            last.append(d)
                        G.free = [t]
                        RT.free = [sp.go(out[it.b].rearrange("(n p) t -> p n t", p=128), RT.t[:, :, :], last)]
                    return [inv, nop, nop, nop, spread, nop, nop, f0, f1, f2, f3(0), f3(1), f4(0), f4(1), f4(2), f4(3), f5]
                pipeline(items_of(), a1, a2, c, p)
                barrier()

        layer0()
        layer1a()
        layer1b()
        layer2()
        layer3()

        block = ctx.enter_context(nc.Block())

        @block.sync
        def _(e):
            sp.run(e)

        @block.gpsimd
        def _(e):
            pool.run(e)

        @block.scalar
        def _(e):
            act.run(e)

        @block.vector
        def _(e):
            dve.run(e)

        @block.tensor
        def _(e):
            pe.run(e)


def lay_out(i):
    a = {k: np.asarray(v) for k, v in i.items()}
    C = np.ascontiguousarray
    colv = lambda v: C(v.reshape(-1, 128).T)
    kvw = a["L1_xattn_kv_w"].reshape(512, 512, 2)
    kvb = a["L1_xattn_kv_b"].reshape(512, 2)
    cols = {"bq0": a["L0_xattn_bq"], "bk0": a["L0_xattn_bk"], "qb1": a["L1_xattn_q_b"], "kb1": kvb[:, 0],
            "pn1": a["L1_xattn_postnorm_w"], "mb1": a["L1_xattn_mlp_b1"], "bq2": a["L2_xattn_bq"], "bk2": a["L2_xattn_bk"],
            "gkv3": a["L3_xattn_ln_kv_g"], "bkv3": a["L3_xattn_ln_kv_b"], "gf3": a["L3_xattn_ffn_ln_g"],
            "bf3": a["L3_xattn_ffn_ln_b"], "b13": a["L3_xattn_b1"], "b23": a["L3_xattn_b2"]}
    rows = {"bv0": a["L0_xattn_bv"], "vb1": kvb[:, 1], "ob1": a["L1_xattn_out_b"], "mb2": a["L1_xattn_mlp_b2"],
            "bv2": a["L2_xattn_bv"], "bo2": a["L2_xattn_bo"], "g2": a["L2_xattn_gamma"], "be2": a["L2_xattn_beta"],
            "gq3": a["L3_xattn_ln_q_g"], "bq3": a["L3_xattn_ln_q_b"]}
    t = np.arange(512, dtype=np.float32)[:, None]
    div = np.exp(np.arange(0, 256, 2, dtype=np.float32) * np.float32(-np.log(10000.0) / 256))
    ang = (t * div).astype(np.float32)
    pos = np.zeros((512, 256), np.float32)
    pos[:, 0::2] = np.sin(ang)
    pos[:, 1::2] = np.cos(ang)
    mask0 = a["mask_Bx1x2048_bf1"]
    return {
        "x": a["x"], "ctx": a["ctx_2048"], "ctxT": C(a["ctx_2048"].transpose(0, 2, 1)),
        "mask0": C(mask0).view(np.uint8), "mask1": a["mask_BxS2_ik0"],
        "mask2": C(a["mask_Bx1xSxS2_ff0"][:, 0]), "mask2T": C(a["mask_Bx1xSxS2_ff0"][:, 0].transpose(0, 2, 1)),
        "cols": C(np.concatenate([colv(cols[n]) for n, _ in COLS], axis=1)),
        "rows": C(np.concatenate([rows[n] for n, _ in ROWS])[None, :]),
        "pos": pos,
        "WqT0": C(a["L0_xattn_Wq"].T), "WkT0": C(a["L0_xattn_Wk"].T), "WvT0": C(a["L0_xattn_Wv"].T),
        "q_w1": a["L1_xattn_q_w"], "k_w1": C(kvw[:, :, 0]), "v_w1": C(kvw[:, :, 1]), "out_w1": a["L1_xattn_out_w"],
        "mlp_w1": a["L1_xattn_mlp_w1"], "mlp_w2": a["L1_xattn_mlp_w2"],
        "Wq2": a["L2_xattn_Wq"], "Wk2": a["L2_xattn_Wk"], "Wv2": a["L2_xattn_Wv"], "Wo2": C(a["L2_xattn_Wo"].reshape(2, 2, 4, 2, 16, 512).transpose(0, 3, 1, 2, 4, 5).reshape(512, 512)),
        "Wq3": a["L3_xattn_Wq"], "Wk3": a["L3_xattn_Wk"], "Wv3": a["L3_xattn_Wv"], "Wo3": a["L3_xattn_Wo"],
        "W13": a["L3_xattn_W1"], "W23": a["L3_xattn_W2"],
    }


def kernel(**inputs):
    import concourse.bacc as _bacc
    from concourse.bass_utils import run_bass_kernel_spmd as _run

    nc = _bacc.Bacc("TRN2", target_bir_lowering=False, num_devices=1)
    arrays, aps = {}, {}
    for name, v in lay_out(inputs).items():
        arrays[f"in_{name}"] = v
        aps[name] = nc.dram_tensor(f"in_{name}", v.shape, mybir.dt.from_np(v.dtype), kind="ExternalInput").ap()
    out = nc.dram_tensor("out_0", [8, 256, 512], mybir.dt.float32, kind="ExternalOutput").ap()
    build_program(nc, aps, out)
    r = _run(nc, [arrays], core_ids=[0])
    return r.results[0]["out_0"]
```

```python
import numpy as np
import concourse.bass as bass
from concourse import mybir
from contextlib import ExitStack

COLS = [("bq0", 2), ("bk0", 2), ("qb1", 4), ("kb1", 4), ("pn1", 4), ("mb1", 16), ("bq2", 4), ("bk2", 1),
        ("gkv3", 2), ("bkv3", 2), ("gf3", 2), ("bf3", 2), ("b13", 4), ("b23", 2)]
ROWS = [("bv0", 256), ("vb1", 512), ("ob1", 512), ("mb2", 512), ("bv2", 128), ("bo2", 512), ("g2", 512), ("be2", 512),
        ("gq3", 256), ("bq3", 256)]
B, HALVES = 8, 2
NEG = 1e30


class Engine:

    def __init__(self, sem):
        self.ops, self.sem, self.n, self.seen = [], sem, 0, {}

    def wait(self, *tokens):
        for t in tokens:
            if t is None:
                continue
            if isinstance(t, list):
                self.wait(*t)
                continue
            sem, value = t
            if self.seen.get(id(sem), 0) < value:
                self.seen[id(sem)] = value
                self.ops.append(lambda e, s=sem, v=value: e.wait_ge(s, v))

    def do(self, f, *waits):
        self.wait(*waits)
        self.n += 1
        self.ops.append(lambda e: f(e).then_inc(self.sem, 1))
        return (self.sem, self.n)

    def quiet(self, f, *waits):
        self.wait(*waits)
        self.ops.append(f)

    def last(self):
        return (self.sem, self.n) if self.n else None

    def run(self, e):
        for f in self.ops:
            f(e)


class Dma(Engine):

    def __init__(self, sems, engine=None):
        super().__init__(None)
        self.sems, self.count, self.k = sems, [0] * len(sems), 0
        if engine:
            self.ops, self.seen = engine.ops, engine.seen

    def go(self, out, in_, *waits):
        i = self.k % len(self.sems)
        self.k += 1
        s = self.sems[i]
        if self.count[i]:
            self.wait((s, self.count[i]))
        self.wait(*waits)
        self.count[i] += 16
        self.ops.append(lambda e: e.dma_start(out, in_).then_inc(s, 16))
        return (s, self.count[i])

    def all(self):
        return [(s, c) for s, c in zip(self.sems, self.count) if c]


class Slot:

    def __init__(self, t):
        self.t, self.ready, self._free, self.taken = t, [], [], False

    @property
    def free(self):
        return self._free

    @free.setter
    def free(self, tokens):
        self._free, self.taken = tokens, False


class Ring:
    def __init__(self, slots):
        self.slots, self.k = slots, 0

    def next(self):
        s = self.slots[self.k % len(self.slots)]
        self.k += 1
        assert not s.taken, "the slot's last reader isn't queued yet"
        s.taken = True
        return s


def merge(*lists):
    placed = []
    for n, (steps, start, end) in enumerate(lists):
        for i, f in enumerate(steps):
            f, delay = f if isinstance(f, tuple) else (f, 0.0)
            placed.append((start + (end - start) * (i + 0.5) / len(steps) + delay, n, i, f))
    for _, _, _, f in sorted(placed, key=lambda x: x[:3]):
        f()


def build_program(nc, I, out, batches=B):
    fp32, bf16, u8, i32 = mybir.dt.float32, mybir.dt.bfloat16, mybir.dt.uint8, mybir.dt.int32
    ALU, ACT, AX = mybir.AluOpType, mybir.ActivationFunctionType, mybir.AxisListType
    ctx = ExitStack()
    with ctx:
        sem = lambda n: ctx.enter_context(nc.semaphore(n))
        pe, act, dve, pool = Engine(sem("s_pe")), Engine(sem("s_act")), Engine(sem("s_dve")), Engine(sem("s_pool"))
        sp = Dma([sem(f"s_dma{i}") for i in range(48)])
        pq = Dma([sem(f"s_pdma{i}") for i in range(16)], pool)
        aq = Dma([sem(f"s_adma{i}") for i in range(16)], act)
        PS = ctx.enter_context(nc.psum_tensor("PS", [128, 8, 512], fp32))
        bankA = Ring([Slot(PS[:, i, :]) for i in (0, 1, 2)])
        bankC = Ring([Slot(PS[:, i, :]) for i in (3, 4, 5)])
        bankV, bankS = Slot(PS[:, 6, :]), Slot(PS[:, 7, :])
        bankVV = Ring([bankV, bankS])

        x1 = nc.dram_tensor("x1_scratch", [B, 256, 512], fp32, kind="Internal").ap()
        y1 = nc.dram_tensor("y1_scratch", [B, 256, 512], fp32, kind="Internal").ap()
        x2 = nc.dram_tensor("x2_scratch", [B, 256, 512], fp32, kind="Internal").ap()
        x3 = nc.dram_tensor("x3_scratch", [B, 256, 512], fp32, kind="Internal").ap()
        NSCR = 4
        scrq = Ring([Slot(nc.dram_tensor(f"q_scratch{i}", [128 * 3 * 512], bf16, kind="Internal").ap()) for i in range(NSCR)])
        scrk = Ring([Slot(nc.dram_tensor(f"k_scratch{i}", [128 * 3 * 1024], bf16, kind="Internal").ap()) for i in range(NSCR)])

        sb_of = lambda c, layer="": (lambda n, shape, dt=fp32: c.enter_context(nc.sbuf_tensor(layer + n, shape, dt)))
        sbg = sb_of(ctx)
        cols = sbg("cols", [128, sum(n for _, n in COLS)])
        col, at = {}, 0
        for n, w in COLS:
            col[n] = cols[:, at:at + w]
            at += w
        row_at, at = {}, 0
        for n, w in ROWS:
            row_at[n] = (at, w)
            at += w
        ident = sbg("ident", [128, 128])
        identb = sbg("identb", [128, 128], bf16)
        onerow = sbg("onerow", [4, 512], bf16)
        zrow = sbg("zrow", [1, 512], bf16)
        ones = sbg("ones", [128, 32])
        t_cols = sp.go(cols[:, :], I["cols"])
        t_id0 = pool.do(lambda e: e.memset(ident[:, :], 0.0))
        t_id = pool.do(lambda e: e.affine_select(out=ident[:, :], in_=ident[:, :], compare_op=ALU.not_equal, fill=1.0,
                                                 base=0, pattern=[[-1, 128]], channel_multiplier=1), t_id0)
        t_ones = pool.do(lambda e: e.memset(ones[:, :], 1.0))
        t_idb = pool.do(lambda e: e.tensor_copy(identb[:, :], ident[:, :]), t_id)
        t_1r = pool.do(lambda e: e.memset(onerow[:, :], 1.0))
        t_0r = pool.do(lambda e: e.memset(zrow[:, :], 0.0))
        for e in (act, dve):
            e.wait(t_cols)
        pe.wait(t_id, t_ones, t_idb)

        def set_rows(t, nh, w, key):
            r = [sp.go(t[96:100, :, :], onerow[:, None, 0:w].broadcast_to([4, nh, w]), t_1r)]
            if key:
                r = [sp.go(t[96:97, :, :], zrow[:, None, 0:w].broadcast_to([1, nh, w]), t_0r, r)]
            return r

        transfers = lambda: sp.all() + pq.all() + aq.all()

        def barrier(moved=None):
            tokens = [x.last() for x in (pe, act, dve, pool)] + (transfers() if moved is None else moved)
            for x in (pe, act, dve, pool, sp):
                x.wait(*tokens)

        def load_rows(sb, names):
            r = {}
            for n in names:
                a, w = row_at[n]
                t = sb("row_" + n, [128, w])
                r[n] = t
                dve.wait(sp.go(t[:, :], I["rows"][0:1, a:a + w].broadcast_to([128, w])))
            return r

        loaded = {}

        def load_w(sb, name, k, n, chunk=None):
            t = sb("w_" + name, [128, k, n])
            loaded[name] = []
            for c in range(0, n, chunk or n):
                x = slice(c, c + (chunk or n))
                loaded[name].append(aq.go(t[:, :, x], I[name].rearrange("(k p) n -> p k n", p=128)[:, :, x]))
            return t

        def project(bank, lo, hi, pairs, *waits):
            pe.wait(bank.free, *waits)
            for i, (l, r) in enumerate(pairs[:-1]):
                pe.quiet(lambda e, l=l, r=r, i=i: e.matmul(bank.t[:, lo:hi], l, r, start=(i == 0), stop=False,
                                                           skip_group_check=True))
            l, r = pairs[-1]
            return pe.do(lambda e: e.matmul(bank.t[:, lo:hi], l, r, start=(len(pairs) == 1), stop=True,
                                            skip_group_check=True))

        def evacuate(src, t_src, T0, F, bias=None, whole=False):
            b = 0.0 if bias is None else bias
            a0 = act.do(lambda e: e.activation(T0, src, ACT.Identity, bias=b), t_src)
            if whole:
                return [act.do(lambda e: e.activation(F.t, src, ACT.Identity, bias=b), F.free)]
            if bias is None:
                return [dve.do(lambda e: e.tensor_tensor(F.t, src, T0, ALU.subtract), a0, F.free)]
            return [dve.do(lambda e: e.scalar_tensor_tensor(out=F.t, in0=src, scalar=bias, in1=T0, op0=ALU.add,
                                                            op1=ALU.subtract), a0, F.free)]

        def split3(T, F, t_F, whole=False):
            f = F.t
            d0 = dve.do(lambda e: e.tensor_tensor(f, f, T[0], ALU.subtract), t_F) if whole else t_F
            d1 = dve.do(lambda e: e.tensor_copy(T[1], f), d0)
            d2 = pool.do(lambda e: e.tensor_tensor(T[2], f, T[1], ALU.subtract), d1)
            F.free = [d2]
            return [t_F, d1, d2]

        def stack(dst, free, T, t_T, scr, parts, nt, d, cols_):
            view = scr.t[0:128 * 3 * nt * cols_].rearrange("(i n p q) -> i n p q", i=3, n=nt, p=128)
            w = sp.go(view.rearrange("i n p q -> p i n q"), T, t_T, scr.free)
            ready = []
            for rows, i in parts:
                ready.append(sp.go(rows, view[i].rearrange("n (h d) q -> d (n h) q", d=d), w, free))
            scr.free = ready
            return w, ready

        def stack_rows(free, T, t_T, scr, parts):
            view = scr.t[0:128 * 3 * 512].rearrange("(i d h q) -> i d h q", i=3, d=16, h=8)
            w = [sp.go(view[i].rearrange("d h q -> h d q"), T[:, i, :], t_T[i], scr.free) for i in range(3)]
            ready = []
            for rows, i, n, same in parts:
                src = view[i:i + 1].broadcast_to([n, 16, 8, 512]) if same else view[i:i + n].rearrange("i d h q -> (i d) h q")
                ready.append(sp.go(rows, src, w, free))
            scr.free = ready
            return w, ready

        def transposes(dsts, srcs, bank, *waits):
            pe.wait(bank.free, *waits)
            for d, s in list(zip(dsts, srcs))[:-1]:
                pe.quiet(lambda e, d=d, s=s: e.transpose(d, s, ident[0:s.shape[0], 0:s.shape[0]]))
            return pe.do(lambda e: e.transpose(dsts[-1], srcs[-1], ident[0:srcs[-1].shape[0], 0:srcs[-1].shape[0]]))

        def maxima_rows(M, t_M, nh, nqt, SP, MT, Q):
            w = nqt * 128
            m, (s3, r) = M.t, SP.t
            m3 = s3[:, :, :].rearrange("p q (i h) -> p i q h", i=3)
            a = dve.do(lambda e: e.tensor_scalar(m3[:, 0], m[:, :, :], -1.0, None, ALU.mult), t_M, SP.free)
            b_ = dve.do(lambda e: e.scalar_tensor_tensor(out=r[:, :, :], in0=m[:, :, :], scalar=-1.0, in1=m3[:, 0], op0=ALU.mult,
                                                         op1=ALU.subtract), a)
            c_ = dve.do(lambda e: e.tensor_copy(m3[:, 1], r[:, :, :]), b_)
            d_ = dve.do(lambda e: e.tensor_tensor(m3[:, 2], r[:, :, :], m3[:, 1], ALU.subtract), c_)
            M.free = [b_]

            def turn():
                bank = bankA.next()
                pe.wait(bank.free, d_)
                for q in range(nqt):
                    f = lambda e, q=q: e.matmul(bank.t[0:3 * nh, q * 128:(q + 1) * 128], s3[:, q, :], identb[:, :], start=True,
                                                stop=True, skip_group_check=True)
                    if q == nqt - 1:
                        t = pe.do(f)
                    else:
                        pe.quiet(f)
                SP.free = [t]
                v = act.do(lambda e: e.activation(MT.t[0:3 * nh, 0:w], bank.t[0:3 * nh, 0:w], ACT.Copy), t, MT.free)
                bank.free = [v]
                rr = [aq.go(Q[97 + i:98 + i, :, :], MT.t[nh * i:nh * i + nh, 0:w], v) for i in range(3)]
                MT.free = rr
                return rr
            return turn

        class Sums:

            def __init__(self, sb, name, rows_, w, n):
                self.dram = Ring([Slot((nc.dram_tensor(f"{name}_sums{i}", [rows_, w], fp32, kind="Internal").ap(),
                                        nc.dram_tensor(f"{name}_recs{i}", [rows_, w], fp32, kind="Internal").ap()))
                                  for i in range(n)])
                self.small = Ring([Slot(sb(f"{name}r{i}", [128, rows_ * w // 128])) for i in range(2)])
                self.w = w

            def take(self):
                d = self.dram.next()
                d.tokens = []
                return d

            def put(self, d, at, src, t):
                x = sp.go(d.t[0][at[0]:at[1], at[2]:at[3]], src, t, d.free)
                d.tokens.append(x)
                return x

            def dense(self, x):
                return x.rearrange("a b -> (a b)").rearrange("(p f) -> p f", p=128)

            def fetch(self, d):
                d.s = self.small.next()
                d.fetched = sp.go(d.s.t[:, :], self.dense(d.t[0]), d.tokens, d.s.free)

            def invert(self, d):
                s = d.s
                b_ = dve.do(lambda e: e.reciprocal(s.t[:, :], s.t[:, :]), d.fetched)
                c_ = sp.go(self.dense(d.t[1]), s.t[:, :], b_)
                s.free = [c_]
                d.tokens = [c_]

            def spread(self, d, dst, lo, hi, rep, free):
                x = sp.go(dst, d.t[1][lo:hi, None, :].broadcast_to([hi - lo, rep, self.w]), d.tokens, free)
                return x

        magic_ = {n: sbg("magic_" + n, [128, 3, 8]) for n in ("in", "out")}

        def rstd_steps(magic, ms, var, eps, scale, waits, done):
            n = ms.shape[1]
            x, y, z = (magic[:, i, 0:n] for i in range(3))
            hold = {}

            def guess():
                t = dve.do(lambda e: e.tensor_scalar(x, var, scale, eps, ALU.mult, ALU.add), waits(), dve.last())
                t = dve.do(lambda e: e.tensor_scalar(z.bitcast(i32), x.bitcast(i32), 1, None, ALU.arith_shift_right), t)
                hold["t"] = dve.do(lambda e: e.tensor_scalar(y.bitcast(i32), z.bitcast(i32), -1.0, float(0x5f3759df), ALU.mult,
                                                             ALU.add), t)

            def newton(k):
                def f():
                    t = dve.do(lambda e: e.tensor_tensor(z, y, y, ALU.mult), hold["t"])
                    t = dve.do(lambda e: e.tensor_tensor(z, z, x, ALU.mult), t)
                    t = dve.do(lambda e: e.tensor_scalar(z, z, -0.5, 1.5, ALU.mult, ALU.add), t)
                    hold["t"] = dve.do(lambda e, o=ms if k == 2 else y: e.tensor_tensor(o, y, z, ALU.mult), t)
                    if k == 2:
                        done(hold["t"])
                return f
            return [guess, newton(0), newton(1), newton(2)]

        class Item:
            pass

        def nop():
            pass

        tail = []

        def pipeline(items, a0, a1, a2, c, p, spans=((0.0, 0.9), (0.0, 0.8), (0.05, 0.8), (0.0, 1.0), (0.0, 1.0)),
                     keep=False, begin=nop):
            n = len(items)
            stages = (a0, a1, a2, c, p)
            first = 0 if a0 else 1
            for i in range(first, n + 4):
                lists = []
                for s, (f, span) in enumerate(zip(stages, spans)):
                    k = i - s
                    if f is None:
                        continue
                    if 0 <= k < n:
                        steps = f(items[k])
                        if steps:
                            lists.append((steps, *span))
                if i == n + 3 and keep:
                    tail.append(lists[0])
                    barrier(moved)
                    return
                if i == n + 2:
                    moved = transfers()
                if i == first and tail:
                    lists.append((tail.pop()[0], 0.0, 0.8))
                    merge(*lists)
                    barrier()
                    begin()
                else:
                    merge(*lists)
            barrier()

        def items_of():
            out_ = []
            for b in range(batches):
                shared = Item()
                for h in range(HALVES):
                    it = Item()
                    it.b, it.h, it.s = b, h, shared
                    out_.append(it)
            return out_

        def attend(it, heads, nkt, w, scale, Pring, lhs, vones, spread=4, bankS=bankS):
            steps = []
            pend = []

            def scores(h):
                def f():
                    P = Pring.next()
                    P.ready = []
                    per = 512 // w
                    for c0 in range(0, nkt, per):
                        bank = bankC.next()
                        pe.wait(bank.free, it.t_rows, it.st.ready, it.t_stack)
                        for i in range(per):
                            mm = lhs(h, c0 + i)
                            for m, (l, r) in enumerate(mm):
                                o = bank.t[:, i * w:(i + 1) * w]
                                g = lambda e, o=o, l=l, r=r, m=m, k=len(mm): e.matmul(
                                    o, l, r, start=(m == 0), stop=(m == k - 1), skip_group_check=True)
                                if i == per - 1 and m == len(mm) - 1:
                                    t = pe.do(g)
                                else:
                                    pe.quiet(g)
                        po = P.t[:, c0 * w:(c0 + per) * w]
                        a = act.do(lambda e, po=po, bank=bank: e.activation(po, bank.t, ACT.Exp, scale=scale), t, P.free)
                        bank.free = [a]
                        P.ready.append(a)
                    pend.append((h, P))
                return f

            def values(g, kt):
                def f():
                    four = pend[4 * g:4 * g + 4]
                    if kt == 0:
                        it.bv = bankV if vones else bankVV.next()
                        pe.wait(it.bv.free)
                    bv = it.bv
                    pe.wait(*[P.ready for _, P in four], it.t_V)
                    if vones:
                        pe.wait(bankS.free if kt == 0 else None)
                    for j, (h, P) in enumerate(four):
                        l = it.V(kt, h)
                        o = bv.t[32 * j:32 * j + l.shape[1], 0:w]
                        r = P.t[:, kt * w:(kt + 1) * w]
                        pe.quiet(lambda e, o=o, r=r, l=l, j=j: e.matmul(
                            o, l, r, start=(kt == 0), stop=(kt == nkt - 1), tile_position=(0, 32 * j), skip_group_check=True))
                    if vones:
                        for j, (h, P) in enumerate(four):
                            o = bankS.t[32 * j:32 * j + 32, 0:w]
                            r = P.t[:, kt * w:(kt + 1) * w]
                            pe.quiet(lambda e, o=o, r=r, j=j: e.matmul(
                                o, ones[:, :], r, start=(kt == 0), stop=(kt == nkt - 1), tile_position=(0, 32 * j),
                                skip_group_check=True))
                    f_last = pe.ops.pop()
                    t = pe.do(f_last)
                    if kt == nkt - 1:
                        for _, P in four:
                            P.free = [t]
                        it.group_done(g, t)
                return f

            ng = len(heads) // 4
            for i, h in enumerate(heads):
                steps.append(scores(h))
                if i >= 4 and (i - 4) % 4 < spread:
                    for kt in range((i - 4) % 4 * nkt // spread, ((i - 4) % 4 + 1) * nkt // spread):
                        steps.append(values((i - 4) // 4, kt))
            for kt in range(nkt):
                steps.append(values(ng - 1, kt))
            return steps

        q_parts = lambda Q: [(Q[0:48, :, :], 0, 3, False), (Q[48:80, :, :], 0, 2, False), (Q[80:96, :, :], 0, 1, False)]
        k_parts = lambda K: [(K[0:48, :, :], 0, 3, True), (K[48:80, :, :], 1, 2, True), (K[80:96, :, :], 2, 1, False)]

        def mask_row(dst, msk, t_m, ne, nh, free):
            return sp.go(dst, msk[0:1, None, 0:ne].broadcast_to([1, nh, ne]), t_m, free)

        def layer0():
            with ExitStack() as lc:
                sb = sb_of(lc, "l0_")
                rows = load_rows(sb, ["bv0"])
                wq, wk, wv = (load_w(sb, n, 2, 256) for n in ("WqT0", "WkT0", "WvT0"))
                C = Ring([Slot(sb(f"C{i}", [128, 2, 512])) for i in range(2)])
                MK8 = Ring([Slot(sb(f"MK8{i}", [128, 512], u8)) for i in range(3)])
                MB = Ring([Slot(sb(f"MB{i}", [1, 512], bf16)) for i in range(2)])
                ST = Ring([Slot((sb(f"QS{i}", [128, 8, 512], bf16), sb(f"KS{i}", [128, 8, 512], bf16))) for i in range(3)])
                T = Ring([Slot(sb(f"T{i}", [128, 3, 512], bf16)) for i in range(2)])
                F = Ring([Slot(sb(f"F{i}", [128, 512])[:, :]) for i in range(2)])
                VV = Ring([Slot(sb(f"V{i}", [128, 4, 8, 32])) for i in range(3)])
                M = Ring([Slot(sb(f"M{i}", [128, 4, 8])) for i in range(2)])
                SP = Slot((sb("M3", [128, 4, 24], bf16), sb("Mr", [128, 4, 8])))
                MT = Slot(sb("MT", [24, 512], bf16))
                P = Ring([Slot(sb(f"P{i}", [128, 2048])) for i in range(8)])
                X = Ring([Slot(sb(f"X{i}", [128, 2, 512])) for i in range(3)])
                MK = Ring([Slot(sb(f"MK{i}", [128, 512])) for i in range(3)])
                SS = Slot(sb("SS", [128, 512]))
                E = Ring([Slot(sb(f"E{i}", [128, 512])) for i in range(2)])
                RB = Slot(sb("RB", [128, 2, 512]))
                ME = Ring([Slot((sb(f"ME{i}", [128, 2, 512]), sb(f"EX{i}", [128, 2, 512]))) for i in range(2)])
                OUT = Slot(sb("OUT", [128, 2, 512]))
                sm = sb("sm", [128, 16])
                sums = Sums(sb, "l0", 8, 512, 4)
                for s in ST.slots:
                    s.ready = [set_rows(t, 8, 512, False) for t in s.t]

                def a1(it):
                    s = it.s
                    it.st, it.vv, it.m = ST.next(), VV.next(), M.next()
                    QS, KS = it.st.t
                    steps = []

                    def load():
                        s.X, s.C, s.mk8, s.mk, s.mb = X.next(), C.next(), MK8.next(), MK.next(), MB.next()
                        s.tX = pq.go(s.X.t[:, :, :], I["x"][it.b].rearrange("(n p) t -> p n t", p=128), s.X.free)
                        s.tC = pq.go(s.C.t[:, :, :], I["ctx"][it.b].rearrange("(n p) t -> p n t", p=128), s.C.free)
                        t8 = pq.go(s.mk8.t[:, :], I["mask0"][it.b].broadcast_to([128, 512]), s.mk8.free)
                        s.tmk = dve.do(lambda e: e.tensor_copy(s.mk.t[:, :], s.mk8.t[:, :]), t8, s.mk.free)
                        s.tmb = dve.do(lambda e: e.tensor_scalar(s.mb.t[:, :], s.mk.t[0:1, :], -1.0, NEG, ALU.add, ALU.mult),
                                       s.tmk, s.mb.free)
                        s.mk8.free = [s.tmk]
                        s.mb.free = []

                    def qk(w, wn, src, tsrc, bias, scr, parts):
                        hold = {}

                        def f():
                            bank, Tn, Fn = bankA.next(), T.next(), F.next()
                            t = project(bank, 0, 512, [(w[:, c, it.h * 128:it.h * 128 + 128], src()[:, c, :]) for c in range(2)],
                                        tsrc(), loaded[wn])
                            act.wait(Tn.free)
                            a1_ = evacuate(bank.t[:, :], t, Tn.t[:, 0, :], Fn, bias[:, it.h:it.h + 1])
                            bank.free = a1_
                            hold["x"] = (Tn, Fn, a1_)

                        def g():
                            Tn, Fn, a = hold["x"]
                            tk = split3([Tn.t[:, i, :] for i in range(3)], Fn, a)
                            wr, ready = stack_rows(it.st.free, Tn.t, tk, scr.next(), parts)
                            Tn.free = wr
                            it.t_stack += ready
                        return [f, (g, 0.04)]

                    def vproj(tp):
                        def f():
                            bank = bankA.next()
                            for k in range(2):
                                tt = 2 * tp + k
                                t = project(bank, 128 * k, 128 * k + 128,
                                            [(s.C.t[:, c, tt * 128:tt * 128 + 128], wv[:, c, it.h * 128:it.h * 128 + 128])
                                             for c in range(2)], s.tC, loaded["WvT0"])
                                bank.free = []
                            Vt = it.vv.t
                            br = rows["bv0"][:, it.h * 128:it.h * 128 + 128].rearrange("p (h d) -> p h d", d=16)
                            dv = []
                            for k in range(2):
                                src = bank.t[:, 128 * k:128 * k + 128].rearrange("p (h d) -> p h d", d=16)
                                dv.append(dve.do(lambda e, k=k, src=src: e.tensor_tensor(
                                    Vt[:, 2 * tp + k, :, 0:16], src, br, ALU.add), t, it.vv.free))
                            bank.free = dv
                            it.t_V += dv
                            for k in range(2):
                                v = Vt[:, 2 * tp + k, :, 0:16]
                                it.t_V.append(pool.do(lambda e, k=k, v=v: e.tensor_tensor(
                                    Vt[:, 2 * tp + k, :, 16:32], v, v, ALU.mult), dv[k], it.vv.free))
                            s.C.free = [t]
                        return f

                    def mrow():
                        it.t_stack.append(mask_row(KS[96:97, :, :], s.mb.t, s.tmb, 512, 8, [it.st.free, it.st.ready]))
                        s.mb.free = s.mb.free + [it.t_stack[-1]]

                    it.t_stack, it.t_V = [], []
                    if it.h == 0:
                        steps.append(load)
                    steps += qk(wq, "WqT0", lambda: s.X.t, lambda: s.tX, col["bq0"], scrq, q_parts(QS))
                    steps += qk(wk, "WkT0", lambda: s.C.t, lambda: s.tC, col["bk0"], scrk, k_parts(KS))
                    steps.append(mrow)
                    steps += [vproj(0), vproj(1)]
                    it.V = lambda kt, h: it.vv.t[:, kt, h, :]
                    return steps

                def a2(it):
                    QS, KS = it.st.t
                    steps = []
                    tk = []

                    def smax(h, qt):
                        def f():
                            bank = bankA.next()
                            t = pe.do(lambda e: e.matmul(bank.t[:, :], QS[0:97, h, qt * 128:qt * 128 + 128], KS[0:97, h, :],
                                                         start=True, stop=True), bank.free, it.t_stack, it.st.ready)
                            d = dve.do(lambda e: e.tensor_reduce(it.m.t[:, qt, h:h + 1], bank.t[:, :], AX.X, ALU.max), t, it.m.free)
                            bank.free = [d]
                            tk.append(d)
                            it.last_s = t
                        return f
                    for qt in range(4):
                        for h in range(8):
                            steps.append(smax(h, qt))

                    def rows_():
                        it.turn = maxima_rows(it.m, [tk[-1]], 8, 4, SP, MT, QS)

                    def turn():
                        it.t_rows = it.turn()
                    return steps + [rows_, (turn, 0.03)]

                def c(it):
                    QS, KS = it.st.t

                    def group_done(g, t):
                        if g == 0 and it.h == 0:
                            it.s.me = ME.next()
                            it.s.t_me = []
                        E_ = E.next()
                        me, ex = it.s.me.t
                        if g == 0:
                            it.sums = sums.take()
                        d = act.do(lambda e: e.activation(SS.t[:, :], bankS.t[:, :], ACT.Copy), t, SS.free)
                        d2 = act.do(lambda e: e.activation(E_.t[:, :], bankV.t[:, :], ACT.Copy), t, E_.free)
                        bankS.free, bankV.free = [d], [d2]
                        SS.free = [sums.put(it.sums, (4 * g, 4 * g + 4, 0, 512), SS.t[0:97:32, :], d)]
                        fr = []
                        for j in range(4):
                            for k, dst in enumerate((me, ex)):
                                p0 = 16 * (4 * g + j)
                                fr.append(sp.go(dst[p0:p0 + 16, it.h, :], E_.t[32 * j + 16 * k:32 * j + 16 * k + 16, :],
                                                d2, it.s.me.free))
                        E_.free = fr
                        it.s.t_me += fr
                        if g == 1:
                            it.st.free = [t]
                            it.vv.free = [t]
                    it.group_done = group_done
                    return attend(it, list(range(8)), 4, 512, 0.25, P,
                                  lambda h, kt: [(KS[0:100, h, kt * 128:kt * 128 + 128], QS[0:100, h, :])], True)

                def p(it):
                    s = it.s

                    def fet():
                        sums.fetch(it.sums)

                    def inv():
                        sums.invert(it.sums)

                    def spread():
                        if it.h == 0:
                            s.t_rb = []
                            s.rbfree = RB.free
                        x = sums.spread(it.sums, RB.t[:, it.h, :], 0, 8, 16, s.rbfree)
                        it.sums.free = [x]
                        s.t_rb.append(x)
                    if it.h == 0:
                        return [nop, fet, nop, nop, inv, nop, nop, spread, nop, nop]
                    me, ex = s.me.t
                    Xt, mk = s.X.t, s.mk.t
                    o = OUT.t

                    def f1(n):
                        def f():
                            a = dve.do(lambda e: e.tensor_tensor_reduce(
                                out=Xt[:, n, :], in0=Xt[:, n, :], in1=mk[:, :], scale=1.0, scalar=0.0, op0=ALU.mult,
                                op1=ALU.add, accum_out=sm[:, n:n + 1]), s.tX, s.tmk, dve.last(), act.last(), pool.last(), s.xread)
                            b_ = act.do(lambda e: e.activation(o[:, n, :], Xt[:, n, :], ACT.Square,
                                                               accum_out=sm[:, 2 + n:3 + n]), a, OUT.free, act.last())
                            s.d = [b_] if n == 0 else s.d + [b_]
                            if n == 1:
                                s.n = dve.do(lambda e: e.tensor_reduce(sm[:, 4:5], mk[:, :], AX.X, ALU.add))
                        return f

                    def f2():
                        t = dve.do(lambda e: e.reciprocal(sm[:, 5:6], sm[:, 4:5]), s.n)
                        t = dve.do(lambda e: e.tensor_scalar(sm[:, 6:10], sm[:, 0:4], sm[:, 5:6], None, ALU.mult), t, s.d)
                        t1 = dve.do(lambda e: e.tensor_tensor(sm[:, 10:12], sm[:, 6:8], sm[:, 6:8], ALU.mult), t)
                        t2 = dve.do(lambda e: e.tensor_tensor(sm[:, 12:14], sm[:, 8:10], sm[:, 10:12], ALU.subtract), t1)
                        s.t3 = dve.do(lambda e: e.tensor_scalar(sm[:, 12:14], sm[:, 12:14], 0.0, 1e-5, ALU.max, ALU.add), t2)

                    def f3(n):
                        def f():
                            if n == 0:
                                s.te, s.tm, s.t4, s.rf = {}, {}, {}, []
                            m, x, y = me[:, n, :], ex[:, n, :], o[:, n, :]
                            s.tm[n] = dve.do(lambda e: e.tensor_tensor(m, m, RB.t[:, n, :], ALU.mult), s.t_me, s.t_rb)
                            t2 = pool.do(lambda e: e.tensor_tensor(x, x, RB.t[:, n, :], ALU.mult), s.t_me, s.t_rb)
                            s.rf += [s.tm[n], t2]
                            if n == 1:
                                RB.free = s.rf
                            t = dve.do(lambda e: e.tensor_tensor(y, m, m, ALU.mult), s.tm[n], s.d)
                            s.te[n] = [t, t2]
                        return f

                    def f3b(n):
                        def f():
                            x, y = ex[:, n, :], o[:, n, :]
                            t = dve.do(lambda e: e.tensor_tensor(x, x, y, ALU.subtract), s.te[n])
                            s.te[n] = dve.do(lambda e: e.tensor_scalar(x, x, 0.0, None, ALU.max), t)
                            if n == 1:
                                s.t4 = act.do(lambda e: e.activation(ex[:, :, :], ex[:, :, :], ACT.Sqrt), list(s.te.values()))
                                s.t5 = act.do(lambda e: e.activation(sm[:, 14:16], sm[:, 12:14], ACT.Sqrt), s.t3)
                        return f

                    def f4(n):
                        def f():
                            if n == 1:
                                s.t6 = dve.do(lambda e: e.reciprocal(sm[:, 12:14], sm[:, 14:16]), s.t5)
                                s.last = {}
                            x = Xt[:, n, :]
                            q = pool if n else dve
                            a = dve.do(lambda e: e.tensor_scalar(x, x, sm[:, 6 + n:7 + n], sm[:, 12 + n:13 + n], ALU.subtract,
                                                                 ALU.mult), s.t6)
                            a = q.do(lambda e: e.tensor_tensor(x, x, mk[:, :], ALU.mult), a)
                            a = q.do(lambda e: e.tensor_tensor(x, x, ex[:, n, :], ALU.mult), a, s.t4)
                            s.last[n] = a
                        return f

                    def f5(n):
                        def f():
                            x = Xt[:, n, :]
                            q = pool if n else dve
                            a = q.do(lambda e: e.tensor_tensor(x, x, me[:, n, :], ALU.add), s.last[n], s.tm[n])
                            s.last[n] = q.do(lambda e: e.tensor_tensor(o[:, n, :], x, mk[:, :], ALU.mult), a)
                            if n == 0:
                                last = list(s.last.values())
                                s.X.free = s.mk.free = s.me.free = last
                                OUT.free = [sp.go(x1[it.b].rearrange("(n p) t -> p n t", p=128), o[:, :, :], last)]
                        return f
                    s.xread = it.t_xread
                    return [nop, fet, f1(0), nop, f1(1), inv, nop, f2, spread, nop, nop, f3(0), f3(1), nop, f3b(0), f3b(1), nop, nop, f4(1), f4(0), nop, f5(1), f5(0)]

                its = items_of()

                def a2w(it):
                    return a2(it)

                def cw(it):
                    it.t_xread = it.t_stack
                    return c(it)
                pipeline(its, None, a1, a2w, cw, p, keep=True)

        def layer1a():
            with ExitStack() as lc:
                sb = sb_of(lc, "l1a_")
                bankT = Slot(PS[:, 6, 256:512])
                bankA.slots.append(bankS)
                rows = load_rows(sb, ["vb1", "ob1"])
                wk = load_w(sb, "k_w1", 4, 512)
                wq = load_w(sb, "q_w1", 4, 512)
                wv = load_w(sb, "v_w1", 4, 512)
                wo = load_w(sb, "out_w1", 4, 512)
                LAT = Ring([Slot(sb(f"LAT{i}", [128, 2, 512])) for i in range(3)])
                HT = Ring([Slot(sb(f"HT{i}", [128, 4, 512])) for i in range(1)])
                MI = Ring([Slot(sb(f"MI{i}", [1, 256], i32)) for i in range(1)])
                MF = Ring([Slot(sb(f"MF{i}", [1, 256])) for i in range(1)])
                MB = Ring([Slot(sb(f"MB{i}", [1, 512], bf16)) for i in range(2)])
                ST = Ring([Slot((sb(f"QA{i}", [128, 8, 256], bf16), sb(f"QB{i}", [96, 8, 256], bf16),
                                 sb(f"KA{i}", [128, 8, 512], bf16), sb(f"KB{i}", [96, 8, 512], bf16))) for i in range(3)])
                TQ = Ring([Slot(sb(f"TQ{i}", [128, 3, 2, 256], bf16)) for i in range(1)])
                TK = Ring([Slot(sb(f"TK{i}", [128, 3, 2, 512], bf16)) for i in range(1)])
                F = Ring([Slot(sb(f"F{i}", [128, 512])) for i in range(2)])
                VV = Ring([Slot(sb(f"V{i}", [128, 4, 256])) for i in range(3)])
                M = Ring([Slot(sb(f"M{i}", [128, 2, 8])) for i in range(2)])
                SP = Slot((sb("M3", [128, 2, 24], bf16), sb("Mr", [128, 2, 8])))
                MT = Slot(sb("MT", [24, 256], bf16))
                P = Ring([Slot(sb(f"P{i}", [128, 1024])) for i in range(8)])
                RB = Slot(sb("RB", [128, 4, 256]))
                sums = Sums(sb, "l1", 8, 256, 4)
                SS = Slot(sb("SS", [128, 256]))
                AT = Ring([Slot(sb(f"AT{i}", [128, 4, 256])) for i in range(2)])
                sm = sb("sm", [128, 4])
                for s in ST.slots:
                    s.ready = [set_rows(s.t[0], 8, 256, False), set_rows(s.t[2], 8, 512, False)]
                for s in MB.slots:
                    s.ready = [dve.do(lambda e, s=s: e.memset(s.t[:, 256:512], 0.0))]

                def begin():
                    pass

                def a1(it):
                    s = it.s
                    it.st, it.vv, it.m = ST.next(), VV.next(), M.next()
                    QA, QB, KA, KB = it.st.t
                    it.t_stack, it.t_V = [], []
                    steps = []

                    def load():
                        s.L, s.H, s.mb = LAT.next(), HT.next(), MB.next()
                        mi, mf = MI.next(), MF.next()
                        s.tL = pq.go(s.L.t[:, :, :], x1[it.b].rearrange("(n p) t -> p n t", p=128), s.L.free)
                        s.tH = [pq.go(s.H.t[:, :, 0:256], I["ctxT"][it.b].rearrange("(n p) t -> p n t", p=128), s.H.free)]
                        t8 = pq.go(mi.t[:, :], I["mask1"][it.b:it.b + 1, :], mi.free)
                        a = dve.do(lambda e: e.tensor_scalar(mf.t[:, :], mi.t[:, :], 0.0, None, ALU.not_equal), t8, mf.free)
                        mi.free = [a]
                        s.tmb = dve.do(lambda e: e.tensor_scalar(s.mb.t[:, 0:256], mf.t[:, :], -1.0, NEG, ALU.add, ALU.mult),
                                       a, s.mb.free, s.mb.ready)
                        mf.free = [s.tmb]
                        s.mb.free = []

                    def lat_t(tt):
                        def f():
                            bank = bankA.next()
                            t = transposes([bank.t[:, q * 128:q * 128 + 128] for q in range(4)],
                                           [s.L.t[:, tt, q * 128:q * 128 + 128] for q in range(4)], bank, s.tL)
                            a = act.do(lambda e: e.activation(s.H.t[:, :, 256 + tt * 128:384 + tt * 128],
                                                              bank.t[:, :].rearrange("p (a b) -> p a b", a=4), ACT.Copy),
                                       t, s.H.free)
                            bank.free = [a]
                            s.tH.append(a)
                        return f

                    def qk(w, wn, bias, dsts, T, scr, nc_, lo):
                        hold = {"tk": []}

                        def f(o):
                            og = 2 * it.h + o
                            if o == 0:
                                hold["T"] = T.next()
                                for x in (act, dve, pool):
                                    x.wait(hold["T"].free)
                            Tn = hold["T"]
                            bank, Fn = bankA.next(), F.next()
                            t = project(bank, 0, nc_, [(w[:, c, og * 128:og * 128 + 128], s.H.t[:, c, lo:lo + nc_])
                                                       for c in range(4)], s.tH, loaded[wn])
                            Fv = Slot(Fn.t[:, 0:nc_])
                            Fv.free = Fn.free
                            a1_ = evacuate(bank.t[:, 0:nc_], t, Tn.t[:, 0, o, :], Fv, bias[:, og:og + 1])
                            bank.free = a1_
                            s.H.free = [t]
                            hold[o] = (Fn, Fv, a1_)

                        def g(o):
                            Tn, (Fn, Fv, a) = hold["T"], hold[o]
                            hold["tk"].append(split3([Tn.t[:, i, o, :] for i in range(3)], Fv, a))
                            Fn.free = Fv.free
                            if o == 1:
                                wr, ready = stack(None, it.st.free, Tn.t[:, :, :, :], hold["tk"], scr.next(),
                                                  [(d[32 * r:32 * r + 32, :, :], i) for d, order in dsts for r, i in enumerate(order)],
                                                  2, 32, nc_)
                                Tn.free = [wr]
                                it.t_stack += ready
                        return [lambda: f(0), (lambda: g(0), 0.04), lambda: f(1), (lambda: g(1), 0.04)]

                    def vproj(tt):
                        def f():
                            bank = bankA.next()
                            t = project(bank, 0, 256, [(s.H.t[:, c, tt * 128:tt * 128 + 128],
                                                        wv[:, c, it.h * 256:it.h * 256 + 256]) for c in range(4)], s.tH, loaded["v_w1"])
                            d = dve.do(lambda e: e.tensor_tensor(it.vv.t[:, tt, :], bank.t[:, 0:256],
                                                                 rows["vb1"][:, it.h * 256:it.h * 256 + 256], ALU.add),
                                       t, it.vv.free)
                            bank.free = [d]
                            it.t_V.append(d)
                            s.H.free = [t]
                        return f

                    def mrow():
                        it.t_stack.append(mask_row(KA[96:97, :, :], s.mb.t, s.tmb, 512, 8, [it.st.free, it.st.ready]))
                        s.mb.free = s.mb.free + [it.t_stack[-1]]

                    if it.h == 0:
                        steps += [load, lat_t(0), lat_t(1)]
                    steps += qk(wk, "k_w1", col["kb1"], [(KA, [0, 1, 0]), (KB, [2, 1, 0])], TK, scrk, 512, 0)
                    steps += qk(wq, "q_w1", col["qb1"], [(QA, [0, 0, 1]), (QB, [0, 1, 2])], TQ, scrq, 256, 256)
                    steps.append(mrow)
                    steps += [vproj(i) for i in range(4)]
                    it.V = lambda kt, h: it.vv.t[:, kt, h * 32:h * 32 + 32]
                    return steps

                def a2(it):
                    QA, QB, KA, KB = it.st.t
                    tk = []

                    def smax(h, qt):
                        def f():
                            bank = bankA.next()
                            t = pe.do(lambda e: e.matmul(bank.t[:, :], QA[0:97, h, qt * 128:qt * 128 + 128], KA[0:97, h, :],
                                                         start=True, stop=True), bank.free, it.t_stack, it.st.ready)
                            d = dve.do(lambda e: e.tensor_reduce(it.m.t[:, qt, h:h + 1], bank.t[:, :], AX.X, ALU.max), t, it.m.free)
                            bank.free = [d]
                            tk.append(d)
                        return f

                    def rows_():
                        it.turn = maxima_rows(it.m, [tk[-1]], 8, 2, SP, MT, QA)

                    def turn():
                        it.t_rows = it.turn()
                    return [smax(h, qt) for qt in range(2) for h in range(8)] + [rows_, (turn, 0.03)]

                def c(it):
                    QA, QB, KA, KB = it.st.t

                    def group_done(g, t):
                        if g == 0 and it.h == 0:
                            it.s.at = AT.next()
                            it.s.t_at = []
                        if g == 0:
                            it.sums = sums.take()
                        d = act.do(lambda e: e.activation(SS.t[:, :], bankT.t[:, 0:256], ACT.Copy), t, SS.free)
                        d2 = act.do(lambda e: e.activation(it.s.at.t[:, 2 * it.h + g, :], bankV.t[:, 0:256], ACT.Copy), t, it.s.at.free)
                        bankT.free, bankV.free = [d], [d2]
                        SS.free = [sums.put(it.sums, (4 * g, 4 * g + 4, 0, 256), SS.t[0:97:32, :], d)]
                        it.s.t_at.append(d2)
                        if g == 1:
                            it.st.free = [t]
                            it.vv.free = [t]
                    it.group_done = group_done
                    return attend(it, list(range(8)), 4, 256, 1.0 / 32, P,
                                  lambda h, kt: [(KA[0:100, h, kt * 128:kt * 128 + 128], QA[0:100, h, :]),
                                                 (KB[0:96, h, kt * 128:kt * 128 + 128], QB[0:96, h, :])], True, bankS=bankT)

                def p(it):
                    s = it.s

                    def fet():
                        sums.fetch(it.sums)

                    def inv():
                        sums.invert(it.sums)

                    def spread():
                        if it.h == 0:
                            s.t_rb = []
                            s.rbfree = RB.free
                        for g in range(2):
                            x = sums.spread(it.sums, RB.t[:, 2 * it.h + g, :], 4 * g, 4 * g + 4, 32, s.rbfree)
                            s.t_rb.append(x)
                        it.sums.free = s.t_rb[-2:]
                    if it.h == 0:
                        return [nop, fet, nop, nop, inv, nop, nop, spread, nop, nop]

                    def f0():
                        t = pool.do(lambda e: e.tensor_tensor(s.at.t[:, :, :], s.at.t[:, :, :], RB.t[:, :, :], ALU.mult), s.t_at, s.t_rb)
                        RB.free = [t]
                        s.t_at = [t]

                    def f1():
                        s.sq, s.banks = [], []
                        L, j = s.L.t, s.at.t.rearrange("p (a b) q -> p a (b q)", a=2)
                        for tt in range(2):
                            bank = bankA.next()
                            t = project(bank, 0, 512, [(s.at.t[:, g, tt * 128:tt * 128 + 128], wo[:, g, :]) for g in range(4)],
                                        s.t_at, loaded["out_w1"])
                            s.banks.append((bank, t))
                        for tt, (bank, t1) in enumerate(s.banks):
                            a = dve.do(lambda e, tt=tt, bank=bank: e.tensor_tensor(L[:, tt, :], bank.t[:, :], L[:, tt, :],
                                                                                 ALU.add), t1)
                            bank.free = [a]
                            b_ = dve.do(lambda e, tt=tt: e.tensor_tensor(L[:, tt, :], L[:, tt, :], rows["ob1"][:, :], ALU.add), a)
                            s.sq.append(act.do(lambda e, tt=tt: e.activation(j[:, tt, :], L[:, tt, :], ACT.Square,
                                                                             accum_out=sm[:, tt:tt + 1]), b_, t, dve.last()))
                        s.at.free = [t, s.sq[-1]]

                    rstd = rstd_steps(magic_["out"], sm[:, 2:4], sm[:, 0:2], 1e-6, 1.0 / 512, lambda: s.sq,
                                      lambda t: setrs(t))

                    def setrs(t):
                        s.t_rs = t

                    def f2():
                        L, t = s.L.t, s.t_rs
                        last = [dve.do(lambda e, tt=tt: e.tensor_scalar(L[:, tt, :], L[:, tt, :], sm[:, 2 + tt:3 + tt],
                                                                        None, ALU.mult), t) for tt in range(2)]
                        s.L.free = [pq.go(y1[it.b].rearrange("(n p) t -> p n t", p=128), L[:, :, :], last)]
                    return [nop, fet, nop, nop, inv, nop, nop, nop, spread, nop, nop, nop, f0, nop, nop, nop, f1, nop] + rstd + [f2]
                pipeline(items_of(), None, a1, a2, c, p, begin=begin)

        def layer1b():
            with ExitStack() as lc:
                sb = sb_of(lc, "l1b_")
                rows = load_rows(sb, ["mb2"])
                w1 = load_w(sb, "mlp_w1", 4, 2048, 256)
                w2 = load_w(sb, "mlp_w2", 16, 512)
                YN = Ring([Slot(sb(f"YN{i}", [128, 4, 512])) for i in range(2)])
                YT = Slot(sb("YT", [128, 4, 512]))
                LT = Ring([Slot(sb(f"LT{i}", [128, 4, 512])) for i in range(2)])
                H1 = Slot(sb("H1", [128, 16, 512]))
                banks = Ring([Slot(PS[:, i, :]) for i in range(8)])
                for b in range(0, batches, 2):
                    nb = min(2, batches - b)
                    n4, w = 2 * nb, 256 * nb
                    yn, lt = YN.next(), LT.next()
                    ty = sp.go(yn.t[:, 0:n4, :], y1[b:b + nb].rearrange("b (n p) t -> p (b n) t", p=128), yn.free)
                    tl = sp.go(lt.t[:, 0:n4, :], x1[b:b + nb].rearrange("b (n p) t -> p (b n) t", p=128), lt.free)
                    ev = []
                    for f in range(4):
                        bank = banks.next()
                        t = transposes([bank.t[:, q * 128:q * 128 + 128] for q in range(n4)],
                                       [yn.t[:, q, f * 128:f * 128 + 128] for q in range(n4)], bank, ty)
                        d = dve.do(lambda e, f=f, bank=bank: e.tensor_scalar(YT.t[:, f, 0:w], bank.t[:, 0:w],
                                                                             col["pn1"][:, f:f + 1], None, ALU.mult), t, YT.free)
                        bank.free = [d]
                        ev.append(d)
                    yn.free = [t]
                    hs = []
                    for o in range(16):
                        bank = banks.next()
                        t = project(bank, 0, w, [(w1[:, c, o * 128:o * 128 + 128], YT.t[:, c, 0:w]) for c in range(4)], ev,
                                    loaded["mlp_w1"][o // 2])
                        a = act.do(lambda e, o=o, bank=bank: e.activation(H1.t[:, o, 0:w], bank.t[:, 0:w], ACT.Gelu_apprx_tanh,
                                                                          bias=col["mb1"][:, o:o + 1]), t, H1.free)
                        bank.free = [a]
                        hs.append(a)
                    YT.free = [t]
                    last = []
                    for tt in range(n4):
                        bank = banks.next()
                        t = project(bank, 0, 512, [(H1.t[:, o, tt * 128:tt * 128 + 128], w2[:, o, :]) for o in range(16)], hs,
                                    loaded["mlp_w2"])
                        d = dve.do(lambda e, tt=tt, bank=bank, lt=lt: e.tensor_tensor(lt.t[:, tt, :], bank.t[:, :], lt.t[:, tt, :],
                                                                                      ALU.add), t, tl)
                        bank.free = [d]
                        last.append(dve.do(lambda e, tt=tt, lt=lt: e.tensor_tensor(lt.t[:, tt, :], lt.t[:, tt, :], rows["mb2"][:, :],
                                                                            ALU.add), d))
                    H1.free = [t]
                    lt.free = [sp.go(x2[b:b + nb].rearrange("b (n p) t -> p (b n) t", p=128), lt.t[:, 0:n4, :], last)]
                for s in bankA.slots + bankC.slots + [bankV]:
                    s.free = []
                bankVV.slots.remove(bankS)
                barrier()

        def layer2():
            with ExitStack() as lc:
                sb = sb_of(lc, "l2_")
                wk = load_w(sb, "Wk2", 4, 128)
                wv = load_w(sb, "Wv2", 4, 128)
                wq = load_w(sb, "Wq2", 4, 512)
                XT = Ring([Slot(sb(f"XT{i}", [128, 4, 256])) for i in range(2)])
                CT = Ring([Slot(sb(f"CT{i}", [128, 4, 256])) for i in range(2)])
                MK = Ring([Slot((sb(f"MK{i}", [128, 2, 256]), sb(f"MKT{i}", [128, 2, 256]))) for i in range(3)])
                QSR = Ring([Slot(sb(f"QS{i}", [128, 16, 256], bf16)) for i in range(3)])
                KSR = Ring([Slot(sb(f"KS{i}", [128, 8, 256], bf16)) for i in range(3)])
                T = Ring([Slot(sb(f"T{i}", [128, 3, 2, 256], bf16)) for i in range(2)])
                F = Ring([Slot(sb(f"F{i}", [128, 256])[:, :]) for i in range(2)])
                VV = Ring([Slot(sb(f"V{i}", [128, 2, 8, 17])) for i in range(3)])
                M = Ring([Slot(sb(f"M{i}", [128, 2, 16])) for i in range(2)])
                SP = Slot((sb("M3", [128, 2, 48], bf16), sb("Mr", [128, 2, 16])))
                MT = Slot(sb("MT", [48, 256], bf16))
                P = Ring([Slot(sb(f"P{i}", [128, 2, 4, 256])) for i in range(4)])
                JK = Ring([Slot(sb(f"JK{i}", [128, 256])) for i in range(2)])
                wo = load_w(sb, "Wo2", 4, 512)
                rows = load_rows(sb, ["bv2", "bo2", "g2", "be2"])
                X = Ring([Slot(sb(f"X{i}", [128, 2, 512])) for i in range(3)])
                AT = Ring([Slot(sb(f"AT{i}", [128, 4, 256])) for i in range(2)])
                E = Ring([Slot(sb(f"E{i}", [128, 512])) for i in range(2)])
                RB = Slot(sb("RB", [128, 4, 256]))
                sums = Sums(sb, "l2", 16, 256, 4)
                Y = Slot(sb("Y", [128, 2, 512]))
                st_ = sb("st", [128, 2, 6])
                mv = sb("mv", [128, 2, 2])
                rs = sb("rs", [128, 2])
                for s in QSR.slots:
                    s.ready = set_rows(s.t, 16, 256, False)
                for s in KSR.slots:
                    s.ready = set_rows(s.t, 8, 256, True)
                for s in VV.slots:
                    s.ready = [pool.do(lambda e, s=s: e.memset(s.t[:, :, :, 16:17], 1.0))]

                def a0(it):
                    s = it.s

                    def load():
                        s.X, s.XT, s.C, s.mk = X.next(), XT.next(), CT.next(), MK.next()
                        s.tX = pq.go(s.X.t[:, :, :], x2[it.b].rearrange("(n p) t -> p n t", p=128), s.X.free)
                        s.tC = pq.go(s.C.t[:, :, :], I["ctxT"][it.b].rearrange("(n p) t -> p n t", p=128), s.C.free)
                        s.tmk = []
                        for t, name in zip(s.mk.t, ("mask2", "mask2T")):
                            a = pq.go(t[:, :, :], I[name][it.b].rearrange("(n p) t -> p n t", p=128), s.mk.free)
                            s.tmk.append(a)

                    def masks():
                        s.tmk = [pool.do(lambda e, t=t: e.tensor_scalar(t[:, :, :], t[:, :, :], 4.0, None, ALU.mult), s.tmk)
                                 for t in s.mk.t]

                    def xt(tt):
                        def f():
                            bank = bankA.next()
                            t = transposes([bank.t[:, q * 128:q * 128 + 128] for q in range(4)],
                                           [s.X.t[:, tt, q * 128:q * 128 + 128] for q in range(4)], bank, s.tX)
                            a = act.do(lambda e: e.activation(s.XT.t[:, :, tt * 128:tt * 128 + 128],
                                                              bank.t[:, :].rearrange("p (a b) -> p a b", a=4), ACT.Copy),
                                       t, s.XT.free)
                            bank.free = [a]
                            s.tXT = [a] if tt == 0 else s.tXT + [a]
                        return f

                    return [] if it.h else [load, nop, nop, nop, xt(0), xt(1), masks]

                def a1(it):
                    s = it.s
                    it.qs, it.m = QSR.next(), M.next()
                    it.st = it.qs
                    it.t_stack = []
                    steps = []
                    if it.h == 0:
                        s.ks, s.vv = KSR.next(), VV.next()
                        s.t_k, s.t_V = [], []

                    def project3(w, wn, o, src, ts, bias, Tn, i_):
                        bank, Fn = bankA.next(), F.next()
                        t = project(bank, 0, 256, [(w[:, c, o:o + 128], src[:, c, :]) for c in range(4)], ts, loaded[wn])
                        a1_ = evacuate(bank.t[:, 0:256], t, Tn.t[:, 0, i_, :], Fn, bias, True)
                        bank.free = a1_
                        return t, Fn, a1_

                    def q():
                        hold = {"tk": []}

                        def f(o):
                            og = 2 * it.h + o
                            if o == 0:
                                hold["T"] = T.next()
                                for x in (act, dve, pool):
                                    x.wait(hold["T"].free)
                            t, *hold[o] = project3(wq, "Wq2", og * 128, s.XT.t, s.tXT, col["bq2"][:, og:og + 1], hold["T"], o)
                            s.XT.free = [t]

                        def g(o):
                            Tn, (Fn, a) = hold["T"], hold[o]
                            hold["tk"].append(split3([Tn.t[:, i, o, :] for i in range(3)], Fn, a, True))
                            if o == 1:
                                Q = it.qs.t
                                wr, ready = stack(None, it.qs.free, Tn.t[:, :, :, :], hold["tk"], scrq.next(),
                                                  [(Q[16 * r:16 * r + 16, :, :], i) for r, i in enumerate([0, 1, 2, 0, 1, 0])],
                                                  2, 16, 256)
                                Tn.free = [wr]
                                it.t_stack += ready + s.t_k
                        return [lambda: f(0), (lambda: g(0), 0.04), lambda: f(1), (lambda: g(1), 0.04)]

                    def k():
                        hold = {}

                        def f():
                            Tn = T.next()
                            for x in (act, dve, pool):
                                x.wait(Tn.free)
                            hold["x"] = (Tn, *project3(wk, "Wk2", 0, s.C.t, s.tC, col["bk2"][:, 0:1], Tn, 0)[1:])

                        def g():
                            Tn, Fn, a = hold["x"]
                            tk = split3([Tn.t[:, i, 0, :] for i in range(3)], Fn, a, True)
                            K = s.ks.t
                            wr, ready = stack(None, s.ks.free, Tn.t[:, :, 0:1, :], tk, scrk.next(),
                                              [(K[16 * r:16 * r + 16, :, :], i) for r, i in enumerate([0, 0, 0, 1, 1, 2])],
                                              1, 16, 256)
                            Tn.free = [wr]
                            s.t_k = ready + s.ks.ready
                        return [f, (g, 0.04)]

                    def v():
                        bank = bankA.next()
                        for tt in range(2):
                            t = project(bank, 128 * tt, 128 * tt + 128,
                                        [(s.C.t[:, c, tt * 128:tt * 128 + 128], wv[:, c, :]) for c in range(4)], s.tC,
                                        loaded["Wv2"])
                            bank.free = []
                        br = rows["bv2"][:, :].rearrange("p (h d) -> p h d", d=16)
                        for tt in range(2):
                            s.t_V.append(dve.do(lambda e, tt=tt: e.tensor_tensor(
                                s.vv.t[:, tt, :, 0:16], bank.t[:, 128 * tt:128 * tt + 128].rearrange("p (h d) -> p h d", d=16),
                                br, ALU.add), t, s.vv.free, s.vv.ready))
                        bank.free = s.t_V[-2:]
                        s.C.free = [t]

                    if it.h == 0:
                        steps += k() + [v]
                    steps += q()
                    return steps

                def a2(it):
                    s, Q = it.s, it.qs.t
                    tk = []

                    def smax(hp, qt):
                        def f():
                            bank = bankA.next()
                            pe.wait(bank.free, it.t_stack, it.qs.ready)
                            for i in range(2):
                                h = 2 * hp + i
                                g = lambda e, i=i, h=h: e.matmul(
                                    bank.t[:, 256 * i:256 * i + 256], Q[0:97, h, qt * 128:qt * 128 + 128],
                                    s.ks.t[0:97, 4 * it.h + h // 4, :], start=True, stop=True, skip_group_check=True)
                                if i:
                                    t = pe.do(g)
                                else:
                                    pe.quiet(g)
                            for i in range(2):
                                jk = JK.next()
                                d = dve.do(lambda e, i=i, jk=jk: e.tensor_tensor_reduce(
                                    out=jk.t[:, :], in0=bank.t[:, 256 * i:256 * i + 256], in1=s.mk.t[0][:, qt, :], scale=1.0,
                                    scalar=-3.0e38, op0=ALU.add, op1=ALU.max,
                                    accum_out=it.m.t[:, qt, 2 * hp + i:2 * hp + i + 1]), t, it.m.free, jk.free, s.tmk)
                                jk.free = [d]
                            bank.free = [d]
                            tk.append(d)
                        return f

                    def rows_():
                        it.turn = maxima_rows(it.m, [tk[-1]], 16, 2, SP, MT, it.qs.t)

                    def turn():
                        it.t_rows = it.turn()
                    return [smax(hp, qt) for qt in range(2) for hp in range(8)] + [rows_, (turn, 0.1)]

                def c(it):
                    s, Q = it.s, it.qs.t
                    pend, steps = [], []

                    def scores(kv, kt):
                        def f():
                            if kt == 0:
                                Pk = P.next()
                                Pk.ready = []
                                pend.append(Pk)
                            Pk = pend[kv]
                            add = []
                            for i in range(2):
                                bank = bankC.next()
                                t = pe.do(lambda e, i=i, bank=bank: e.matmul(
                                    bank.t, s.ks.t[0:100, 4 * it.h + kv, kt * 128:kt * 128 + 128],
                                    Q[0:100, 4 * kv + 2 * i:4 * kv + 2 * i + 2, :], start=True, stop=True),
                                    bank.free, it.t_rows, it.t_stack, it.qs.ready)
                                mk = s.mk.t[1][:, kt:kt + 1, :].broadcast_to([128, 2, 256])
                                d = dve.do(lambda e, i=i, mk=mk, bank=bank: e.tensor_tensor(
                                    Pk.t[:, kt, 2 * i:2 * i + 2, :], bank.t.rearrange("p (b q) -> p b q", b=2), mk, ALU.add),
                                    t, Pk.free, s.tmk)
                                bank.free = [d]
                                add.append(d)
                            Pk.ready.append(act.do(lambda e: e.activation(Pk.t[:, kt, :, :], Pk.t[:, kt, :, :], ACT.Exp,
                                                                          scale=0.25), add))
                        return f

                    def values(g, kt):
                        def f():
                            two = pend[2 * g:2 * g + 2]
                            if kt == 0:
                                it.bv = bankVV.next()
                                pe.wait(it.bv.free)
                            pe.wait(*[x.ready for x in two], s.t_V)
                            bv = it.bv
                            for j in range(4):
                                kv = 2 * g + j // 2
                                l = s.vv.t[:, kt, 4 * it.h + kv, :]
                                r = two[j // 2].t[:, kt, 2 * (j % 2):2 * (j % 2) + 2, :]
                                h = lambda e, j=j, l=l, r=r: e.matmul(
                                    bv.t[32 * j:32 * j + 17, :], l, r, start=(kt == 0), stop=(kt == 1),
                                    tile_position=(0, 32 * j), skip_group_check=True)
                                if j == 3:
                                    t = pe.do(h)
                                else:
                                    pe.quiet(h)
                            if kt == 1:
                                for x in two:
                                    x.free = [t]
                                if g == 0 and it.h == 0:
                                    s.at = AT.next()
                                    s.t_at = []
                                if g == 0:
                                    it.sums = sums.take()
                                E_ = E.next()
                                a = act.do(lambda e: e.activation(E_.t[:, :], bv.t[:, :], ACT.Copy), t, E_.free)
                                bv.free = [a]
                                fr = [sums.put(it.sums, (8 * g, 8 * g + 8, 0, 256), E_.t[16:113:32, :], a)]
                                for j in range(4):
                                    fr.append(sp.go(s.at.t[64 * g + 16 * j:64 * g + 16 * j + 16, 2 * it.h:2 * it.h + 2, :],
                                                    E_.t[32 * j:32 * j + 16, :], a, s.at.free))
                                E_.free = fr
                                s.t_at += fr
                                if g == 1:
                                    it.qs.free = [t]
                                    if it.h == 1:
                                        s.ks.free = [t]
                                        s.vv.free = [t]
                                        s.mk.free = [dve.last()]
                        return f
                    steps = [scores(0, 0), scores(0, 1), scores(1, 0), scores(1, 1), scores(2, 0), values(0, 0), scores(2, 1),
                             values(0, 1), scores(3, 0), scores(3, 1), nop, values(1, 0), values(1, 1)]
                    return steps

                def p(it):
                    s = it.s

                    def fet():
                        sums.fetch(it.sums)

                    def inv():
                        sums.invert(it.sums)

                    def spread():
                        if it.h == 0:
                            s.t_rb = []
                            s.rbfree = RB.free
                        x = [sp.go(RB.t[64 * g:64 * g + 64, 2 * it.h + i, :],
                                   it.sums.t[1][8 * g:8 * g + 8, None, :].rearrange("(j i) r q -> i j r q", i=2)[i]
                                   .broadcast_to([4, 16, 256]), it.sums.tokens, s.rbfree) for g in range(2) for i in range(2)]
                        it.sums.free = x
                        s.t_rb += x
                    if it.h == 0:
                        return [nop, fet, nop, nop, inv, nop, nop, spread, nop, nop]

                    def f0():
                        t = pool.do(lambda e: e.tensor_tensor(s.at.t[:, :, :], s.at.t[:, :, :], RB.t[:, :, :], ALU.mult), s.t_at, s.t_rb)
                        RB.free = [t]
                        s.t_at = [t]

                    def f1(tt):
                        def f():
                            y = Y.t[:, tt, :]
                            bank = bankA.next()
                            t = project(bank, 0, 512, [(s.at.t[:, g, tt * 128:tt * 128 + 128], wo[:, g, :]) for g in range(4)], s.t_at,
                                        loaded["Wo2"])
                            a = dve.do(lambda e: e.tensor_tensor(y, bank.t[:, :], s.X.t[:, tt, :], ALU.add), t, Y.free)
                            bank.free = [a]
                            a = dve.do(lambda e: e.tensor_tensor(y, y, rows["bo2"][:, :], ALU.add), a)
                            a = dve.do(lambda e: e.bn_stats(st_[:, tt, :], y), a)
                            a = dve.do(lambda e: e.bn_aggr(mv[:, tt, :], st_[:, tt, :]), a)
                            s.a = [a] if tt == 0 else s.a + [a]
                            if tt == 1:
                                s.at.free = [t]
                                s.X.free = [a]
                        return f

                    def setrs(t):
                        s.t_rs = t
                    rstd = rstd_steps(magic_["out"], rs[:, :], mv[:, :, 1], 1e-6, 1.0, lambda: s.a, setrs)

                    def f3(tt):
                        def f():
                            y = Y.t[:, tt, :]
                            a = dve.do(lambda e: e.tensor_scalar(y, y, mv[:, tt, 0:1], rs[:, tt:tt + 1], ALU.subtract, ALU.mult),
                                       s.t_rs)
                            a = dve.do(lambda e: e.tensor_tensor(y, y, rows["g2"][:, :], ALU.mult), a)
                            a = dve.do(lambda e: e.tensor_tensor(y, y, rows["be2"][:, :], ALU.add), a)
                            s.last = [a] if tt == 0 else s.last + [a]
                            if tt == 1:
                                Y.free = [sp.go(x3[it.b].rearrange("(n p) t -> p n t", p=128), Y.t[:, :, :], s.last)]
                        return f
                    return [nop, nop, fet, nop, nop, inv, nop, nop, spread, nop, nop, f0, nop, nop, nop, f1(0), f1(1)] + rstd + [f3(0), f3(1)]

                pipeline(items_of(), a0, a1, a2, c, p, ((0.0, 0.9), (0.0, 0.65), (0.1, 0.72), (0.0, 1.0), (0.0, 1.0)), keep=True)

        def layer3():
            with ExitStack() as lc:
                sb = sb_of(lc, "l3_")
                rows = load_rows(sb, ["gq3", "bq3"])
                wq, wk, wv, wo = (load_w(sb, n, 2, 256) for n in ("Wq3", "Wk3", "Wv3", "Wo3"))
                w1 = load_w(sb, "W13", 2, 512)
                w2 = load_w(sb, "W23", 4, 256)
                pos = sb("pos", [128, 4, 256])
                t_pos = sp.go(pos[:, :, :], I["pos"].rearrange("(n p) c -> p n c", p=128))
                dve.wait(t_pos)
                X = Ring([Slot(sb(f"X{i}", [128, 2, 512])) for i in range(1)])
                QN = Ring([Slot(sb(f"QN{i}", [128, 4, 256])) for i in range(3)])
                KN = Ring([Slot(sb(f"KN{i}", [128, 4, 256])) for i in range(1)])
                QT = Ring([Slot((sb(f"QT{i}", [128, 2, 512]), sb(f"KT{i}", [128, 2, 512]))) for i in range(2)])
                ST = Ring([Slot((sb(f"QS{i}", [128, 8, 512], bf16), sb(f"KS{i}", [128, 8, 512], bf16))) for i in range(3)])
                st_ = sb("st", [128, 8, 6])
                mv = sb("mv", [128, 8, 2])
                rs = sb("rs", [128, 8])
                T = Ring([Slot(sb(f"T{i}", [128, 3, 512], bf16)) for i in range(2)])
                F = Ring([Slot(sb(f"F{i}", [128, 512])[:, :]) for i in range(1)])
                VV = Ring([Slot(sb(f"V{i}", [128, 4, 8, 17])) for i in range(3)])
                M = Ring([Slot(sb(f"M{i}", [128, 4, 8])) for i in range(2)])
                SP = Slot((sb("M3", [128, 4, 24], bf16), sb("Mr", [128, 4, 8])))
                MT = Slot(sb("MT", [24, 512], bf16))
                P = Ring([Slot(sb(f"P{i}", [128, 2048])) for i in range(6)])
                E = Ring([Slot(sb(f"E{i}", [128, 512])) for i in range(1)])
                NCR = Ring([Slot(sb(f"NC{i}", [128, 2, 512])) for i in range(1)])
                RB = Slot(sb("RB", [128, 2, 512]))
                sums = Sums(sb, "l3", 8, 512, 4)
                HH = Slot(sb("HH", [128, 4, 256]))
                HTT = Slot(sb("HTT", [128, 2, 512]))
                RT = Slot(sb("RT", [128, 2, 512]))
                G = Slot(sb("G", [128, 4, 512]))
                st2 = sb("st2", [128, 4, 6])
                mv2 = sb("mv2", [128, 4, 2])
                rs2 = sb("rs2", [128, 4])
                for s in ST.slots:
                    s.ready = [set_rows(t, 8, 512, k == 1) for k, t in enumerate(s.t)]
                def begin():
                    for s in VV.slots:
                        s.ready = [pool.do(lambda e, s=s: e.memset(s.t[:, :, :, 16:17], 1.0))]

                def a0(it):
                    s = it.s

                    def load():
                        s.X, s.qn, s.kn, s.qt = X.next(), QN.next(), KN.next(), QT.next()
                        s.tX = pq.go(s.X.t[:, :, :], x3[it.b].rearrange("(n p) t -> p n t", p=128), s.X.free)
                        s.tC = pq.go(s.kn.t[:, :, :], I["ctxT"][it.b].rearrange("(n p) t -> p n t", p=128), s.kn.free)
                        s.ln = []

                    def kn():
                        s.t_kn = pool.do(lambda e: e.tensor_tensor(s.kn.t[:, :, :], s.kn.t[:, :, :], pos[:, :, :], ALU.add), s.tC,
                                         t_pos)

                    def kst(lo):
                        def f():
                            for tt in range(lo, lo + 2):
                                b_ = dve.do(lambda e, tt=tt: e.bn_stats(st_[:, 4 + tt, :], s.kn.t[:, tt, :]), s.t_kn)
                                s.ln.append(dve.do(lambda e, tt=tt: e.bn_aggr(mv[:, 4 + tt, :], st_[:, 4 + tt, :]), b_))
                        return f

                    def qn(tp):
                        def f():
                            bank = bankA.next()
                            t = transposes([bank.t[:, (2 * k + cc) * 128:(2 * k + cc) * 128 + 128] for k in range(2) for cc in range(2)],
                                           [s.X.t[:, cc, (2 * tp + k) * 128:(2 * tp + k) * 128 + 128] for k in range(2) for cc in range(2)],
                                           bank, s.tX)
                            d = dve.do(lambda e: e.tensor_tensor(s.qn.t[:, 2 * tp:2 * tp + 2, :],
                                                                 bank.t[:, :].rearrange("p (a b) -> p a b", a=2),
                                                                 pos[:, 2 * tp:2 * tp + 2, :], ALU.add), t, s.qn.free)
                            bank.free = [d]
                            s.X.free = [t]
                            for k in range(2):
                                tt = 2 * tp + k
                                b_ = dve.do(lambda e, tt=tt: e.bn_stats(st_[:, tt, :], s.qn.t[:, tt, :]), d)
                                s.ln.append(dve.do(lambda e, tt=tt: e.bn_aggr(mv[:, tt, :], st_[:, tt, :]), b_))
                        return f

                    def setrs(t):
                        s.t_rs = t
                        s.tq, s.tk = [], []
                    rstd = rstd_steps(magic_["in"], rs[:, :], mv[:, :, 1], 1e-5, 1.0, lambda: s.ln, setrs)

                    def norm(tt):
                        def f():
                            q, k = s.qn.t[:, tt, :], s.kn.t[:, tt, :]
                            a = dve.do(lambda e: e.tensor_scalar(q, q, mv[:, tt, 0:1], rs[:, tt:tt + 1], ALU.subtract, ALU.mult),
                                       s.t_rs)
                            a = dve.do(lambda e: e.tensor_tensor(q, q, rows["gq3"][:, :], ALU.mult), a)
                            s.tq.append(dve.do(lambda e: e.tensor_tensor(q, q, rows["bq3"][:, :], ALU.add), a))
                            s.tk.append(dve.do(lambda e: e.tensor_scalar(k, k, mv[:, 4 + tt, 0:1], rs[:, 4 + tt:5 + tt],
                                                                         ALU.subtract, ALU.mult), s.t_rs))
                        return f

                    def tr(cc):
                        def f():
                            QTt, KTt = s.qt.t
                            if cc == 0:
                                s.t_qt, s.t_kt = [], []
                            bank = bankA.next()
                            t = transposes([bank.t[:, tt * 128:tt * 128 + 128] for tt in range(4)],
                                           [s.qn.t[:, tt, cc * 128:cc * 128 + 128] for tt in range(4)], bank, s.tq)
                            a = act.do(lambda e, bank=bank: e.activation(QTt[:, cc, :], bank.t[:, :], ACT.Copy), t, s.qt.free)
                            bank.free = [a]
                            s.t_qt.append(a)
                            bank = bankA.next()
                            t = transposes([bank.t[:, tt * 128:tt * 128 + 128] for tt in range(4)],
                                           [s.kn.t[:, tt, cc * 128:cc * 128 + 128] for tt in range(4)], bank, s.tk)
                            a = act.do(lambda e, bank=bank: e.activation(KTt[:, cc, :], bank.t[:, :], ACT.Identity,
                                                                         bias=col["bkv3"][:, cc:cc + 1],
                                                                         scale=col["gkv3"][:, cc:cc + 1]), t, s.qt.free)
                            bank.free = [a]
                            s.t_kt.append(a)
                            s.kn.free = [t]
                        return f

                    return [] if it.h else ([load, nop, nop, kn, nop, qn(0), qn(1), kst(0), kst(2)] + rstd
                                             + [norm(0), norm(1), norm(2), norm(3), nop, tr(0), tr(1)])

                def a1(it):
                    s = it.s
                    it.st, it.vv, it.m = ST.next(), VV.next(), M.next()
                    QS, KS = it.st.t
                    it.t_stack, it.t_V = [], []
                    steps = []

                    def qk(w, wn, k_, scr, parts):
                        hold = {}

                        def f():
                            src, ts = s.qt.t[k_], (s.t_kt if k_ else s.t_qt)
                            bank, Tn, Fn = bankA.next(), T.next(), F.next()
                            t = project(bank, 0, 512, [(w[:, c, it.h * 128:it.h * 128 + 128], src[:, c, :]) for c in range(2)], ts,
                                        loaded[wn])
                            act.wait(Tn.free)
                            a1_ = evacuate(bank.t[:, :], t, Tn.t[:, 0, :], Fn)
                            bank.free = a1_
                            hold["x"] = (Tn, Fn, a1_)

                        def g():
                            Tn, Fn, a = hold["x"]
                            tk = split3([Tn.t[:, i, :] for i in range(3)], Fn, a)
                            wr, ready = stack_rows(it.st.free, Tn.t, tk, scr.next(), parts)
                            Tn.free = wr
                            it.t_stack += ready
                        return [f, (g, 0.04)]

                    def vproj(tp):
                        def f():
                            bank = bankA.next()
                            for k in range(2):
                                tt = 2 * tp + k
                                t = project(bank, 128 * k, 128 * k + 128,
                                            [(s.qt.t[1][:, c, tt * 128:tt * 128 + 128], wv[:, c, it.h * 128:it.h * 128 + 128])
                                             for c in range(2)], s.t_kt, loaded["Wv3"])
                                bank.free = []
                            d = dve.do(lambda e: e.tensor_copy(
                                it.vv.t[:, 2 * tp:2 * tp + 2, :, 0:16],
                                bank.t[:, 0:256].rearrange("p (a h d) -> p a h d", a=2, d=16)), t, it.vv.free, it.vv.ready)
                            bank.free = [d]
                            it.t_V.append(d)
                            s.qt.free = [t]
                        return f

                    steps += qk(wq, "Wq3", 0, scrq, q_parts(QS))
                    steps += qk(wk, "Wk3", 1, scrk, k_parts(KS))
                    steps += [vproj(0), vproj(1)]
                    it.V = lambda kt, h: it.vv.t[:, kt, h, :]
                    return steps

                def a2(it):
                    QS, KS = it.st.t
                    tk = []

                    def smax(h, qt):
                        def f():
                            bank = bankA.next()
                            t = pe.do(lambda e: e.matmul(bank.t[:, :], QS[0:97, h, qt * 128:qt * 128 + 128], KS[0:97, h, :],
                                                         start=True, stop=True), bank.free, it.t_stack, it.st.ready)
                            d = dve.do(lambda e: e.tensor_reduce(it.m.t[:, qt, h:h + 1], bank.t[:, :], AX.X, ALU.max), t, it.m.free)
                            bank.free = [d]
                            tk.append(d)
                        return f

                    def rows_():
                        it.turn = maxima_rows(it.m, [tk[-1]], 8, 4, SP, MT, QS)

                    def turn():
                        it.t_rows = it.turn()
                    return [smax(h, qt) for qt in range(4) for h in range(8)] + [rows_, (turn, 0.03)]

                def c(it):
                    QS, KS = it.st.t

                    def group_done(g, t):
                        s = it.s
                        if g == 0 and it.h == 0:
                            s.nc = NCR.next()
                            s.t_nc = []
                        if g == 0:
                            it.sums = sums.take()
                        E_ = E.next()
                        bv = it.bv
                        a = act.do(lambda e: e.activation(E_.t[:, :], bv.t[:, :], ACT.Copy), t, E_.free)
                        bv.free = [a]
                        fr = [sums.put(it.sums, (4 * g, 4 * g + 4, 0, 512), E_.t[16:113:32, :], a)]
                        for j in range(4):
                            p0 = 16 * (4 * g + j)
                            fr.append(sp.go(s.nc.t[p0:p0 + 16, it.h, :], E_.t[32 * j:32 * j + 16, :], a, s.nc.free))
                        E_.free = fr
                        s.t_nc += fr
                        if g == 1:
                            it.st.free = [t]
                            it.vv.free = [t]
                    it.group_done = group_done
                    return attend3(it)

                def attend3(it):
                    QS, KS = it.st.t
                    return attend(it, list(range(8)), 4, 512, 0.25, P,
                                  lambda h, kt: [(KS[0:100, h, kt * 128:kt * 128 + 128], QS[0:100, h, :])], False, 2)

                def p(it):
                    s = it.s

                    def fet():
                        sums.fetch(it.sums)

                    def inv():
                        sums.invert(it.sums)

                    def spread():
                        if it.h == 0:
                            s.t_rb = []
                            s.rbfree = RB.free
                        x = sums.spread(it.sums, RB.t[:, it.h, :], 0, 8, 16, s.rbfree)
                        it.sums.free = [x]
                        s.t_rb.append(x)
                    if it.h == 0:
                        return [nop, fet, nop, nop, inv, nop, nop, spread, nop, nop]

                    def f0():
                        s.t_at = [q.do(lambda e, n=n: e.tensor_tensor(s.nc.t[:, n, :], s.nc.t[:, n, :], RB.t[:, n, :], ALU.mult),
                                       s.t_nc, s.t_rb) for n, q in enumerate((dve, pool))]
                        RB.free = s.t_at

                    def f1(tt):
                        def f():
                            bank = bankA.next()
                            t = project(bank, 0, 256, [(s.nc.t[:, c, tt * 128:tt * 128 + 128], wo[:, c, :]) for c in range(2)],
                                        s.t_at, loaded["Wo3"])
                            q = s.qn.t[:, tt, :]
                            a = dve.do(lambda e: e.tensor_tensor(q, bank.t[:, 0:256], q, ALU.add), t)
                            bank.free = [a]
                            a = dve.do(lambda e: e.bn_stats(st2[:, tt, :], q), a)
                            a = dve.do(lambda e: e.bn_aggr(mv2[:, tt, :], st2[:, tt, :]), a)
                            s.a = [a] if tt == 0 else s.a + [a]
                            if tt == 3:
                                s.nc.free = [t]
                        return f

                    def setrs2(t):
                        s.t_rs2 = t
                        s.th = []
                    rstd = rstd_steps(magic_["out"], rs2[:, :], mv2[:, :, 1], 1e-5, 1.0, lambda: s.a, setrs2)

                    def f2b(tt):
                        return lambda: s.th.append(dve.do(lambda e: e.tensor_scalar(
                            HH.t[:, tt, :], s.qn.t[:, tt, :], mv2[:, tt, 0:1], rs2[:, tt:tt + 1], ALU.subtract, ALU.mult),
                            s.t_rs2, HH.free))

                    def f3(cc):
                        def f():
                            if cc == 0:
                                s.t_ht, s.t_rt = [], []
                            bank = bankA.next()
                            t = transposes([bank.t[:, tt * 128:tt * 128 + 128] for tt in range(4)],
                                           [HH.t[:, tt, cc * 128:cc * 128 + 128] for tt in range(4)], bank, s.th)
                            a = act.do(lambda e, bank=bank: e.activation(HTT.t[:, cc, :], bank.t[:, :], ACT.Identity,
                                                                         bias=col["bf3"][:, cc:cc + 1],
                                                                         scale=col["gf3"][:, cc:cc + 1]), t, HTT.free)
                            bank.free = [a]
                            HH.free = [t]
                            s.t_ht.append(a)
                            bank = bankA.next()
                            t = transposes([bank.t[:, tt * 128:tt * 128 + 128] for tt in range(4)],
                                           [s.qn.t[:, tt, cc * 128:cc * 128 + 128] for tt in range(4)], bank)
                            a = act.do(lambda e, bank=bank: e.activation(RT.t[:, cc, :], bank.t[:, :], ACT.Copy), t, RT.free)
                            bank.free = [a]
                            s.t_rt.append(a)
                            s.qn.free = [t]
                        return f

                    def f4(o):
                        def f():
                            if o == 0:
                                s.tg = []
                            bank = bankA.next()
                            t = project(bank, 0, 512, [(w1[:, c, o * 128:o * 128 + 128], HTT.t[:, c, :]) for c in range(2)], s.t_ht,
                                        loaded["W13"])
                            s.tg.append(dve.do(lambda e: e.tensor_scalar(G.t[:, o, :], bank.t[:, :], col["b13"][:, o:o + 1], None,
                                                                         ALU.add), t, G.free))
                            bank.free = [s.tg[-1]]
                            if o == 3:
                                HTT.free = [t]
                                s.tg = [act.do(lambda e: e.activation(G.t[:, :, :], G.t[:, :, :], ACT.Gelu), s.tg)]
                        return f

                    def f5(cc):
                        def f():
                            bank = bankA.next()
                            t = project(bank, 0, 512, [(w2[:, o, cc * 128:cc * 128 + 128], G.t[:, o, :]) for o in range(4)], s.tg,
                                        loaded["W23"])
                            d = dve.do(lambda e: e.scalar_tensor_tensor(
                                out=RT.t[:, cc, :], in0=bank.t[:, :], scalar=col["b23"][:, cc:cc + 1], in1=RT.t[:, cc, :],
                                op0=ALU.add, op1=ALU.add), t, s.t_rt)
                            bank.free = [d]
                            s.last = [d] if cc == 0 else s.last + [d]
                            if cc == 1:
                                G.free = [t]
                                RT.free = [sp.go(out[it.b].rearrange("(n p) t -> p n t", p=128), RT.t[:, :, :], s.last)]
                        return f
                    return ([nop, nop, fet, nop, nop, nop, inv, nop, nop, nop, spread, nop, nop, nop, nop, nop, nop, f0, nop, nop] + [f1(i) for i in range(4)] + [nop] + rstd
                            + [f2b(i) for i in range(4)] + [nop, f3(0), f3(1), nop] + [f4(i) for i in range(4)]
                            + [nop, nop, nop, nop, nop, nop, f5(0), f5(1)])
                pipeline(items_of(), a0, a1, a2, c, p, begin=begin)

        layer0()
        layer1a()
        layer1b()
        layer2()
        layer3()

        block = ctx.enter_context(nc.Block())

        @block.sync
        def _(e):
            sp.run(e)

        @block.gpsimd
        def _(e):
            pool.run(e)

        @block.scalar
        def _(e):
            act.run(e)

        @block.vector
        def _(e):
            dve.run(e)

        @block.tensor
        def _(e):
            pe.run(e)


def lay_out(i):
    a = {k: np.asarray(v) for k, v in i.items()}
    C = np.ascontiguousarray
    colv = lambda v: C(v.reshape(-1, 128).T)
    kvw = a["L1_xattn_kv_w"].reshape(512, 512, 2)
    kvb = a["L1_xattn_kv_b"].reshape(512, 2)
    cols = {"bq0": a["L0_xattn_bq"], "bk0": a["L0_xattn_bk"], "qb1": a["L1_xattn_q_b"], "kb1": kvb[:, 0],
            "pn1": a["L1_xattn_postnorm_w"], "mb1": a["L1_xattn_mlp_b1"], "bq2": a["L2_xattn_bq"], "bk2": a["L2_xattn_bk"],
            "gkv3": a["L3_xattn_ln_kv_g"], "bkv3": a["L3_xattn_ln_kv_b"], "gf3": a["L3_xattn_ffn_ln_g"],
            "bf3": a["L3_xattn_ffn_ln_b"], "b13": a["L3_xattn_b1"], "b23": a["L3_xattn_b2"]}
    rows = {"bv0": a["L0_xattn_bv"], "vb1": kvb[:, 1], "ob1": a["L1_xattn_out_b"], "mb2": a["L1_xattn_mlp_b2"],
            "bv2": a["L2_xattn_bv"], "bo2": a["L2_xattn_bo"], "g2": a["L2_xattn_gamma"], "be2": a["L2_xattn_beta"],
            "gq3": a["L3_xattn_ln_q_g"], "bq3": a["L3_xattn_ln_q_b"]}
    t = np.arange(512, dtype=np.float32)[:, None]
    div = np.exp(np.arange(0, 256, 2, dtype=np.float32) * np.float32(-np.log(10000.0) / 256))
    ang = (t * div).astype(np.float32)
    pos = np.zeros((512, 256), np.float32)
    pos[:, 0::2] = np.sin(ang)
    pos[:, 1::2] = np.cos(ang)
    mask0 = a["mask_Bx1x2048_bf1"]
    return {
        "x": a["x"], "ctx": a["ctx_2048"], "ctxT": C(a["ctx_2048"].transpose(0, 2, 1)),
        "mask0": C(mask0).view(np.uint8), "mask1": a["mask_BxS2_ik0"],
        "mask2": C(a["mask_Bx1xSxS2_ff0"][:, 0]), "mask2T": C(a["mask_Bx1xSxS2_ff0"][:, 0].transpose(0, 2, 1)),
        "cols": C(np.concatenate([colv(cols[n]) for n, _ in COLS], axis=1)),
        "rows": C(np.concatenate([rows[n] for n, _ in ROWS])[None, :]),
        "pos": pos,
        "WqT0": C(a["L0_xattn_Wq"].T), "WkT0": C(a["L0_xattn_Wk"].T), "WvT0": C(a["L0_xattn_Wv"].T),
        "q_w1": a["L1_xattn_q_w"], "k_w1": C(kvw[:, :, 0]), "v_w1": C(kvw[:, :, 1]), "out_w1": a["L1_xattn_out_w"],
        "mlp_w1": a["L1_xattn_mlp_w1"], "mlp_w2": a["L1_xattn_mlp_w2"],
        "Wq2": a["L2_xattn_Wq"], "Wk2": a["L2_xattn_Wk"], "Wv2": a["L2_xattn_Wv"], "Wo2": C(a["L2_xattn_Wo"].reshape(2, 2, 4, 2, 16, 512).transpose(0, 3, 1, 2, 4, 5).reshape(512, 512)),
        "Wq3": a["L3_xattn_Wq"], "Wk3": a["L3_xattn_Wk"], "Wv3": a["L3_xattn_Wv"], "Wo3": a["L3_xattn_Wo"],
        "W13": a["L3_xattn_W1"], "W23": a["L3_xattn_W2"],
    }


def kernel(**inputs):
    import concourse.bacc as _bacc
    from concourse.bass_utils import run_bass_kernel_spmd as _run

    nc = _bacc.Bacc("TRN2", target_bir_lowering=False, num_devices=1)
    arrays, aps = {}, {}
    for name, v in lay_out(inputs).items():
        arrays[f"in_{name}"] = v
        aps[name] = nc.dram_tensor(f"in_{name}", v.shape, mybir.dt.from_np(v.dtype), kind="ExternalInput").ap()
    out = nc.dram_tensor("out_0", [8, 256, 512], mybir.dt.float32, kind="ExternalOutput").ap()
    build_program(nc, aps, out)
    r = _run(nc, [arrays], core_ids=[0])
    return r.results[0]["out_0"]
```
